# Optimizing a Trainium2 kernel written in Bass

```python
import numpy as np
import jax
import jax.numpy as jnp

def _softmax(x, axis=-1):
    return jax.nn.softmax(x, axis=axis)

def _gelu(x):
    return jax.nn.gelu(x, approximate=True)

def _silu(x):
    return jax.nn.silu(x)

def _sigmoid(x):
    return jax.nn.sigmoid(x)

def _layernorm(x, axis=-1, eps=1e-05):
    m = jnp.mean(x, axis=axis, keepdims=True)
    v = jnp.var(x, axis=axis, keepdims=True)
    return (x - m) / jnp.sqrt(v + eps)

def _scatter_add(tgt, idx, src, axis=0):
    return tgt.at[idx].add(src)

def _segment_sum(src, seg, n):
    return jax.ops.segment_sum(src, seg, n)
kernel_name = 'mk_gps_d1_gnn_r64_318643'

def setup_inputs(seed: int=0):
    np.random.seed(seed)
    _w = jnp.asarray

    def _rec_inputs():
        import jax
        import jax.numpy as jnp
        _gk = jax.random.key(seed)
        x = -0.0002117 + 1 * jax.random.normal(jax.random.fold_in(_gk, 1), (50000, 256), jnp.float32)
        src = jax.random.randint(jax.random.fold_in(_gk, 2), (25000,), 0, 50000, jnp.int32)
        dst = jax.random.randint(jax.random.fold_in(_gk, 3), (25000,), 0, 50000, jnp.int32)
        _o = jnp.argsort(dst, stable=True)
        src = src[_o]
        dst = dst[_o]
        edge_weight = jax.random.uniform(jax.random.fold_in(_gk, 12), (25000,), jnp.float32, 0.0, 1)
        return (x, src, dst, edge_weight)
    x, src, dst, edge_weight = _rec_inputs()

    def _L0_gnn_setup():
        import jax, jax.numpy as jnp
        import numpy as np
        N_NODES = 100000
        N_EDGES = 50000
        DIM = 256
        PRESERVE = 0.1

        def _gcn_conv(x, W, b, src, dst, ew, n_nodes):
            loop = jnp.arange(n_nodes, dtype=src.dtype)
            src2 = jnp.concatenate([src, loop])
            dst2 = jnp.concatenate([dst, loop])
            ew2 = jnp.concatenate([ew, jnp.ones((n_nodes,), dtype=ew.dtype)])
            deg = jax.ops.segment_sum(ew2, dst2, num_segments=n_nodes)
            dinv = jnp.where(deg > 0, jax.lax.rsqrt(jnp.maximum(deg, 1e-30)), 0.0)
            norm = dinv[src2] * ew2 * dinv[dst2]
            xw = x @ W
            msg = xw[src2] * norm[:, None]
            out = jax.ops.segment_sum(msg, dst2, num_segments=n_nodes)
            return out + b
        key = jax.random.key(seed)
        k = jax.random.split(key, 8)
        skill_embed = jax.random.normal(k[0], (N_NODES, DIM), dtype=jnp.float32)
        adj_list = jax.random.randint(k[1], (2, N_EDGES), 0, N_NODES, dtype=jnp.int64)
        edge_attr = jax.random.uniform(k[2], (N_EDGES,), dtype=jnp.float32)
        s = 1.0 / np.sqrt(DIM)
        W1 = jax.random.uniform(k[3], (DIM, DIM), dtype=jnp.float32, minval=-s, maxval=s)
        b1 = jnp.zeros((DIM,), dtype=jnp.float32)
        W2 = jax.random.uniform(k[4], (DIM, DIM), dtype=jnp.float32, minval=-s, maxval=s)
        b2 = jnp.zeros((DIM,), dtype=jnp.float32)
        return {'skill_embed': skill_embed, 'adj_list': adj_list, 'edge_attr': edge_attr, 'W1': W1, 'b1': b1, 'W2': W2, 'b2': b2}
    _L0_gnn_all = _L0_gnn_setup()
    _L0_gnn_in = {k: v for k, v in _L0_gnn_all.items() if k in ('W1', 'b1', 'W2', 'b2')}
    del _L0_gnn_all

    def _L0_mix_setup():
        import jax, jax.numpy as jnp
        import numpy as np
        B, N, C, H = (8, 256, 256, 8)
        D = C // H
        GH = C // 4
        key = jax.random.key(seed)
        ks = jax.random.split(key, 6)
        s = 0.02
        return {'x': jax.random.normal(ks[0], (B, N, C), dtype=jnp.float32), 'Wqkv': jax.random.normal(ks[1], (C, 3 * C), dtype=jnp.float32) * s, 'Wproj': jax.random.normal(ks[2], (C, C), dtype=jnp.float32) * s, 'bproj': jnp.zeros((C,), dtype=jnp.float32), 'ln_g': jnp.ones((C,), dtype=jnp.float32), 'ln_b': jnp.zeros((C,), dtype=jnp.float32), 'Wg1': jax.random.normal(ks[3], (C, GH), dtype=jnp.float32) * s, 'bg1': jnp.zeros((GH,), dtype=jnp.float32), 'Wg2': jax.random.normal(ks[4], (GH, C), dtype=jnp.float32) * s, 'bg2': jnp.zeros((C,), dtype=jnp.float32)}
    _L0_mix_all = _L0_mix_setup()
    _L0_mix_in = {k: v for k, v in _L0_mix_all.items() if k in ('Wqkv', 'Wproj', 'bproj', 'ln_g', 'ln_b', 'Wg1', 'bg1', 'Wg2', 'bg2')}
    del _L0_mix_all

    def _L0_ffn_setup():
        import jax, jax.numpy as jnp
        import numpy as np
        EPS = 1e-08
        key = jax.random.key(seed)
        kx, kw, kb = jax.random.split(key, 3)
        B, S, K, N = (64, 64, 256, 256)
        x = jax.random.normal(kx, (B, S, K), dtype=jnp.float32)
        bound_w = np.sqrt(6.0 / K) / np.sqrt(1.0 + 5.0)
        weight = jax.random.uniform(kw, (N, K), dtype=jnp.float32, minval=-bound_w, maxval=bound_w)
        bound_b = 1.0 / np.sqrt(K)
        bias = jax.random.uniform(kb, (N,), dtype=jnp.float32, minval=-bound_b, maxval=bound_b)
        return {'x': x, 'weight': weight, 'bias': bias}
    _L0_ffn_all = _L0_ffn_setup()
    _L0_ffn_in = {k: v for k, v in _L0_ffn_all.items() if k in ('weight', 'bias')}
    del _L0_ffn_all
    return {'x': x, 'src': src, 'dst': dst, 'edge_weight': edge_weight, 'L0_gnn_W1': _L0_gnn_in['W1'], 'L0_gnn_b1': _L0_gnn_in['b1'], 'L0_gnn_W2': _L0_gnn_in['W2'], 'L0_gnn_b2': _L0_gnn_in['b2'], 'L0_mix_Wqkv': _L0_mix_in['Wqkv'], 'L0_mix_Wproj': _L0_mix_in['Wproj'], 'L0_mix_bproj': _L0_mix_in['bproj'], 'L0_mix_ln_g': _L0_mix_in['ln_g'], 'L0_mix_ln_b': _L0_mix_in['ln_b'], 'L0_mix_Wg1': _L0_mix_in['Wg1'], 'L0_mix_bg1': _L0_mix_in['bg1'], 'L0_mix_Wg2': _L0_mix_in['Wg2'], 'L0_mix_bg2': _L0_mix_in['bg2'], 'L0_ffn_weight': _L0_ffn_in['weight'], 'L0_ffn_bias': _L0_ffn_in['bias']}

def reference(x, src, dst, edge_weight, L0_gnn_W1, L0_gnn_b1, L0_gnn_W2, L0_gnn_b2, L0_mix_Wqkv, L0_mix_Wproj, L0_mix_bproj, L0_mix_ln_g, L0_mix_ln_b, L0_mix_Wg1, L0_mix_bg1, L0_mix_Wg2, L0_mix_bg2, L0_ffn_weight, L0_ffn_bias):
    import jax
    import jax.numpy as jnp

    def _L0_gnn_ref(skill_embed, adj_list, edge_attr, W1, b1, W2, b2):
        import jax, jax.numpy as jnp
        import numpy as np
        N_NODES = 100000
        N_EDGES = 50000
        DIM = 256
        PRESERVE = 0.1

        def _gcn_conv(x, W, b, src, dst, ew, n_nodes):
            loop = jnp.arange(n_nodes, dtype=src.dtype)
            src2 = jnp.concatenate([src, loop])
            dst2 = jnp.concatenate([dst, loop])
            ew2 = jnp.concatenate([ew, jnp.ones((n_nodes,), dtype=ew.dtype)])
            deg = jax.ops.segment_sum(ew2, dst2, num_segments=n_nodes)
            dinv = jnp.where(deg > 0, jax.lax.rsqrt(jnp.maximum(deg, 1e-30)), 0.0)
            norm = dinv[src2] * ew2 * dinv[dst2]
            xw = x @ W
            msg = xw[src2] * norm[:, None]
            out = jax.ops.segment_sum(msg, dst2, num_segments=n_nodes)
            return out + b
        src, dst = (adj_list[0], adj_list[1])
        n = skill_embed.shape[0]
        temp = skill_embed
        out = _gcn_conv(skill_embed, W1, b1, src, dst, edge_attr, n)
        temp = (1.0 - PRESERVE) * out + PRESERVE * temp
        out = _gcn_conv(temp, W2, b2, src, dst, edge_attr, n)
        temp = (1.0 - PRESERVE) * out + PRESERVE * temp
        return temp

    def _L0_mix_ref(x, Wqkv, Wproj, bproj, ln_g, ln_b, Wg1, bg1, Wg2, bg2):
        import jax, jax.numpy as jnp
        import numpy as np
        B, N, C, H = (8, 256, 256, 8)
        D = C // H
        GH = C // 4
        b, n, c = x.shape
        h, d = (H, D)
        qkv = (x @ Wqkv).reshape(b, n, 3, h, d)
        q, k, v = (qkv[:, :, 0], qkv[:, :, 1], qkv[:, :, 2])
        k = jax.nn.softmax(k, axis=1)
        context = jnp.einsum('bnhd,bnhv->bhdv', k, v)
        out = jnp.einsum('bnhd,bhdv->bnhv', q, context).reshape(b, n, c)
        mu = jnp.mean(x, axis=-1, keepdims=True)
        var = jnp.var(x, axis=-1, keepdims=True)
        xn = (x - mu) * jax.lax.rsqrt(var + 1e-05) * ln_g + ln_b
        hgate = jax.nn.gelu(xn @ Wg1 + bg1, approximate=False)
        gate = jax.nn.sigmoid(hgate @ Wg2 + bg2)
        return out * gate @ Wproj + bproj

    def _L0_ffn_ref(x, weight, bias):
        import jax, jax.numpy as jnp
        import numpy as np
        EPS = 1e-08
        'LNS inference path of LNSLinear.\n\n            log_out[m, n] = logsumexp_k(log(|x[m,k]|+eps) + log(|w[n,k]|+eps))\n            out = sign(sign(x) @ sign(w).T) * exp(log_out) + bias\n            Computed stably as log(exp(lx - mx) @ exp(lw - mw).T) + mx + mw.\n            '
        orig_shape = x.shape
        K = weight.shape[1]
        xf = x.reshape(-1, K)
        log_x = jnp.log(jnp.abs(xf) + EPS)
        x_sign = jnp.sign(xf)
        log_w = jnp.log(jnp.abs(weight) + EPS)
        w_sign = jnp.sign(weight)
        mx = jnp.max(log_x, axis=-1, keepdims=True)
        mw = jnp.max(log_w, axis=-1, keepdims=True)
        acc = jnp.einsum('mk,nk->mn', jnp.exp(log_x - mx), jnp.exp(log_w - mw))
        log_out = jnp.log(acc) + mx + mw.T
        out_sign = jnp.sign(jnp.einsum('mk,nk->mn', x_sign, w_sign))
        out = out_sign * jnp.exp(log_out) + bias
        return out.reshape(orig_shape[:-1] + (weight.shape[0],))
    edge_index = jnp.stack([src, dst])
    xn = _layernorm(x, axis=-1)
    x = x + _L0_gnn_ref(xn, edge_index, edge_weight, L0_gnn_W1, L0_gnn_b1, L0_gnn_W2, L0_gnn_b2) + _L0_mix_ref(xn[None], L0_mix_Wqkv, L0_mix_Wproj, L0_mix_bproj, L0_mix_ln_g, L0_mix_ln_b, L0_mix_Wg1, L0_mix_bg1, L0_mix_Wg2, L0_mix_bg2)[0]
    x = x + _L0_ffn_ref(_layernorm(x, axis=-1)[None], L0_ffn_weight, L0_ffn_bias)[0]
    return x

_drawn_inputs = setup_inputs


def setup_inputs(seed=0):
    import zlib

    import numpy as np

    out = dict(_drawn_inputs(seed))
    spreads = {'L0_gnn_b1': (0.0, 0.1),
     'L0_gnn_b2': (0.0, 0.1),
     'L0_mix_bproj': (0.0, 0.1),
     'L0_mix_ln_g': (1.0, 0.6),
     'L0_mix_ln_b': (0.0, 0.8),
     'L0_mix_bg1': (0.0, 0.8),
     'L0_mix_bg2': (0.0, 0.285)}
    factors = {'L0_mix_Wg1': 5.022, 'L0_mix_Wg2': 4.341, 'L0_ffn_bias': 8.0}
    for name, (base, spread) in spreads.items():
        noise = np.random.default_rng([zlib.crc32(name.encode()), seed]).standard_normal(out[name].shape)
        drawn = base * np.exp(spread * noise) if base else spread * noise
        out[name] = jnp.asarray(drawn.astype(out[name].dtype))
    for name, factor in factors.items():
        out[name] = (out[name] * factor).astype(out[name].dtype)
    return out
```

```python
from contextlib import ExitStack

import concourse.bass as bass
from concourse import mybir

NODES, D, EDGES = 50000, 256, 25000
HEADS, GATE = 8, 64
HD = D // HEADS
KEEP = 0.1
MIX = 1.0 - KEEP
LN_EPS, FFN_EPS, DEG_FLOOR = 1e-5, 1e-8, 1e-30

P, ROWS = 128, 4
TILE = P * ROWS
FULL = NODES // TILE
TAIL_ROWS = 3
TAIL_P = (NODES - FULL * TILE) // TAIL_ROWS
TILES = FULL + 1

EP, CH = 125, 4
GROUP = EP * CH
GROUPS = EDGES // GROUP
assert GROUPS * GROUP == EDGES and GROUPS % 2 == 0 and FULL * TILE + TAIL_P * TAIL_ROWS == NODES

LO = -(-NODES // P)
EC = EDGES // EP

SPARE = NODES
FILL = GROUPS // 2
FILL_ROWS = 16
SCRATCH_ROWS = P * FILL * FILL_ROWS
assert SCRATCH_ROWS >= SPARE + GROUP and LO * P <= SCRATCH_ROWS
W1COLS = D + 8


def after(engine, semaphore, value):
    if isinstance(value, int) and value <= 0:
        return
    engine.wait_ge(semaphore, value)


def before_fixed(engine, carried):
    engine.sem_inc(carried, 1)


class Chain:

    def __init__(self, engine, semaphore, per, rnd, carried=None):
        self.engine, self.semaphore, self.per, self.rnd, self.n, self.carried = engine, semaphore, per, rnd, 0, carried

    def link(self, instruction):
        instruction.then_inc(self.semaphore, 1)
        self.n += 1

    def now(self):
        self.engine.wait_ge(self.semaphore, self.rnd * self.per + self.n)
        if self.carried is not None:
            before_fixed(self.engine, self.carried)

    def end(self):
        assert self.n == self.per, (self.n, self.per)


def build_gps(nc, x, src, dst, edge_weight, W1, b1, W2, b2, Wqkv, Wproj, bproj, ln_g, ln_b,
              Wg1, bg1, Wg2, bg2, ffn_w, ffn_b, out):
    f32, bf16, i32 = mybir.dt.float32, mybir.dt.bfloat16, mybir.dt.int32
    ALU, ACT, AX = mybir.AluOpType, mybir.ActivationFunctionType, mybir.AxisListType

    with ExitStack() as ctx:
        def sb(name, shape, dt=f32):
            return ctx.enter_context(nc.sbuf_tensor(name, shape, dt))

        def ps(name, shape, dt=f32):
            return ctx.enter_context(nc.psum_tensor(name, shape, dt))

        def sem(name):
            return ctx.enter_context(nc.semaphore(name))

        def sems(name):
            return [sem(f"{name}0"), sem(f"{name}1")]

        def two(name, shape, dt=f32):
            return [sb(f"{name}0", shape, dt), sb(f"{name}1", shape, dt)]

        dinv_d = nc.dram_tensor("dinv_d", (P * LO, 1), f32, kind="Internal").ap()
        agg1_d = nc.dram_tensor("agg1_d", (SCRATCH_ROWS, W1COLS), f32, kind="Internal").ap()
        agg2_d = nc.dram_tensor("agg2_d", (SCRATCH_ROWS, D), f32, kind="Internal").ap()
        msg_d = nc.dram_tensor("msg_d", (EDGES, D), f32, kind="Internal").ap()
        dsrc_d = nc.dram_tensor("dsrc_d", (EDGES,), f32, kind="Internal").ap()

        wqkv = sb("wqkv", [P, 2, 3 * D])
        w1, w2, wproj = sb("w1", [P, 2, D]), sb("w2", [P, 2, D]), sb("wproj", [P, 2, D])
        wffn = sb("wffn", [P, 2, D])
        wg1, wg2 = sb("wg1", [P, 2, GATE]), sb("wg2", [GATE, D])
        b1c, lngc, lnbc, bg2c = sb("b1c", [P, 2]), sb("lngc", [P, 2]), sb("lnbc", [P, 2]), sb("bg2c", [P, 2])
        b1_row, b2_row, bproj_row = sb("b1_row", [P, D]), sb("b2_row", [P, D]), sb("bproj_row", [P, D])
        ffnb_row, bg1_row = sb("ffnb_row", [P, D]), sb("bg1_row", [P, GATE])
        ident = sb("ident", [P, P])
        zeros = sb("zeros", [P, FILL_ROWS * W1COLS])
        minus_half = sb("minus_half", [P, LO])
        tri = sb("tri", [EP, GROUP])
        spare = sb("spare", [EP, CH])
        headmask = sb("headmask", [P, 2, D])
        w1T, wqT = sb("w1T", [P, 2, D]), sb("wqT", [P, 2, D])
        wA, wB = sb("wA", [P, 2, D]), sb("wB", [P, 2, D])
        wM = sb("wM", [P, 2, D])
        wg1g = sb("wg1g", [P, 2, GATE])
        b1b, lnbb = sb("b1b", [P, 2, P]), sb("lnbb", [P, 2, P])
        wabsT, wsgnT = sb("wabsT", [P, 2, D]), sb("wsgnT", [P, 2, D], bf16)
        s_row, c_row, h_row = sb("s_row", [P, D]), sb("c_row", [P, D]), sb("h_row", [P, GATE])

        xt = two("xt", [P, ROWS, D])
        stat = two("stat", [P, ROWS, 6])
        mv = two("mv", [P, ROWS, 2])
        veps, rstd, nmean, nmr = two("veps", [P, ROWS]), two("rstd", [P, ROWS]), two("nmean", [P, ROWS]), two("nmr", [P, ROWS])
        xn = two("xn", [P, ROWS, D])
        xnT = sb("xnT", [P, 2, TILE])

        pT = ps("pT", [P, 2, TILE])
        pK = ps("pK", [P, 2, TILE])
        narrow = ctx.enter_context(ExitStack())
        pG = narrow.enter_context(nc.psum_tensor("pG", [P, 2, D], f32))
        pB = narrow.enter_context(nc.psum_tensor("pB", [P, 512], f32))
        pC = [narrow.enter_context(nc.psum_tensor(f"pC{n}", [P, 512], f32)) for n in range(2)]

        rows_ready, carried_pool, carried_pe, carried_dve = sem("rows_ready"), sem("carried_pool"), sem("carried_pe"), sem("carried_dve")
        loaded, setup_pool, setup_dve, setup_pe, setup_act = (
            sem("loaded"), sem("setup_pool"), sem("setup_dve"), sem("setup_pe"), sem("setup_act"))

        N_LOADS = 18
        with ExitStack() as s0:
            def sb0(name, shape, dt=f32):
                return s0.enter_context(nc.sbuf_tensor(name, shape, dt))

            dst_i = sb0("dst_i", [EP, EC], i32)
            ew_all = sb0("ew_all", [EP, EC])
            dstf, hi, lo, fix = sb0("dstf", [EP, EC]), sb0("hi", [EP, EC]), sb0("lo", [EP, EC]), sb0("fix", [EP, EC])
            hi_i = sb0("hi_i", [EP, EC], i32)
            iota_hi, iota_lo = sb0("iota_hi", [EP, P]), sb0("iota_lo", [EP, LO])
            UN = 4
            oneh = [sb0(f"oneh{u}", [EP, P]) for u in range(UN)]
            onel = [sb0(f"onel{u}", [EP, LO]) for u in range(UN)]
            deg, dpos, dinv = sb0("deg", [P, LO]), sb0("dpos", [P, LO]), sb0("dinv", [P, LO])
            dpow = sb0("dpow", [P, LO])
            hot_ready, hot_used = sem("hot_ready"), sem("hot_used")
            deg_sum, deg_ready, pow_ready, dinv_ready, dinv_stored, zero1 = (
                sem("deg_sum"), sem("deg_ready"), sem("pow_ready"), sem("dinv_ready"), sem("dinv_stored"), sem("zero1"))
            deg_steps, row_steps, abs_ready = sem("deg_steps"), sem("row_steps"), sem("abs_ready")
            block = s0.enter_context(nc.Block())

            @block.sync
            def _(sp):
                sp.dma_start(dst_i[:, :], dst.rearrange("(p c) -> p c", c=EC)).then_inc(loaded, 16)
                sp.dma_start(ew_all[:, :], edge_weight.rearrange("(p c) -> p c", c=EC)).then_inc(loaded, 16)
                for tile, w in ((wqkv, Wqkv), (w1, W1), (w2, W2), (wproj, Wproj), (wffn, ffn_w), (wg1, Wg1)):
                    sp.dma_start(tile[:, :, :], w.rearrange("(c p) n -> p c n", p=P)).then_inc(loaded, 16)
                sp.dma_start(wg2[:, :], Wg2[:, :]).then_inc(loaded, 16)
                with nc.allow_non_contiguous_dma("four short columns of parameters"):
                    for tile, v in ((b1c, b1), (lngc, ln_g), (lnbc, ln_b), (bg2c, bg2)):
                        sp.dma_start(tile[:, :], v.rearrange("(c p) -> p c", p=P)).then_inc(loaded, 16)
                for tile, v in ((b1_row, b1), (b2_row, b2), (bproj_row, bproj), (ffnb_row, ffn_b), (bg1_row, bg1)):
                    sp.dma_start(tile[:, :], v.rearrange("(a n) -> a n", a=1).partition_broadcast(P)).then_inc(loaded, 16)
                sp.wait_ge(dinv_ready, 1)
                sp.dma_start(dinv_d.rearrange("(p c) a -> p (c a)", c=LO), dinv[:, :]).then_inc(dinv_stored, 16)
                sp.wait_ge(dinv_stored, 16)

            @block.gpsimd
            def _(pool):
                pool.iota(iota_hi[:, :], [[1, P]], base=0, channel_multiplier=0, allow_small_or_imprecise_dtypes=True)
                pool.iota(iota_lo[:, :], [[1, LO]], base=0, channel_multiplier=0, allow_small_or_imprecise_dtypes=True).then_inc(setup_pool, 1)
                pool.memset(zeros[:, :], 0.0).then_inc(setup_pool, 1)
                pool.memset(minus_half[:, :], -0.5)
                pool.iota(spare[:, :], [[1, CH]], base=SPARE, channel_multiplier=CH, allow_small_or_imprecise_dtypes=True)
                pool.memset(ident[:, :], 0.0)
                pool.memset(headmask[:, :, :], 1.0)
                pool.memset(tri[:, :], 1.0).then_inc(setup_pool, 1)
                pool.wait_ge(setup_pool, 3)
                pool.affine_select(out=ident[:, :], in_=ident[:, :], compare_op=ALU.not_equal, fill=1.0,
                                   base=0, pattern=[[-1, P]], channel_multiplier=1)
                pool.affine_select(out=tri[:, 0:EP], in_=tri[:, 0:EP], compare_op=ALU.is_ge, fill=0.0,
                                   base=0, pattern=[[1, EP]], channel_multiplier=-1)
                per_chunk = P // HD
                for c in range(2):
                    m = headmask[:, c, :].rearrange("p (h v) -> p h v", v=HD)
                    last = pool.affine_select(out=m, in_=m, compare_op=ALU.is_ge, fill=0.0,
                                              base=c * P, pattern=[[-HD, HEADS], [0, HD]], channel_multiplier=1)
                last.then_inc(setup_pool, 1)
                pool.wait_ge(setup_pool, 4)
                for c in range(2):
                    m = headmask[:, c, :].rearrange("p (h v) -> p h v", v=HD)
                    last = pool.affine_select(out=m, in_=m, compare_op=ALU.is_ge, fill=0.0,
                                              base=HD - 1 - c * P, pattern=[[HD, HEADS], [0, HD]], channel_multiplier=-1)
                last.then_inc(setup_pool, 1)
                pool.wait_ge(deg_ready, 1)
                pool.tensor_tensor(dpow[:, :], deg[:, :], minus_half[:, 0:LO], ALU.pow).then_inc(pow_ready, 1)

            @block.vector
            def _(dve):
                v = nc.vector
                dve.wait_ge(loaded, 16 * N_LOADS)
                dve.wait_ge(setup_pool, 5)
                ch = Chain(dve, setup_dve, 8, 0)
                ch.link(v.tensor_copy(dstf[:, :], dst_i[:, :]))
                ch.now()
                ch.link(v.tensor_scalar(hi_i[:, :], dstf[:, :], 1.0 / LO, -0.5, ALU.mult, ALU.add))
                ch.now()
                ch.link(v.tensor_copy(hi[:, :], hi_i[:, :]))
                ch.now()
                ch.link(v.scalar_tensor_tensor(lo[:, :], hi[:, :], -float(LO), dstf[:, :], ALU.mult, ALU.add))
                ch.now()
                v.tensor_scalar(fix[:, :], lo[:, :], float(LO) - 0.5, None, ALU.is_gt)
                ch.link(v.tensor_scalar(hi_i[:, :], lo[:, :], -0.5, None, ALU.is_lt))
                ch.now()
                ch.link(v.tensor_tensor(fix[:, :], fix[:, :], hi_i[:, :], ALU.subtract))
                ch.now()
                ch.link(v.tensor_tensor(hi[:, :], hi[:, :], fix[:, :], ALU.add))
                ch.link(v.scalar_tensor_tensor(lo[:, :], fix[:, :], -float(LO), lo[:, :], ALU.mult, ALU.add))
                ch.now()
                ch.end()

                def hot(i, u):
                    c = i * UN + u
                    after(dve, hot_used, c - UN + 1)
                    col = slice(c, c + 1) if isinstance(c, int) else bass.ds(c, 1)
                    v.tensor_scalar(oneh[u][:, :], iota_hi[:, :], hi[:, col], None, ALU.is_equal)
                    v.tensor_scalar(onel[u][:, :], iota_lo[:, :], lo[:, col], ew_all[:, col],
                                    ALU.is_equal, ALU.mult).then_inc(hot_ready, 1)

                for u in range(UN):
                    hot(0, u)
                with dve.Fori(1, EC // UN) as i:
                    for u in range(UN):
                        hot(i, u)
                dve.wait_ge(deg_sum, 1)
                ch = Chain(dve, deg_steps, 1, 0)
                ch.link(v.tensor_scalar(deg[:, :], pB[:, 0:LO], 1.0, None, ALU.add))
                ch.now()
                ch.end()
                v.tensor_scalar(dpos[:, :], deg[:, :], 0.0, None, ALU.is_gt)
                v.tensor_scalar(deg[:, :], deg[:, :], DEG_FLOOR, None, ALU.max).then_inc(deg_ready, 1)
                dve.wait_ge(pow_ready, 1)
                v.tensor_tensor(dinv[:, :], dpow[:, :], dpos[:, :], ALU.mult).then_inc(dinv_ready, 1)
                v.tensor_tensor(wB[:, :, :], w1[:, :, :], w2[:, :, :], ALU.add)
                for c in range(2):
                    v.tensor_scalar(wg1g[:, c, :], wg1[:, c, :], lngc[:, c:c + 1], None, ALU.mult)
                    v.tensor_copy(b1b[:, c, :], b1c[:, c:c + 1].broadcast_to([P, P]))
                    v.tensor_copy(lnbb[:, c, :], lnbc[:, c:c + 1].broadcast_to([P, P]))
                v.tensor_scalar(b1_row[:, :], b1_row[:, :], MIX * KEEP, None, ALU.mult)
                ch = Chain(dve, row_steps, 2, 0)
                v.tensor_scalar(bg2c[:, :], bg2c[:, :], 0.5, None, ALU.mult)
                ch.link(v.tensor_scalar(wproj[:, :, :], wproj[:, :, :], 0.5, None, ALU.mult))
                ch.now()
                ch.link(v.scalar_tensor_tensor(c_row[:, :], b2_row[:, :], MIX, b1_row[:, :], ALU.mult, ALU.add))
                ch.now()
                v.tensor_scalar(wB[:, :, :], wB[:, :, :], MIX * KEEP, None, ALU.mult)
                v.tensor_tensor(c_row[:, :], c_row[:, :], bproj_row[:, :], ALU.add).then_inc(rows_ready, 1)
                ch.end()
                dve.wait_ge(setup_pe, 1)
                v.tensor_copy(w1T[:, :, :], pT[:, 0, :].rearrange("p (c n) -> p c n", c=2))
                v.tensor_copy(wqT[:, :, :], pT[:, 1, :].rearrange("p (c n) -> p c n", c=2)).then_inc(setup_act, 1)
                dve.wait_ge(abs_ready, 1)
                v.tensor_scalar(wabsT[:, :, :], wabsT[:, :, :], FFN_EPS, None, ALU.add)
                dve.wait_ge(setup_pe, 2)
                v.tensor_scalar(wA[:, :, :], pG[:, :, :], MIX * MIX, None, ALU.mult)
                v.tensor_scalar(s_row[:, :], pC[0][:, 0:D], MIX * MIX, None, ALU.mult)
                v.tensor_tensor(h_row[:, :], pC[1][:, 0:GATE], bg1_row[:, :], ALU.add).then_inc(setup_act, 1)

            @block.tensor
            def _(pe):
                t = nc.tensor
                pe.wait_ge(setup_pool, 5)
                t.matmul(pB[:, 0:LO], zeros[0:EP, 0:P], zeros[0:EP, 0:LO], start=True, stop=False)

                def add_chunk(i, u):
                    pe.wait_ge(hot_ready, i * UN + u + 1)
                    t.matmul(pB[:, 0:LO], oneh[u][:, :], onel[u][:, :], start=False, stop=False).then_inc(hot_used, 1)

                with pe.Fori(0, EC // UN) as i:
                    for u in range(UN):
                        add_chunk(i, u)
                t.matmul(pB[:, 0:LO], zeros[0:EP, 0:P], zeros[0:EP, 0:LO], start=False, stop=True).then_inc(deg_sum, 1)
                pe.wait_ge(loaded, 16 * N_LOADS)
                for area, w in ((pT[:, 0, :], w1), (pT[:, 1, :], wqkv), (pK[:, 0, :], wffn)):
                    for c in range(2):
                        for k in range(2):
                            last = t.transpose(area[:, k * D + c * P:k * D + (c + 1) * P], w[:, c, k * P:(k + 1) * P], ident[:, :])
                last.then_inc(setup_pe, 1)
                pe.wait_ge(setup_act, 1)
                pe.wait_ge(rows_ready, 1)
                for c in range(2):
                    for k in range(2):
                        t.matmul(pG[:, c, :], w1T[:, k, c * P:(c + 1) * P], w2[:, k, :], start=k == 0, stop=k == 1)
                for k in range(2):
                    t.matmul(pC[0][:, 0:D], b1b[:, k, :], w2[:, k, :], start=k == 0, stop=k == 1)
                for k in range(2):
                    last = t.matmul(pC[1][:, 0:GATE], lnbb[:, k, :], wg1[:, k, :], start=k == 0, stop=k == 1)
                last.then_inc(setup_pe, 1)

            @block.scalar
            def _(act):
                act.wait_ge(setup_pool, 2)
                with act.Fori(0, FILL) as i:
                    act.dma_start(agg1_d.rearrange("(k p r) w -> k p (r w)", k=FILL, p=P)[bass.ds(i, 1), :, :].rearrange("k p n -> (k p) n"),
                                  zeros[:, :]).then_inc(zero1, 16)
                act.wait_ge(setup_pe, 1)
                nc.scalar.activation(wabsT[:, :, :], pK[:, 0, :].rearrange("p (c n) -> p c n", c=2), ACT.Abs).then_inc(abs_ready, 1)
                nc.scalar.activation(wsgnT[:, :, :], pK[:, 0, :].rearrange("p (c n) -> p c n", c=2), ACT.Sign)
                act.wait_ge(zero1, 16 * FILL)

        E2 = GROUPS * 2
        gsum = sb("gsum", [P, 2, D])
        esum = sb("esum", [P, 2])
        with ExitStack() as s1:
            def sb1(name, shape, dt=f32):
                return s1.enter_context(nc.sbuf_tensor(name, shape, dt))

            def two1(name, shape, dt=f32):
                return [sb1(f"{name}0", shape, dt), sb1(f"{name}1", shape, dt)]

            eT = sb1("eT", [P, 2, TILE])
            en = two1("en", [P, ROWS, D])
            blkmax = sb1("blkmax", [P, 2])
            kmax, negmax, drop, alpha, rsum = (two1("kmax", [P, 2]), two1("negmax", [P, 2]), two1("drop", [P, 2]),
                                               two1("alpha", [P, 2]), two1("rsum", [P, 2]))
            esrc, edst = two1("esrc", [EP, CH], i32), two1("edst", [EP, CH], i32)
            eew, dsrc, edstf = two1("eew", [EP, CH]), two1("dsrc", [EP, CH]), two1("edstf", [EP, CH])
            xg = two1("xg", [EP, CH, W1COLS])
            xgd = [a[:, :, :].rearrange("p c w -> p (c w)")[:, 0:CH * D].rearrange("p (c w) -> p c w", c=CH) for a in xg]
            m1t = two1("m1t", [EP, CH, D])
            estat_t, emv = two1("estat_t", [EP, CH, 6]), two1("emv", [EP, CH, 2])
            everp, erstd, enmean, enmr = (two1("everp", [EP, CH]), two1("erstd", [EP, CH]),
                                          two1("enmean", [EP, CH]), two1("enmr", [EP, CH]))
            coef, ca, cb = two1("coef", [EP, CH]), two1("ca", [EP, CH]), two1("cb", [EP, CH])
            msg = two1("msg", [EP, CH, W1COLS])
            same = sb1("same", [EP, CH, GROUP])
            cnt, toodd, rowf = sb1("cnt", [EP, CH]), sb1("toodd", [EP, CH]), sb1("rowf", [EP, CH])
            rowi = two1("rowi", [EP, CH], i32)
            comb = two1("comb", [EP, CH, W1COLS])
            comb2 = [a[:, :, :].rearrange("p c w -> p (c w)")[:, 0:CH * D].rearrange("p (c w) -> p c w", c=CH) for a in comb]

            x_in, e_in, g_in, m_in, m_out = sems("x_in"), sems("e_in"), sems("g_in"), sems("m_in"), sems("m_out")
            zero2, scattered = sem("zero2"), sem("scattered")
            (stat_r, rstd_r, xn_r, xT_p, xT_r, k_p, max_r, e_r, en_p, en_r, g_p, g_r) = (sem(n) for n in (
                "stat_r", "rstd_r", "xn_r", "xT_p", "xT_r", "k_p", "max_r", "e_r", "en_p", "en_r", "g_p", "g_r"))
            (dst_r, estat_r, erstd_r, msg_r, row_p, same_r, comb_p, comb_r) = (sem(n) for n in (
                "dst_r", "estat_r", "erstd_r", "msg_r", "row_p", "same_r", "comb_p", "comb_r"))
            n_steps, e_steps, r_steps, er_steps, init = sem("n_steps"), sem("e_steps"), sem("r_steps"), sem("er_steps"), sem("init")
            s_steps, e2_steps = sem("s_steps"), sem("e2_steps")
            block = s1.enter_context(nc.Block())

            def nodes_of(array, t, rows, parts, width):
                first = t * TILE
                view = array[first:first + parts * rows, :] if isinstance(first, int) else array[bass.ds(first, parts * rows), :]
                return view.rearrange("(p r) w -> p (r w)", r=rows)

            def group_of(vector, g):
                first = g * GROUP
                view = vector[first:first + GROUP] if isinstance(first, int) else vector[bass.ds(first, GROUP)]
                return view.rearrange("(p c) -> p c", c=CH)

            def group_rows(array, g):
                first = g * GROUP
                view = array[first:first + GROUP, :] if isinstance(first, int) else array[bass.ds(first, GROUP), :]
                return view.rearrange("(p c) w -> p (c w)", c=CH)

            def shape(t):
                return (TAIL_P, TAIL_ROWS) if isinstance(t, int) and t == FULL else (P, ROWS)

            def walk(engine, step):
                half = GROUPS // 2
                step(0, 0, 1)
                step(0, 1, 1)
                with engine.Fori(1, half) as i:
                    for b in range(2):
                        step(i, b, 1)
                with engine.Fori(half, FULL // 2) as i:
                    for b in range(2):
                        step(i, b, 2)
                for i in range(FULL // 2, GROUPS):
                    for b in range(2):
                        step(i, b, 2)

            def has_tile(t):
                return not (isinstance(t, int) and t >= TILES)

            @block.sync
            def _(sp):
                def step(i, b, layer):
                    t = 2 * i + b
                    if has_tile(t):
                        parts, rows = shape(t)
                        after(sp, xn_r, t - 1)
                        sp.dma_start(xt[b][0:parts, 0:rows, :].rearrange("p r w -> p (r w)"), nodes_of(x, t, rows, parts, D)).then_inc(x_in[b], 16)
                    g = t if layer == 1 else t - GROUPS
                    after(sp, msg_r, t - 1)
                    after(sp, same_r, t - 1)
                    for tile, vec in ((esrc, src), (edst, dst), (eew, edge_weight)):
                        sp.dma_start(tile[b][:, :], group_of(vec, g)).then_inc(e_in[b], 16)
                    if layer == 1:
                        if b == 0:
                            row = i * P * FILL_ROWS
                            view = agg2_d[row:row + P * FILL_ROWS, :] if isinstance(row, int) else agg2_d[bass.ds(row, P * FILL_ROWS), :]
                            sp.dma_start(view.rearrange("(p r) w -> p (r w)", p=P), zeros[:, 0:FILL_ROWS * D]).then_inc(zero2, 16)
                        keep(t - 1, 1 - b)
                    else:
                        sp.dma_start(dsrc[b][:, :], group_of(dsrc_d, g)).then_inc(m_in[b], 16)
                        sp.dma_start(m1t[b][:, :, :].rearrange("p c w -> p (c w)"), group_rows(msg_d, g)).then_inc(m_in[b], 16)

                def keep(t, b):
                    if isinstance(t, int) and t < 0:
                        return
                    sp.wait_ge(msg_r, t + 1)
                    sp.dma_start(group_rows(msg_d, t).rearrange("p (c w) -> p c w", c=CH), msg[b][:, :, 0:D]).then_inc(m_out[b], 16)
                    sp.dma_start(group_of(dsrc_d, t), dsrc[b][:, :]).then_inc(m_out[b], 16)

                half = GROUPS // 2
                step(0, 0, 1)
                step(0, 1, 1)
                with sp.Fori(1, half) as i:
                    for b in range(2):
                        step(i, b, 1)
                keep(GROUPS - 1, 1)
                for b in range(2):
                    sp.wait_ge(m_out[b], 32 * half)
                with sp.Fori(half, FULL // 2) as i:
                    for b in range(2):
                        step(i, b, 2)
                for i in range(FULL // 2, GROUPS):
                    for b in range(2):
                        step(i, b, 2)
                sp.wait_ge(zero2, 16 * FILL)

            @block.gpsimd
            def _(pool):
                def gathers(i, b, layer):
                    t = 2 * i + b
                    after(pool, msg_r, t - 1)
                    pool.wait_ge(e_in[b], 48 * (i + 1))
                    if layer == 1:
                        after(pool, m_out[b], 32 * i)
                    before_fixed(pool, carried_pool)
                    if layer == 1:
                        for c in range(CH):
                            where = bass.IndirectOffsetOnAxis(esrc[b][:, c:c + 1], 0)
                            pool.indirect_dma_start(xg[b][:, c, 0:D], None, x[:, :], where).then_inc(g_in[b], 16)
                            pool.indirect_dma_start(dsrc[b][:, c:c + 1], None, dinv_d[:, :], where).then_inc(g_in[b], 16)
                    else:
                        for c in range(CH):
                            where = bass.IndirectOffsetOnAxis(esrc[b][:, c:c + 1], 0)
                            pool.indirect_dma_start(xg[b][:, c, :], None, agg1_d[:, :], where).then_inc(g_in[b], 16)

                def inverse_root(ch, mvt, ve, r, nm, nr, parts, rows):
                    ch.link(pool.tensor_scalar(ve[0:parts, 0:rows], mvt[0:parts, 0:rows, 1], LN_EPS, None, ALU.add))
                    pool.tensor_scalar(nm[0:parts, 0:rows], mvt[0:parts, 0:rows, 0], -1.0, None, ALU.mult)
                    ch.now()
                    ch.link(pool.tensor_tensor(r[0:parts, 0:rows], ve[0:parts, 0:rows], minus_half[0:parts, 0:rows], ALU.pow))
                    ch.now()
                    return pool.tensor_tensor(nr[0:parts, 0:rows], nm[0:parts, 0:rows], r[0:parts, 0:rows], ALU.mult)

                def tile_root(t, b):
                    if not has_tile(t):
                        return
                    parts, rows = shape(t)
                    pool.wait_ge(stat_r, t + 1)
                    before_fixed(pool, carried_pool)
                    ch = Chain(pool, r_steps, 2, t, carried_pool)
                    inverse_root(ch, mv[b], veps[b], rstd[b], nmean[b], nmr[b], parts, rows).then_inc(rstd_r, 1)
                    ch.end()

                def step(i, b, layer, ahead=True):
                    t = 2 * i + b
                    if layer == 1:
                        pool.wait_ge(estat_r, t + 1)
                        before_fixed(pool, carried_pool)
                        ch = Chain(pool, er_steps, 2, t, carried_pool)
                        inverse_root(ch, emv[b], everp[b], erstd[b], enmean[b], enmr[b], EP, CH).then_inc(erstd_r, 1)
                        ch.end()
                    if ahead:
                        gathers(i + (1 if b else 0), 1 - b, layer)
                    tile_root(t + 1, 1 - b)
                    if not isinstance(t, int) or t > 0:
                        pool.wait_ge(scattered, 64 * t)
                    pool.wait_ge(comb_r, CH * (t + 1))
                    before_fixed(pool, carried_pool)
                    for c in range(CH):
                        where = bass.IndirectOffsetOnAxis(rowi[b][:, c:c + 1], 0)
                        if layer == 1:
                            pool.indirect_dma_start(agg1_d[:, :], where, comb[b][:, c, :], None,
                                                    compute_op=ALU.add).then_inc(scattered, 16)
                        else:
                            pool.indirect_dma_start(agg2_d[:, :], where, comb2[b][:, c, :], None,
                                                    compute_op=ALU.add).then_inc(scattered, 16)

                for b in range(2):
                    pool.memset(comb[b][:, :, :], 0.0)
                    pool.memset(msg[b][:, :, :], 0.0)
                pool.memset(gsum[:, :, :], 0.0)
                pool.memset(esum[:, :], 0.0)
                pool.memset(kmax[1][:, :], -1e30).then_inc(init, 1)
                tile_root(0, 0)
                gathers(0, 0, 1)
                half = GROUPS // 2
                step(0, 0, 1)
                step(0, 1, 1)
                with pool.Fori(1, half - 1) as i:
                    for b in range(2):
                        step(i, b, 1)
                step(half - 1, 0, 1)
                step(half - 1, 1, 1, ahead=False)
                pool.wait_ge(scattered, 64 * GROUPS)
                gathers(half, 0, 2)
                pool.wait_ge(zero2, 16 * FILL)
                with pool.Fori(half, FULL // 2) as i:
                    for b in range(2):
                        step(i, b, 2)
                for i in range(FULL // 2, GROUPS):
                    step(i, 0, 2)
                    step(i, 1, 2, ahead=i < GROUPS - 1)
                pool.wait_ge(scattered, 64 * E2)

            @block.vector
            def _(dve):
                v = nc.vector

                def statistics(source, st, agg, parts, rows, ch):
                    for r in range(rows):
                        last = v.bn_stats(st[0:parts, r, :], source[0:parts, r, 0:D])
                    ch.link(last)
                    ch.now()
                    for r in range(rows):
                        last = v.bn_aggr(agg[0:parts, r, :], st[0:parts, r, :])
                    return last

                def tile_stats(i, b):
                    t = 2 * i + b
                    if not has_tile(t):
                        return
                    parts, rows = shape(t)
                    dve.wait_ge(x_in[b], 16 * (i + 1))
                    ch = Chain(dve, s_steps, 1, t, carried_dve)
                    statistics(xt[b], stat[b], mv[b], parts, rows, ch).then_inc(stat_r, 1)
                    ch.end()

                def tile_norm(i, b):
                    t = 2 * i + b
                    if not has_tile(t):
                        return
                    parts, rows = shape(t)
                    dve.wait_ge(rstd_r, t + 1)
                    after(dve, g_p, t - 1)
                    for r in range(rows):
                        last = v.tensor_scalar(xn[b][0:parts, r, :], xt[b][0:parts, r, :], rstd[b][0:parts, r:r + 1],
                                               nmr[b][0:parts, r:r + 1], ALU.mult, ALU.add)
                    last.then_inc(xn_r, 1)

                def running_max(t, b):
                    parts, rows = shape(t)
                    n = parts * rows
                    dve.wait_ge(k_p, t + 1)
                    ch = Chain(dve, n_steps, 2, t)
                    ch.link(v.reduce_max(blkmax[:, :], pK[:, :, 0:n], AX.X))
                    ch.now()
                    ch.link(v.tensor_tensor(kmax[b][:, :], kmax[1 - b][:, :], blkmax[:, :], ALU.max))
                    ch.now()
                    ch.end()
                    v.tensor_scalar(negmax[b][:, :], kmax[b][:, :], -1.0, None, ALU.mult)
                    v.tensor_tensor(drop[b][:, :], kmax[1 - b][:, :], kmax[b][:, :], ALU.subtract).then_inc(max_r, 1)

                def add_sums(t, b):
                    if isinstance(t, int) and (t < 0 or t >= TILES):
                        return
                    dve.wait_ge(g_p, t + 1)
                    for c in range(2):
                        v.scalar_tensor_tensor(gsum[:, c, :], gsum[:, c, :], alpha[b][:, c:c + 1], pG[:, c, :], ALU.mult, ALU.add)
                        last = v.scalar_tensor_tensor(esum[:, c:c + 1], esum[:, c:c + 1], alpha[b][:, c:c + 1], rsum[b][:, c:c + 1], ALU.mult, ALU.add)
                    last.then_inc(g_r, 1)

                def step(i, b, layer):
                    t = 2 * i + b
                    dve.wait_ge(e_in[b], 48 * (i + 1))
                    after(dve, row_p, t - 1)
                    v.tensor_copy(edstf[b][:, :], edst[b][:, :]).then_inc(dst_r, 1)
                    if layer == 1:
                        dve.wait_ge(g_in[b], 16 * 2 * CH * (i + 1))
                    else:
                        dve.wait_ge(g_in[b], 16 * 2 * CH * (GROUPS // 2) + 16 * CH * (i + 1 - GROUPS // 2))
                        dve.wait_ge(m_in[b], 32 * (i + 1 - GROUPS // 2))
                    ch = Chain(dve, e_steps, 6, t, carried_dve) if layer == 1 else Chain(dve, e2_steps, 5, t - GROUPS)
                    if layer == 1:
                        statistics(xg[b], estat_t[b], emv[b], EP, CH, ch).then_inc(estat_r, 1)
                        ch.link(v.tensor_tensor(coef[b][:, :], eew[b][:, :], dsrc[b][:, :], ALU.mult))
                    else:
                        ch.link(v.tensor_tensor(ca[b][:, :], dsrc[b][:, :], dsrc[b][:, :], ALU.mult))
                        ch.now()
                        ch.link(v.tensor_tensor(cb[b][:, :], ca[b][:, :], eew[b][:, :], ALU.mult))
                        ch.now()
                    dve.wait_ge(row_p, t + 1)
                    after(dve, comb_p, CH * t)
                    for c in range(CH):
                        v.scalar_tensor_tensor(same[:, c, c * EP:GROUP], pB[0:EP, c * EP:GROUP], edstf[b][:, c:c + 1],
                                               tri[:, 0:GROUP - c * EP], ALU.is_equal, ALU.mult, accum_out=cnt[:, c:c + 1])
                    ch.link(v.tensor_tensor(rowf[:, :], spare[:, :], edstf[b][:, :], ALU.subtract))
                    ch.now()
                    ch.link(v.scalar_tensor_tensor(toodd[:, :], cnt[:, :], 1.5, rowf[:, :], ALU.is_gt, ALU.mult))
                    ch.now()
                    after(dve, scattered, 64 * (t - 1))
                    v.tensor_tensor(rowi[b][:, :], toodd[:, :], edstf[b][:, :], ALU.add).then_inc(same_r, 1)
                    if not isinstance(t, int) or t >= 2:
                        dve.wait_ge(comb_p, CH * (t - 1))
                    if layer == 1:
                        dve.wait_ge(erstd_r, t + 1)
                        if not isinstance(i, int) or i > 0:
                            dve.wait_ge(m_out[b], 32 * i)
                        ch.link(v.tensor_tensor(ca[b][:, :], erstd[b][:, :], coef[b][:, :], ALU.mult))
                        ch.link(v.tensor_tensor(cb[b][:, :], enmr[b][:, :], coef[b][:, :], ALU.mult))
                        ch.now()
                        for c in range(CH):
                            v.tensor_scalar(msg[b][:, c, 0:D], xg[b][:, c, 0:D], ca[b][:, c:c + 1], cb[b][:, c:c + 1], ALU.mult, ALU.add)
                        v.tensor_copy(msg[b][:, :, D], coef[b][:, :]).then_inc(msg_r, 1)
                    else:
                        dve.wait_ge(m_out[b], 32 * (GROUPS // 2))
                        for c in range(CH):
                            last = v.tensor_scalar(m1t[b][:, c, :], m1t[b][:, c, :], ca[b][:, c:c + 1], None, ALU.mult)
                        ch.link(last)
                        ch.now()
                        for c in range(CH):
                            last = v.scalar_tensor_tensor(msg[b][:, c, 0:D], xg[b][:, c, 0:D], cb[b][:, c:c + 1], m1t[b][:, c, :], ALU.mult, ALU.add)
                        last.then_inc(msg_r, 1)
                    ch.end()
                    nxt = (i + (1 if b else 0), 1 - b)
                    tile_stats(*nxt)
                    add_sums(t - 1, 1 - b)
                    if has_tile(t):
                        running_max(t, b)
                    tile_norm(*nxt)

                dve.wait_ge(init, 1)
                tile_stats(0, 0)
                tile_norm(0, 0)
                walk(dve, step)

            @block.tensor
            def _(pe):
                te = nc.tensor

                def sums(t, b):
                    if isinstance(t, int) and (t < 0 or t >= TILES):
                        return
                    parts, rows = shape(t)
                    pe.wait_ge(en_r, t + 1)
                    after(pe, g_r, t)
                    for c in range(2):
                        for r in range(rows):
                            last = te.matmul(pG[:, c, :], en[b][0:parts, r, c * P:(c + 1) * P], xn[b][0:parts, r, :],
                                             start=r == 0, stop=r == rows - 1)
                    last.then_inc(g_p, 1)

                def step(i, b, layer):
                    t = 2 * i + b
                    if has_tile(t):
                        parts, rows = shape(t)
                        pe.wait_ge(xn_r, t + 1)
                        after(pe, en_r, t)
                        for c in range(2):
                            for r in range(rows):
                                last = te.transpose(pT[:, c, r * parts:(r + 1) * parts], xn[b][0:parts, r, c * P:(c + 1) * P],
                                                    ident[0:parts, 0:parts])
                        last.then_inc(xT_p, 1)
                    sums(t - 1, 1 - b)
                    pe.wait_ge(dst_r, t + 1)
                    after(pe, same_r, t)
                    for c in range(CH):
                        last = te.matmul(pB[0:EP, c * EP:(c + 1) * EP], edstf[b][:, c:c + 1].broadcast_to([EP, EP]), ident[0:EP, 0:EP],
                                         start=True, stop=True)
                    last.then_inc(row_p, 1)
                    if has_tile(t):
                        n = parts * rows
                        pe.wait_ge(xT_r, t + 1)
                        after(pe, e_r, t)
                        for c in range(2):
                            for k in range(2):
                                last = te.matmul(pK[:, c, 0:n], wqkv[:, k, D + c * P:D + (c + 1) * P], xnT[:, k, 0:n],
                                                 start=k == 0, stop=k == 1)
                        last.then_inc(k_p, 1)
                    width = D + 1 if layer == 1 else D
                    pe.wait_ge(same_r, t + 1)
                    pe.wait_ge(msg_r, t + 1)
                    for c in range(CH):
                        if not (isinstance(t, int) and t == 0 and c < 2):
                            pe.wait_ge(comb_r, CH * t + c - 1)
                        for k in range(c + 1):
                            last = te.matmul(pC[c % 2][0:EP, 0:width], same[:, k, c * EP:(c + 1) * EP], msg[b][:, k, 0:width],
                                             start=k == 0, stop=k == c)
                        last.then_inc(comb_p, 1)
                    if has_tile(t):
                        pe.wait_ge(e_r, t + 1)
                        for r in range(rows):
                            for c in range(2):
                                last = te.transpose(pT[0:parts, r // 2, (r % 2) * D + c * P:(r % 2) * D + (c + 1) * P],
                                                    eT[:, c, r * parts:(r + 1) * parts], ident[:, :])
                        last.then_inc(en_p, 1)

                walk(pe, step)

            @block.scalar
            def _(act):
                a = nc.scalar

                def step(i, b, layer):
                    t = 2 * i + b
                    if has_tile(t):
                        parts, rows = shape(t)
                        n = parts * rows
                        act.wait_ge(xT_p, t + 1)
                        after(act, k_p, t)
                        for c in range(2):
                            last = a.activation(xnT[:, c, 0:n], pT[:, c, 0:n], ACT.Copy)
                        last.then_inc(xT_r, 1)
                        act.wait_ge(max_r, t + 1)
                        after(act, en_p, t)
                        after(act, g_r, t - 1)
                        for c in range(2):
                            a.activation(eT[:, c, 0:n], pK[:, c, 0:n], ACT.Exp, bias=negmax[b][:, c:c + 1], accum_out=rsum[b][:, c:c + 1])
                        a.activation(alpha[b][:, :], drop[b][:, :], ACT.Exp).then_inc(e_r, 1)
                    after(act, scattered, 64 * (t - 1))
                    for c in range(CH):
                        act.wait_ge(comb_p, CH * t + c + 1)
                        if layer == 1:
                            last = a.activation(comb[b][:, c, 0:D + 1], pC[c % 2][0:EP, 0:D + 1], ACT.Copy)
                        else:
                            last = a.activation(comb2[b][:, c, :], pC[c % 2][0:EP, 0:D], ACT.Copy)
                        last.then_inc(comb_r, 1)
                    if has_tile(t):
                        act.wait_ge(en_p, t + 1)
                        after(act, g_p, t - 1)
                        for r in range(0, rows, 2):
                            w = min(2, rows - r)
                            last = a.activation(en[b][0:parts, r:r + w, :], pT[0:parts, r // 2, 0:w * D].rearrange("p (r n) -> p r n", r=w), ACT.Copy)
                        last.then_inc(en_r, 1)

                act.wait_ge(init, 1)
                walk(act, step)

        with ExitStack() as s2:
            rinv = s2.enter_context(nc.sbuf_tensor("rinv", [P, 2], f32))
            ctxn = s2.enter_context(nc.sbuf_tensor("ctxn", [P, 2, D], f32))
            ctxT = s2.enter_context(nc.sbuf_tensor("ctxT", [P, 2, D], f32))
            ctxb = s2.enter_context(nc.sbuf_tensor("ctxb", [P, 2, D], f32))
            c_dve, c_pe = sem("c_dve"), sem("c_pe")
            block = s2.enter_context(nc.Block())

            @block.vector
            def _(dve):
                v = nc.vector
                v.reciprocal(rinv[:, :], esum[:, :]).then_inc(c_dve, 1)
                dve.wait_ge(c_dve, 1)
                for c in range(2):
                    last = v.tensor_scalar(ctxn[:, c, :], gsum[:, c, :], rinv[:, c:c + 1], None, ALU.mult)
                last.then_inc(c_dve, 1)
                dve.wait_ge(c_pe, 1)
                v.tensor_copy(ctxT[:, :, :], pT[:, 0, :].rearrange("p (c n) -> p c n", c=2)).then_inc(c_dve, 1)
                dve.wait_ge(c_pe, 2)
                v.tensor_tensor(ctxb[:, :, :], pG[:, :, :], headmask[:, :, :], ALU.mult).then_inc(c_dve, 1)
                dve.wait_ge(c_pe, 3)
                v.tensor_copy(wM[:, :, :], pK[:, 0, :].rearrange("p (c n) -> p c n", c=2)).then_inc(c_dve, 1)

            @block.tensor
            def _(pe):
                t = nc.tensor
                pe.wait_ge(c_dve, 2)
                for c in range(2):
                    for k in range(2):
                        last = t.transpose(pT[:, 0, k * D + c * P:k * D + (c + 1) * P], ctxn[:, c, k * P:(k + 1) * P], ident[:, :])
                last.then_inc(c_pe, 1)
                pe.wait_ge(c_dve, 3)
                for c in range(2):
                    for k in range(2):
                        last = t.matmul(pG[:, c, :], ctxT[:, k, c * P:(c + 1) * P], wqkv[:, k, 2 * D:3 * D], start=k == 0, stop=k == 1)
                last.then_inc(c_pe, 1)
                pe.wait_ge(c_dve, 4)
                for c in range(2):
                    for k in range(2):
                        last = t.matmul(pK[:, 0, c * D:(c + 1) * D], wqT[:, k, c * P:(c + 1) * P], ctxb[:, k, :], start=k == 0, stop=k == 1)
                last.then_inc(c_pe, 1)

        narrow.close()
        pA = ps("pA", [P, 2, TILE])
        pZ = ps("pZ", [P, 2, TILE])
        pO = pK

        a1, a2, dv = two("a1", [P, ROWS, W1COLS]), two("a2", [P, ROWS, D]), two("dv", [P, ROWS])
        dd, deg1, mix2, mixn = two("dd", [P, ROWS]), two("deg1", [P, ROWS]), two("mix2", [P, ROWS]), two("mixn", [P, ROWS])
        var2, rsq, r2 = two("var2", [P, ROWS]), two("rsq", [P, ROWS]), two("r2", [P, ROWS])
        u1, u2 = sb("u1", [P, ROWS, D]), sb("u2", [P, ROWS, D])
        u1T, u2T, yT, gT = sb("u1T", [P, 2, TILE]), sb("u2T", [P, 2, TILE]), sb("yT", [P, 2, TILE]), sb("gT", [P, 2, TILE])
        hpre, hid = sb("hpre", [P, ROWS, GATE]), sb("hid", [P, ROWS, GATE])
        hT = sb("hT", [GATE, TILE])
        xb, x2 = two("xb", [P, ROWS, D]), two("x2", [P, ROWS, D])
        stat2, mv2 = sb("stat2", [P, ROWS, 6]), sb("mv2", [P, ROWS, 2])
        ve2, rstd2, nm2, nmr2 = sb("ve2", [P, ROWS]), sb("rstd2", [P, ROWS]), sb("nm2", [P, ROWS]), sb("nmr2", [P, ROWS])
        xf = sb("xf", [P, ROWS, D])
        absT, sgnT = sb("absT", [P, 2, TILE]), sb("sgnT", [P, 2, TILE], bf16)
        osgn = sb("osgn", [P, ROWS, D], bf16)
        prod, x2b, res = sb("prod", [P, ROWS, D]), sb("x2b", [P, ROWS, D]), two("res", [P, ROWS, D])

        t_in, t_out = sems("t_in"), sems("t_out")
        (tstat_r, troot_r, scaled_r, base_r, tnorm_r, u_r, xnT_p, xnT_r, u1_p, u1T_r, u2_p, u2T_r, h_p, hpre_r, hid_r,
         hT_p, hT_r, o_p, gate_p, gate_r, y_r, z_p, x2_r, fstat_r, froot_r, xf_r, xf_p, sgnT_r, absT_r, ffn_p, osgn_r, prod_r,
         bias_r, res_r) = (sem(n) for n in (
             "tstat_r", "troot_r", "scaled_r", "base_r", "tnorm_r", "u_r", "xnT_p", "xnT_r", "u1_p", "u1T_r", "u2_p", "u2T_r",
             "h_p", "hpre_r", "hid_r", "hT_p", "hT_r", "o_p", "gate_p", "gate_r", "y_r", "z_p", "x2_r", "fstat_r",
             "froot_r", "xf_r", "xf_p", "sgnT_r", "absT_r", "ffn_p", "osgn_r", "prod_r", "bias_r", "res_r"))
        absx_r = sem("absx_r")
        ts_steps, tu_steps, tx_steps, tr_steps, fr_steps = sem("ts_steps"), sem("tu_steps"), sem("tx_steps"), sem("tr_steps"), sem("fr_steps")
        block = ctx.enter_context(nc.Block())

        def tile_rows(array, t):
            if isinstance(t, int):
                first = min(t * TILE, NODES - TILE)
                view = array[first:first + TILE, :]
            else:
                view = array[bass.ds(t * TILE, TILE), :]
            return view.rearrange("(p r) w -> p (r w)", r=ROWS)

        def flat(tile):
            return tile[:, :, :].rearrange("p r w -> p (r w)")

        def halves(bank_pair):
            return bank_pair[:, :, :].rearrange("p c (r n) -> p (c r) n", n=D)

        def walk_tiles(engine, step):
            step(0, 0)
            step(0, 1)
            with engine.Fori(1, FULL // 2) as i:
                for b in range(2):
                    step(i, b)
            step(FULL // 2, 0)
            step(FULL // 2, 1)
            step(FULL // 2 + 1, 0)

        def runs(t):
            return not isinstance(t, int) or 0 <= t < TILES

        @block.sync
        def _(sp):
            def load(i, b):
                t = 2 * i + b
                if not runs(t):
                    return
                after(sp, base_r, t - 1)
                after(sp, tnorm_r, t - 1)
                after(sp, u_r, t - 1)
                sp.dma_start(flat(xt[b]), tile_rows(x, t)).then_inc(t_in[b], 16)
                sp.dma_start(dv[b][:, :], tile_rows(dinv_d, t)).then_inc(t_in[b], 16)
                sp.dma_start(flat(a1[b]), tile_rows(agg1_d, t)).then_inc(t_in[b], 16)
                sp.dma_start(flat(a2[b]), tile_rows(agg2_d, t)).then_inc(t_in[b], 16)

            def store(i, b):
                t = 2 * i + b
                if isinstance(t, int) and t < 0:
                    return
                sp.wait_ge(res_r, t + 1)
                if isinstance(t, int) and t == TILES - 1:
                    sp.wait_ge(t_out[0], 16 * (FULL // 2 + 1))
                sp.dma_start(tile_rows(out, t), flat(res[b])).then_inc(t_out[b], 16)

            def step(i, b):
                load(i + (1 if b else 0), 1 - b)
                store(i - 1, b)

            load(0, 0)
            walk_tiles(sp, step)
            store(FULL // 2, 1)
            for b in range(2):
                sp.wait_ge(t_out[b], 16 * (FULL // 2 + 1))

        @block.gpsimd
        def _(pool):
            def prepare(i, b):
                t = 2 * i + b
                if not runs(t):
                    return
                pool.wait_ge(t_in[b], 64 * (i + 1))
                after(pool, x2_r, t - 1)
                before_fixed(pool, carried_pool)
                ch = Chain(pool, tr_steps, 9, t, carried_pool)
                ch.link(pool.tensor_tensor(dd[b][:, :], dv[b][:, :], dv[b][:, :], ALU.mult))
                ch.link(pool.tensor_tensor(deg1[b][:, :], dv[b][:, :], a1[b][:, :, D], ALU.mult))
                ch.now()
                pool.tensor_tensor(deg1[b][:, :], deg1[b][:, :], dd[b][:, :], ALU.add)
                for r in range(ROWS):
                    pool.tensor_scalar(a1[b][:, r, 0:D], a1[b][:, r, 0:D], dv[b][:, r:r + 1], None, ALU.mult)
                    last = pool.tensor_scalar(a2[b][:, r, :], a2[b][:, r, :], dv[b][:, r:r + 1], None, ALU.mult)
                last.then_inc(scaled_r, 1)
                pool.wait_ge(tstat_r, t + 1)
                after(pool, hpre_r, t - 1)
                before_fixed(pool, carried_pool)
                ch.link(pool.tensor_scalar(veps[b][:, :], mv[b][:, :, 1], LN_EPS, None, ALU.add))
                pool.tensor_scalar(nmean[b][:, :], mv[b][:, :, 0], -1.0, None, ALU.mult)
                ch.now()
                ch.link(pool.tensor_tensor(rstd[b][:, :], veps[b][:, :], minus_half[:, 0:ROWS], ALU.pow))
                ch.now()
                pool.tensor_tensor(nmr[b][:, :], nmean[b][:, :], rstd[b][:, :], ALU.mult).then_inc(troot_r, 1)
                ch.link(pool.tensor_tensor(rsq[b][:, :], rstd[b][:, :], rstd[b][:, :], ALU.mult))
                ch.now()
                ch.link(pool.tensor_tensor(var2[b][:, :], rsq[b][:, :], mv[b][:, :, 1], ALU.mult))
                ch.now()
                ch.link(pool.tensor_scalar(var2[b][:, :], var2[b][:, :], LN_EPS, None, ALU.add))
                ch.now()
                pool.tensor_tensor(r2[b][:, :], var2[b][:, :], minus_half[:, 0:ROWS], ALU.pow)
                pool.tensor_scalar(mixn[b][:, :], nmr[b][:, :], KEEP * KEEP, None, ALU.mult)
                ch.link(pool.tensor_scalar(mix2[b][:, :], rstd[b][:, :], KEEP * KEEP, 1.0, ALU.mult, ALU.add))
                ch.now()
                for r in range(ROWS):
                    last = pool.tensor_scalar(xb[b][:, r, :], xt[b][:, r, :], mix2[b][:, r:r + 1], mixn[b][:, r:r + 1], ALU.mult, ALU.add)
                ch.link(last)
                ch.now()
                for r in range(ROWS):
                    last = pool.tensor_tensor(xb[b][:, r, :], xb[b][:, r, :], c_row[:, :], ALU.add)
                last.then_inc(base_r, 1)
                ch.end()

            def step(i, b):
                t = 2 * i + b
                prepare(i + (1 if b else 0), 1 - b)
                if runs(t - 1):
                    pool.wait_ge(bias_r, t)
                    pool.wait_ge(prod_r, t)
                    pi = i - 1 if b == 0 else i
                    after(pool, t_out[1 - b], 16 * pi)
                    before_fixed(pool, carried_pool)
                    pool.tensor_tensor(res[1 - b][:, :, :], prod[:, :, :], x2b[:, :, :], ALU.add).then_inc(res_r, 1)
                if runs(t):
                    pool.wait_ge(fstat_r, t + 1)
                    if not isinstance(t, int) or t > 0:
                        pool.wait_ge(res_r, t)
                    before_fixed(pool, carried_pool)
                    ch = Chain(pool, fr_steps, 2, t, carried_pool)
                    ch.link(pool.tensor_scalar(ve2[:, :], mv2[:, :, 1], LN_EPS, None, ALU.add))
                    pool.tensor_scalar(nm2[:, :], mv2[:, :, 0], -1.0, None, ALU.mult)
                    ch.now()
                    ch.link(pool.tensor_tensor(rstd2[:, :], ve2[:, :], minus_half[:, 0:ROWS], ALU.pow))
                    ch.now()
                    ch.end()
                    pool.tensor_tensor(nmr2[:, :], nm2[:, :], rstd2[:, :], ALU.mult).then_inc(froot_r, 1)
                    for r in range(ROWS):
                        last = pool.tensor_tensor(x2b[:, r, :], x2[b][:, r, :], ffnb_row[:, :], ALU.add)
                    last.then_inc(bias_r, 1)

            prepare(0, 0)
            walk_tiles(pool, step)

        @block.vector
        def _(dve):
            v = nc.vector

            def statistics(i, b):
                t = 2 * i + b
                if not runs(t):
                    return
                dve.wait_ge(t_in[b], 64 * (i + 1))
                if not isinstance(t, int) or t > 1:
                    dve.wait_ge(base_r, t - 1)
                ch = Chain(dve, ts_steps, 1, t, carried_dve)
                for r in range(ROWS):
                    last = v.bn_stats(stat[b][:, r, :], xt[b][:, r, :])
                ch.link(last)
                ch.now()
                ch.end()
                for r in range(ROWS):
                    last = v.bn_aggr(mv[b][:, r, :], stat[b][:, r, :])
                last.then_inc(tstat_r, 1)

            def features(i, b):
                t = 2 * i + b
                if not runs(t):
                    return
                dve.wait_ge(troot_r, t + 1)
                after(dve, xnT_p, t - 1)
                for r in range(ROWS):
                    last = v.tensor_scalar(xn[b][:, r, :], xt[b][:, r, :], rstd[b][:, r:r + 1], nmr[b][:, r:r + 1], ALU.mult, ALU.add)
                last.then_inc(tnorm_r, 1)
                dve.wait_ge(scaled_r, t + 1)
                after(dve, u2_p, t)
                dve.wait_ge(tnorm_r, t + 1)
                ch = Chain(dve, tu_steps, 1, t)
                for r in range(ROWS):
                    last = v.scalar_tensor_tensor(u1[:, r, :], xn[b][:, r, :], dd[b][:, r:r + 1], a1[b][:, r, 0:D], ALU.mult, ALU.add)
                ch.link(last)
                ch.now()
                ch.end()
                for r in range(ROWS):
                    last = v.scalar_tensor_tensor(u2[:, r, :], u1[:, r, :], dd[b][:, r:r + 1], a2[b][:, r, :], ALU.mult, ALU.add)
                last.then_inc(u_r, 1)

            def step(i, b):
                t = 2 * i + b
                nxt = (i + (1 if b else 0), 1 - b)
                if runs(t):
                    dve.wait_ge(base_r, t + 1)
                    dve.wait_ge(h_p, t + 1)
                    for r in range(ROWS):
                        last = v.scalar_tensor_tensor(hpre[:, r, :], pA[:, 0, r * GATE:(r + 1) * GATE], r2[b][:, r:r + 1], h_row[:, :], ALU.mult, ALU.add)
                    last.then_inc(hpre_r, 1)
                statistics(*nxt)
                if runs(t - 1):
                    dve.wait_ge(absx_r, t)
                    v.tensor_scalar(absT[:, :, :], absT[:, :, :], FFN_EPS, None, ALU.add).then_inc(absT_r, 1)
                if runs(t):
                    dve.wait_ge(o_p, t + 1)
                    dve.wait_ge(gate_r, t + 1)
                    v.scalar_tensor_tensor(yT[:, :, :], gT[:, :, :], 1.0, pO[:, :, :], ALU.add, ALU.mult).then_inc(y_r, 1)
                if runs(t - 1):
                    dve.wait_ge(ffn_p, t)
                    dve.wait_ge(osgn_r, t)
                    after(dve, res_r, t - 1)
                    v.tensor_tensor(prod[:, :, :], halves(pZ), osgn[:, :, :], ALU.mult).then_inc(prod_r, 1)
                features(*nxt)
                if runs(t):
                    ch = Chain(dve, tx_steps, 2, t, carried_dve)
                    after(dve, bias_r, t - 1)
                    for r in range(ROWS):
                        last = v.scalar_tensor_tensor(x2[b][:, r, :], s_row[:, :], deg1[b][:, r:r + 1], xb[b][:, r, :], ALU.mult, ALU.add)
                    ch.link(last)
                    ch.now()
                    for half in range(2):
                        dve.wait_ge(z_p, 2 * t + half + 1)
                        rows = slice(2 * half, 2 * half + 2)
                        last = v.tensor_tensor(x2[b][:, rows, :], x2[b][:, rows, :], pZ[:, half, :].rearrange("p (r n) -> p r n", n=D), ALU.add)
                    last.then_inc(x2_r, 1)
                    dve.wait_ge(x2_r, t + 1)
                    after(dve, froot_r, t)
                    for r in range(ROWS):
                        last = v.bn_stats(stat2[:, r, :], x2[b][:, r, :])
                    ch.link(last)
                    ch.now()
                    ch.end()
                    for r in range(ROWS):
                        last = v.bn_aggr(mv2[:, r, :], stat2[:, r, :])
                    last.then_inc(fstat_r, 1)
                    dve.wait_ge(froot_r, t + 1)
                    after(dve, xf_p, t)
                    for r in range(ROWS):
                        last = v.tensor_scalar(xf[:, r, :], x2[b][:, r, :], rstd2[:, r:r + 1], nmr2[:, r:r + 1], ALU.mult, ALU.add)
                    last.then_inc(xf_r, 1)

            statistics(0, 0)
            features(0, 0)
            walk_tiles(dve, step)

        @block.tensor
        def _(pe):
            te = nc.tensor

            def turn(area, rows_tile):
                for c in range(2):
                    for r in range(ROWS):
                        last = te.transpose(area[:, c, r * P:(r + 1) * P], rows_tile[:, r, c * P:(c + 1) * P], ident[:, :])
                return last

            def step(i, b):
                t = 2 * i + b
                if runs(t):
                    pe.wait_ge(tnorm_r, t + 1)
                    after(pe, osgn_r, t - 1)
                    turn(pT, xn[b]).then_inc(xnT_p, 1)
                    pe.wait_ge(u_r, t + 1)
                    after(pe, y_r, t)
                    turn(pO, u1).then_inc(u1_p, 1)
                    pe.wait_ge(xnT_r, t + 1)
                    after(pe, gate_r, t)
                    for r in range(ROWS):
                        for k in range(2):
                            last = te.matmul(pA[:, 0, r * GATE:(r + 1) * GATE], xnT[:, k, r * P:(r + 1) * P], wg1g[:, k, :], start=k == 0, stop=k == 1)
                    last.then_inc(h_p, 1)
                    turn(pT, u2).then_inc(u2_p, 1)
                    pe.wait_ge(u1T_r, t + 1)
                    for c in range(2):
                        for k in range(2):
                            last = te.matmul(pO[:, c, :], wM[:, k, c * P:(c + 1) * P], xnT[:, k, :], start=k == 0, stop=k == 1)
                    last.then_inc(o_p, 1)
                    pe.wait_ge(hid_r, t + 1)
                    before_fixed(pe, carried_pe)
                    for r in range(ROWS):
                        last = te.transpose(pA[0:GATE, 1, r * P:(r + 1) * P], hid[:, r, :], ident[:, :])
                    last.then_inc(hT_p, 1)
                if runs(t - 1):
                    pe.wait_ge(xf_r, t)
                    if runs(t):
                        pe.wait_ge(u2T_r, t + 1)
                    else:
                        pe.wait_ge(osgn_r, t - 1)
                    turn(pT, xf).then_inc(xf_p, 1)
                if runs(t):
                    pe.wait_ge(hT_r, t + 1)
                    for c in range(2):
                        last = te.matmul(pA[:, c, :], wg2[:, c * P:(c + 1) * P], hT[:, :], start=True, stop=True)
                    last.then_inc(gate_p, 1)
                if runs(t - 1):
                    pe.wait_ge(absT_r, t)
                    pe.wait_ge(sgnT_r, t)
                    pe.wait_ge(x2_r, t)
                    acc, sg = halves(pZ), halves(pT)
                    for r in range(ROWS):
                        for k in range(2):
                            te.matmul(sg[:, r, :], sgnT[:, k, r * P:(r + 1) * P], wsgnT[:, k, :], start=k == 0, stop=k == 1)
                    for r in range(ROWS):
                        for k in range(2):
                            last = te.matmul(acc[:, r, :], absT[:, k, r * P:(r + 1) * P], wabsT[:, k, :], start=k == 0, stop=k == 1)
                    last.then_inc(ffn_p, 1)
                if runs(t):
                    pe.wait_ge(u2T_r, t + 1)
                    pe.wait_ge(y_r, t + 1)
                    after(pe, prod_r, t)
                    z = halves(pZ)
                    for r in range(ROWS):
                        parts = [(u1T, wB), (u2T, wA), (yT, wproj)]
                        for n, (a, w) in enumerate(parts):
                            for k in range(2):
                                last = te.matmul(z[:, r, :], a[:, k, r * P:(r + 1) * P], w[:, k, :], start=n == 0 and k == 0, stop=n == 2 and k == 1)
                        if r % 2 == 1:
                            last.then_inc(z_p, 1)

            walk_tiles(pe, step)

        @block.scalar
        def _(act):
            a = nc.scalar

            def copy2(dst_tile, area):
                for c in range(2):
                    last = a.activation(dst_tile[:, c, :], area[:, c, :], ACT.Copy)
                return last

            def step(i, b):
                t = 2 * i + b
                if runs(t):
                    act.wait_ge(xnT_p, t + 1)
                    copy2(xnT, pT).then_inc(xnT_r, 1)
                    act.wait_ge(u1_p, t + 1)
                    copy2(u1T, pO).then_inc(u1T_r, 1)
                    act.wait_ge(hpre_r, t + 1)
                    a.activation(hid[:, :, :], hpre[:, :, :], ACT.Gelu).then_inc(hid_r, 1)
                    act.wait_ge(u2_p, t + 1)
                    copy2(u2T, pT).then_inc(u2T_r, 1)
                    act.wait_ge(hT_p, t + 1)
                    a.activation(hT[:, :], pA[0:GATE, 1, :], ACT.Copy).then_inc(hT_r, 1)
                if runs(t - 1):
                    act.wait_ge(xf_p, t)
                    a.activation(absT[:, :, :], pT[:, :, :], ACT.Abs).then_inc(absx_r, 1)
                    a.activation(sgnT[:, :, :], pT[:, :, :], ACT.Sign).then_inc(sgnT_r, 1)
                if runs(t):
                    act.wait_ge(gate_p, t + 1)
                    after(act, y_r, t)
                    for c in range(2):
                        last = a.activation(gT[:, c, :], pA[:, c, :], ACT.Tanh, bias=bg2c[:, c:c + 1], scale=0.5)
                    last.then_inc(gate_r, 1)
                if runs(t - 1):
                    act.wait_ge(ffn_p, t)
                    after(act, prod_r, t - 1)
                    a.activation(osgn[:, :, :], halves(pT), ACT.Sign).then_inc(osgn_r, 1)

            walk_tiles(act, step)


_INS = ["x", "src", "dst", "edge_weight", "L0_gnn_W1", "L0_gnn_b1", "L0_gnn_W2", "L0_gnn_b2", "L0_mix_Wqkv", "L0_mix_Wproj",
        "L0_mix_bproj", "L0_mix_ln_g", "L0_mix_ln_b", "L0_mix_Wg1", "L0_mix_bg1", "L0_mix_Wg2", "L0_mix_bg2",
        "L0_ffn_weight", "L0_ffn_bias"]


def kernel(**inputs):
    import numpy as _np
    import concourse.bacc as _bacc
    from concourse import mybir as _mybir
    from concourse.bass_utils import run_bass_kernel_spmd as _run

    nc = _bacc.Bacc("TRN2", target_bir_lowering=False, num_devices=1)
    arrays, args = {}, []
    for name in _INS:
        a = _np.ascontiguousarray(inputs[name])
        arrays[f"in_{name}"] = a
        args.append(nc.dram_tensor(f"in_{name}", a.shape, _mybir.dt.from_np(a.dtype), kind="ExternalInput").ap())
    args.append(nc.dram_tensor("out_0", (NODES, D), _mybir.dt.float32, kind="ExternalOutput").ap())
    build_gps(nc, *args)
    r = _run(nc, [arrays], core_ids=[0])
    return r.results[0]["out_0"]
```

```python
from contextlib import ExitStack

import concourse.bass as bass
from concourse import mybir

NODES, D, EDGES = 50000, 256, 25000
HEADS, GATE = 8, 64
HD = D // HEADS
KEEP = 0.1
MIX = 1.0 - KEEP
LN_EPS, FFN_EPS, DEG_FLOOR = 1e-5, 1e-8, 1e-30

P, ROWS = 128, 4
TILE = P * ROWS
FULL = NODES // TILE
TAIL_ROWS = 3
TAIL_P = (NODES - FULL * TILE) // TAIL_ROWS
TILES = FULL + 1

EP, CH = 125, 4
GROUP = EP * CH
GROUPS = EDGES // GROUP
assert GROUPS * GROUP == EDGES and GROUPS % 2 == 0 and FULL * TILE + TAIL_P * TAIL_ROWS == NODES

LO = -(-NODES // P)
EC = EDGES // EP

SPARE = NODES
FILL = GROUPS // 2
FILL_ROWS = 16
SCRATCH_ROWS = P * FILL * FILL_ROWS
assert SCRATCH_ROWS >= SPARE + GROUP and LO * P <= SCRATCH_ROWS
W1COLS = D + 8


def after(engine, semaphore, value):
    if isinstance(value, int) and value <= 0:
        return
    engine.wait_ge(semaphore, value)


def before_fixed(engine, carried):
    engine.sem_inc(carried, 1)


class Chain:

    def __init__(self, engine, semaphore, per, rnd, carried=None):
        self.engine, self.semaphore, self.per, self.rnd, self.n, self.carried = engine, semaphore, per, rnd, 0, carried

    def link(self, instruction):
        instruction.then_inc(self.semaphore, 1)
        self.n += 1

    def now(self):
        self.engine.wait_ge(self.semaphore, self.rnd * self.per + self.n)
        if self.carried is not None:
            before_fixed(self.engine, self.carried)

    def end(self):
        assert self.n == self.per, (self.n, self.per)


def build_gps(nc, x, src, dst, edge_weight, W1, b1, W2, b2, Wqkv, Wproj, bproj, ln_g, ln_b,
              Wg1, bg1, Wg2, bg2, ffn_w, ffn_b, out):
    f32, f32r, bf16, i32 = mybir.dt.float32, mybir.dt.float32r, mybir.dt.bfloat16, mybir.dt.int32
    ALU, ACT, AX = mybir.AluOpType, mybir.ActivationFunctionType, mybir.AxisListType

    with ExitStack() as ctx:
        def sb(name, shape, dt=f32):
            return ctx.enter_context(nc.sbuf_tensor(name, shape, dt))

        def ps(name, shape, dt=f32):
            return ctx.enter_context(nc.psum_tensor(name, shape, dt))

        def sem(name):
            return ctx.enter_context(nc.semaphore(name))

        def parts_of(name, shape):
            return sb(f"{name}_hi", shape, f32r), sb(f"{name}_lo", shape, f32r)

        PASSES = ((0, 0), (0, 1), (1, 0))

        def sems(name):
            return [sem(f"{name}0"), sem(f"{name}1")]

        def two(name, shape, dt=f32):
            return [sb(f"{name}0", shape, dt), sb(f"{name}1", shape, dt)]

        dinv_d = nc.dram_tensor("dinv_d", (P * LO, 1), f32, kind="Internal").ap()
        agg1_d = nc.dram_tensor("agg1_d", (SCRATCH_ROWS, W1COLS), f32, kind="Internal").ap()
        agg2_d = nc.dram_tensor("agg2_d", (SCRATCH_ROWS, D), f32, kind="Internal").ap()
        msg_d = nc.dram_tensor("msg_d", (EDGES, D), f32, kind="Internal").ap()
        dsrc_d = nc.dram_tensor("dsrc_d", (EDGES,), f32, kind="Internal").ap()

        wqkv = sb("wqkv", [P, 2, 3 * D])
        wg2, bg2c = sb("wg2", [GATE, D]), sb("bg2c", [P, 2])
        ffnb_row, bg1_row = sb("ffnb_row", [P, D]), sb("bg1_row", [P, GATE])
        ident = sb("ident", [P, P])
        minus_half = sb("minus_half", [P, LO])
        headmask = sb("headmask", [P, 2, D])
        wqT, wM = sb("wqT", [P, 2, D]), sb("wM", [P, 2, D])
        wsgnT = sb("wsgnT", [P, 2, D], bf16)
        wA_s, wB_s, wproj_s, wabsT_s, wM_s = (parts_of(n, [P, 2, D]) for n in ("wA", "wB", "wproj", "wabsT", "wM"))
        wg1g_s = parts_of("wg1g", [P, 2, GATE])
        ones, c_parts = sb("ones", [2, P], f32r), sb("c_parts", [2, 2, D], f32r)
        s_row, c_row, h_row = sb("s_row", [P, D]), sb("c_row", [P, D]), sb("h_row", [P, GATE])

        xt = two("xt", [P, ROWS, D])
        stat = two("stat", [P, ROWS, 6])
        mv = two("mv", [P, ROWS, 2])
        veps, rstd, nmean, nmr = two("veps", [P, ROWS]), two("rstd", [P, ROWS]), two("nmean", [P, ROWS]), two("nmr", [P, ROWS])
        xn = two("xn", [P, ROWS, D])
        xnT = sb("xnT", [P, 2, TILE])

        gsum = sb("gsum", [P, 2, D])
        esum = sb("esum", [P, 2])

        early = ctx.enter_context(ExitStack())

        def sbe(name, shape, dt=f32):
            return early.enter_context(nc.sbuf_tensor(name, shape, dt))

        w1, w2, wproj, wffn = (sbe(n, [P, 2, D]) for n in ("w1", "w2", "wproj", "wffn"))
        w1T, wA, wB, wabsT = (sbe(n, [P, 2, D]) for n in ("w1T", "wA", "wB", "wabsT"))
        wg1, wg1g = sbe("wg1", [P, 2, GATE]), sbe("wg1g", [P, 2, GATE])
        b1c, lngc, lnbc = sbe("b1c", [P, 2]), sbe("lngc", [P, 2]), sbe("lnbc", [P, 2])
        b1b, lnbb = sbe("b1b", [P, 2, P]), sbe("lnbb", [P, 2, P])
        b1_row, b2_row, bproj_row = sbe("b1_row", [P, D]), sbe("b2_row", [P, D]), sbe("bproj_row", [P, D])
        c_hi, c_lo, c_steps = sbe("c_hi", [2, D], f32r), sbe("c_lo", [2, D]), sem("c_steps")
        zeros = sbe("zeros", [P, FILL_ROWS * W1COLS])
        tri = sbe("tri", [EP, GROUP])
        spare = sbe("spare", [EP, CH])

        pT = ps("pT", [P, 2, TILE])
        pK = ps("pK", [P, 2, TILE])
        narrow = ctx.enter_context(ExitStack())
        pG = narrow.enter_context(nc.psum_tensor("pG", [P, 2, D], f32))
        pB = narrow.enter_context(nc.psum_tensor("pB", [P, 512], f32))
        pC = [narrow.enter_context(nc.psum_tensor(f"pC{n}", [P, 512], f32)) for n in range(2)]

        rows_ready, carried_pool, carried_pe, carried_dve = sem("rows_ready"), sem("carried_pool"), sem("carried_pe"), sem("carried_dve")
        split_r = sem("split_r")
        loaded, setup_pool, setup_dve, setup_pe, setup_act = (
            sem("loaded"), sem("setup_pool"), sem("setup_dve"), sem("setup_pe"), sem("setup_act"))

        N_LOADS = 18
        with ExitStack() as s0:
            def sb0(name, shape, dt=f32):
                return s0.enter_context(nc.sbuf_tensor(name, shape, dt))

            dst_i = sb0("dst_i", [EP, EC], i32)
            ew_all = sb0("ew_all", [EP, EC])
            dstf, hi, lo, fix = sb0("dstf", [EP, EC]), sb0("hi", [EP, EC]), sb0("lo", [EP, EC]), sb0("fix", [EP, EC])
            hi_i = sb0("hi_i", [EP, EC], i32)
            iota_hi, iota_lo = sb0("iota_hi", [EP, P]), sb0("iota_lo", [EP, LO])
            UN = 4
            oneh = [sb0(f"oneh{u}", [EP, P]) for u in range(UN)]
            onel = [sb0(f"onel{u}", [EP, LO]) for u in range(UN)]
            deg, dpos, dinv = sb0("deg", [P, LO]), sb0("dpos", [P, LO]), sb0("dinv", [P, LO])
            dpow = sb0("dpow", [P, LO])
            hot_ready, hot_used = sem("hot_ready"), sem("hot_used")
            deg_sum, deg_ready, pow_ready, dinv_ready, dinv_stored, zero1 = (
                sem("deg_sum"), sem("deg_ready"), sem("pow_ready"), sem("dinv_ready"), sem("dinv_stored"), sem("zero1"))
            deg_steps, row_steps, abs_ready = sem("deg_steps"), sem("row_steps"), sem("abs_ready")
            block = s0.enter_context(nc.Block())

            @block.sync
            def _(sp):
                sp.dma_start(dst_i[:, :], dst.rearrange("(p c) -> p c", c=EC)).then_inc(loaded, 16)
                sp.dma_start(ew_all[:, :], edge_weight.rearrange("(p c) -> p c", c=EC)).then_inc(loaded, 16)
                for tile, w in ((wqkv, Wqkv), (w1, W1), (w2, W2), (wproj, Wproj), (wffn, ffn_w), (wg1, Wg1)):
                    sp.dma_start(tile[:, :, :], w.rearrange("(c p) n -> p c n", p=P)).then_inc(loaded, 16)
                sp.dma_start(wg2[:, :], Wg2[:, :]).then_inc(loaded, 16)
                with nc.allow_non_contiguous_dma("four short columns of parameters"):
                    for tile, v in ((b1c, b1), (lngc, ln_g), (lnbc, ln_b), (bg2c, bg2)):
                        sp.dma_start(tile[:, :], v.rearrange("(c p) -> p c", p=P)).then_inc(loaded, 16)
                for tile, v in ((b1_row, b1), (b2_row, b2), (bproj_row, bproj), (ffnb_row, ffn_b), (bg1_row, bg1)):
                    sp.dma_start(tile[:, :], v.rearrange("(a n) -> a n", a=1).partition_broadcast(P)).then_inc(loaded, 16)
                sp.wait_ge(dinv_ready, 1)
                sp.dma_start(dinv_d.rearrange("(p c) a -> p (c a)", c=LO), dinv[:, :]).then_inc(dinv_stored, 16)
                sp.wait_ge(dinv_stored, 16)

            @block.gpsimd
            def _(pool):
                pool.iota(iota_hi[:, :], [[1, P]], base=0, channel_multiplier=0, allow_small_or_imprecise_dtypes=True)
                pool.iota(iota_lo[:, :], [[1, LO]], base=0, channel_multiplier=0, allow_small_or_imprecise_dtypes=True).then_inc(setup_pool, 1)
                pool.memset(zeros[:, :], 0.0).then_inc(setup_pool, 1)
                pool.memset(minus_half[:, :], -0.5)
                pool.iota(spare[:, :], [[1, CH]], base=SPARE, channel_multiplier=CH, allow_small_or_imprecise_dtypes=True)
                pool.memset(ident[:, :], 0.0)
                pool.memset(headmask[:, :, :], 1.0)
                pool.memset(tri[:, :], 1.0).then_inc(setup_pool, 1)
                pool.wait_ge(setup_pool, 3)
                pool.affine_select(out=ident[:, :], in_=ident[:, :], compare_op=ALU.not_equal, fill=1.0,
                                   base=0, pattern=[[-1, P]], channel_multiplier=1)
                pool.affine_select(out=tri[:, 0:EP], in_=tri[:, 0:EP], compare_op=ALU.is_ge, fill=0.0,
                                   base=0, pattern=[[1, EP]], channel_multiplier=-1)
                per_chunk = P // HD
                for c in range(2):
                    m = headmask[:, c, :].rearrange("p (h v) -> p h v", v=HD)
                    last = pool.affine_select(out=m, in_=m, compare_op=ALU.is_ge, fill=0.0,
                                              base=c * P, pattern=[[-HD, HEADS], [0, HD]], channel_multiplier=1)
                last.then_inc(setup_pool, 1)
                pool.wait_ge(setup_pool, 4)
                for c in range(2):
                    m = headmask[:, c, :].rearrange("p (h v) -> p h v", v=HD)
                    last = pool.affine_select(out=m, in_=m, compare_op=ALU.is_ge, fill=0.0,
                                              base=HD - 1 - c * P, pattern=[[HD, HEADS], [0, HD]], channel_multiplier=-1)
                last.then_inc(setup_pool, 1)
                pool.wait_ge(deg_ready, 1)
                pool.tensor_tensor(dpow[:, :], deg[:, :], minus_half[:, 0:LO], ALU.pow).then_inc(pow_ready, 1)

            @block.vector
            def _(dve):
                v = nc.vector
                dve.wait_ge(loaded, 16 * N_LOADS)
                dve.wait_ge(setup_pool, 5)
                ch = Chain(dve, setup_dve, 8, 0)
                ch.link(v.tensor_copy(dstf[:, :], dst_i[:, :]))
                ch.now()
                ch.link(v.tensor_scalar(hi_i[:, :], dstf[:, :], 1.0 / LO, -0.5, ALU.mult, ALU.add))
                ch.now()
                ch.link(v.tensor_copy(hi[:, :], hi_i[:, :]))
                ch.now()
                ch.link(v.scalar_tensor_tensor(lo[:, :], hi[:, :], -float(LO), dstf[:, :], ALU.mult, ALU.add))
                ch.now()
                v.tensor_scalar(fix[:, :], lo[:, :], float(LO) - 0.5, None, ALU.is_gt)
                ch.link(v.tensor_scalar(hi_i[:, :], lo[:, :], -0.5, None, ALU.is_lt))
                ch.now()
                ch.link(v.tensor_tensor(fix[:, :], fix[:, :], hi_i[:, :], ALU.subtract))
                ch.now()
                ch.link(v.tensor_tensor(hi[:, :], hi[:, :], fix[:, :], ALU.add))
                ch.link(v.scalar_tensor_tensor(lo[:, :], fix[:, :], -float(LO), lo[:, :], ALU.mult, ALU.add))
                ch.now()
                ch.end()

                def hot(i, u):
                    c = i * UN + u
                    after(dve, hot_used, c - UN + 1)
                    col = slice(c, c + 1) if isinstance(c, int) else bass.ds(c, 1)
                    v.tensor_scalar(oneh[u][:, :], iota_hi[:, :], hi[:, col], None, ALU.is_equal)
                    v.tensor_scalar(onel[u][:, :], iota_lo[:, :], lo[:, col], ew_all[:, col],
                                    ALU.is_equal, ALU.mult).then_inc(hot_ready, 1)

                for u in range(UN):
                    hot(0, u)
                with dve.Fori(1, EC // UN) as i:
                    for u in range(UN):
                        hot(i, u)
                dve.wait_ge(deg_sum, 1)
                ch = Chain(dve, deg_steps, 1, 0)
                ch.link(v.tensor_scalar(deg[:, :], pB[:, 0:LO], 1.0, None, ALU.add))
                ch.now()
                ch.end()
                v.tensor_scalar(dpos[:, :], deg[:, :], 0.0, None, ALU.is_gt)
                v.tensor_scalar(deg[:, :], deg[:, :], DEG_FLOOR, None, ALU.max).then_inc(deg_ready, 1)
                dve.wait_ge(pow_ready, 1)
                v.tensor_tensor(dinv[:, :], dpow[:, :], dpos[:, :], ALU.mult).then_inc(dinv_ready, 1)
                v.tensor_tensor(wB[:, :, :], w1[:, :, :], w2[:, :, :], ALU.add)
                for c in range(2):
                    v.tensor_scalar(wg1g[:, c, :], wg1[:, c, :], lngc[:, c:c + 1], None, ALU.mult)
                    v.tensor_copy(b1b[:, c, :], b1c[:, c:c + 1].broadcast_to([P, P]))
                    v.tensor_copy(lnbb[:, c, :], lnbc[:, c:c + 1].broadcast_to([P, P]))
                v.tensor_scalar(b1_row[:, :], b1_row[:, :], MIX * KEEP, None, ALU.mult)
                ch = Chain(dve, row_steps, 2, 0)
                v.tensor_scalar(bg2c[:, :], bg2c[:, :], 0.5, None, ALU.mult)
                ch.link(v.tensor_scalar(wproj[:, :, :], wproj[:, :, :], 0.5, None, ALU.mult))
                ch.now()
                ch.link(v.scalar_tensor_tensor(c_row[:, :], b2_row[:, :], MIX, b1_row[:, :], ALU.mult, ALU.add))
                ch.now()
                v.tensor_scalar(wB[:, :, :], wB[:, :, :], MIX * KEEP, None, ALU.mult)
                v.tensor_tensor(c_row[:, :], c_row[:, :], bproj_row[:, :], ALU.add).then_inc(rows_ready, 1)
                ch.end()
                dve.wait_ge(setup_pe, 1)
                v.tensor_copy(w1T[:, :, :], pT[:, 0, :].rearrange("p (c n) -> p c n", c=2))
                v.tensor_copy(wqT[:, :, :], pT[:, 1, :].rearrange("p (c n) -> p c n", c=2)).then_inc(setup_act, 1)
                dve.wait_ge(abs_ready, 1)
                v.tensor_scalar(wabsT[:, :, :], wabsT[:, :, :], FFN_EPS, None, ALU.add)
                dve.wait_ge(setup_pe, 2)
                v.tensor_scalar(s_row[:, :], pC[0][:, 0:D], MIX * MIX, None, ALU.mult)
                v.tensor_tensor(h_row[:, :], pC[1][:, 0:GATE], bg1_row[:, :], ALU.add)
                v.tensor_scalar(wA[:, :, :], pG[:, :, :], MIX * MIX, None, ALU.mult).then_inc(setup_act, 1)
                dve.wait_ge(setup_act, 2)
                pairs = ((wA, wA_s), (wB, wB_s), (wproj, wproj_s), (wabsT, wabsT_s), (wg1g, wg1g_s))
                for w, parts in pairs:
                    last = v.tensor_copy(parts[0][:, :, :], w[:, :, :])
                last.then_inc(split_r, 1)
                dve.wait_ge(split_r, 1)
                for w, parts in pairs:
                    v.tensor_tensor(parts[1][:, :, :], w[:, :, :], parts[0][:, :, :].bitcast(f32), ALU.subtract)
                ch = Chain(dve, c_steps, 3, 0)
                v.tensor_scalar(ones[:, :], zeros[0:2, 0:P], 1.0, None, ALU.add)
                ch.link(v.tensor_copy(c_hi[:, :], c_row[0:2, :]))
                ch.now()
                ch.link(v.tensor_tensor(c_lo[:, :], c_row[0:2, :], c_hi[:, :].bitcast(f32), ALU.subtract))
                ch.now()
                ch.link(v.tensor_scalar(c_lo[:, :], c_lo[:, :], ident[0:2, 1:2], None, ALU.mult))
                ch.now()
                ch.end()
                for r in range(2):
                    v.scalar_tensor_tensor(c_parts[:, r, :], c_hi[:, :].bitcast(f32), ident[0:2, 0:1], c_lo[:, :], ALU.mult, ALU.add)

            @block.tensor
            def _(pe):
                t = nc.tensor
                pe.wait_ge(setup_pool, 5)
                t.matmul(pB[:, 0:LO], zeros[0:EP, 0:P], zeros[0:EP, 0:LO], start=True, stop=False)

                def add_chunk(i, u):
                    pe.wait_ge(hot_ready, i * UN + u + 1)
                    t.matmul(pB[:, 0:LO], oneh[u][:, :], onel[u][:, :], start=False, stop=False).then_inc(hot_used, 1)

                with pe.Fori(0, EC // UN) as i:
                    for u in range(UN):
                        add_chunk(i, u)
                t.matmul(pB[:, 0:LO], zeros[0:EP, 0:P], zeros[0:EP, 0:LO], start=False, stop=True).then_inc(deg_sum, 1)
                pe.wait_ge(loaded, 16 * N_LOADS)
                for area, w in ((pT[:, 0, :], w1), (pT[:, 1, :], wqkv), (pK[:, 0, :], wffn)):
                    for c in range(2):
                        for k in range(2):
                            last = t.transpose(area[:, k * D + c * P:k * D + (c + 1) * P], w[:, c, k * P:(k + 1) * P], ident[:, :])
                last.then_inc(setup_pe, 1)
                pe.wait_ge(setup_act, 1)
                pe.wait_ge(rows_ready, 1)
                for c in range(2):
                    for k in range(2):
                        t.matmul(pG[:, c, :], w1T[:, k, c * P:(c + 1) * P], w2[:, k, :], start=k == 0, stop=k == 1)
                for k in range(2):
                    t.matmul(pC[0][:, 0:D], b1b[:, k, :], w2[:, k, :], start=k == 0, stop=k == 1)
                for k in range(2):
                    last = t.matmul(pC[1][:, 0:GATE], lnbb[:, k, :], wg1[:, k, :], start=k == 0, stop=k == 1)
                last.then_inc(setup_pe, 1)

            @block.scalar
            def _(act):
                act.wait_ge(setup_pool, 2)
                with act.Fori(0, FILL) as i:
                    act.dma_start(agg1_d.rearrange("(k p r) w -> k p (r w)", k=FILL, p=P)[bass.ds(i, 1), :, :].rearrange("k p n -> (k p) n"),
                                  zeros[:, :]).then_inc(zero1, 16)
                act.wait_ge(setup_pe, 1)
                nc.scalar.activation(wabsT[:, :, :], pK[:, 0, :].rearrange("p (c n) -> p c n", c=2), ACT.Abs).then_inc(abs_ready, 1)
                nc.scalar.activation(wsgnT[:, :, :], pK[:, 0, :].rearrange("p (c n) -> p c n", c=2), ACT.Sign)
                act.wait_ge(zero1, 16 * FILL)

        E2 = GROUPS * 2
        with ExitStack() as s1:
            def sb1(name, shape, dt=f32):
                return s1.enter_context(nc.sbuf_tensor(name, shape, dt))

            def two1(name, shape, dt=f32):
                return [sb1(f"{name}0", shape, dt), sb1(f"{name}1", shape, dt)]

            eT = sb1("eT", [P, 2, TILE])
            en = two1("en", [P, ROWS, D])
            blkmax = sb1("blkmax", [P, 2])
            kmax, negmax, drop, alpha, rsum = (two1("kmax", [P, 2]), two1("negmax", [P, 2]), two1("drop", [P, 2]),
                                               two1("alpha", [P, 2]), two1("rsum", [P, 2]))
            esrc, edst = two1("esrc", [EP, CH], i32), two1("edst", [EP, CH], i32)
            drow = two1("drow", [EP, GROUP], i32)
            dview = [a[:, :].rearrange("p (l c) -> p c l", c=CH) for a in drow]
            eew, dsrc, edstf = two1("eew", [EP, CH]), two1("dsrc", [EP, CH]), sb1("edstf", [EP, CH])
            xg = two1("xg", [EP, CH, W1COLS])
            m1t = two1("m1t", [EP, CH, D])
            stat_rows = two1("stat_rows", [P, ROWS + CH, 6])
            mvs = two1("mvs", [P, ROWS + CH, 2])
            roots, vars_eps, neg_mean, shift = (two1("roots", [P, ROWS + CH]), sb1("vars_eps", [P, ROWS + CH]),
                                                sb1("neg_mean", [P, ROWS + CH]), two1("shift", [P, ROWS + CH]))
            coef, ca, cb = sb1("coef", [EP, CH]), sb1("ca", [EP, CH]), sb1("cb", [EP, CH])
            msg = two1("msg", [EP, CH, W1COLS])
            same = two1("same", [EP, CH, GROUP])
            cnt, toodd, rowf = sb1("cnt", [EP, CH]), sb1("toodd", [EP, CH]), sb1("rowf", [EP, CH])
            rowi = two1("rowi", [EP, CH], i32)
            comb = two1("comb", [EP, CH, W1COLS])
            comb2 = [a[:, :, :].rearrange("p c w -> p (c w)")[:, 0:CH * D].rearrange("p (c w) -> p c w", c=CH) for a in comb]

            x_in, e_in, g_in, m_in, m_out = sems("x_in"), sems("e_in"), sems("g_in"), sems("m_in"), sems("m_out")
            zero2, scattered = sem("zero2"), sem("scattered")
            (stat_r, root_r, xn_r, xT_p, xT_r, k_p, max_r, e_r, en_p, en_r, g_p, g_r) = (sem(n) for n in (
                "stat_r", "root_r", "xn_r", "xT_p", "xT_r", "k_p", "max_r", "e_r", "en_p", "en_r", "g_p", "g_r"))
            msg_r, same_r, comb_p, comb_r = sem("msg_r"), sem("same_r"), sem("comb_p"), sem("comb_r")
            n_steps, e_steps, e2_steps, r_steps, s_steps, init = (
                sem("n_steps"), sem("e_steps"), sem("e2_steps"), sem("r_steps"), sem("s_steps"), sem("init"))
            block = s1.enter_context(nc.Block())

            def nodes_of(array, t, rows, parts, width):
                first = t * TILE
                view = array[first:first + parts * rows, :] if isinstance(first, int) else array[bass.ds(first, parts * rows), :]
                return view.rearrange("(p r) w -> p (r w)", r=rows)

            def group_of(vector, g):
                first = g * GROUP
                view = vector[first:first + GROUP] if isinstance(first, int) else vector[bass.ds(first, GROUP)]
                return view.rearrange("(p c) -> p c", c=CH)

            def group_rows(array, g):
                first = g * GROUP
                view = array[first:first + GROUP, :] if isinstance(first, int) else array[bass.ds(first, GROUP), :]
                return view.rearrange("(p c) w -> p (c w)", c=CH)

            def shape(t):
                return (TAIL_P, TAIL_ROWS) if isinstance(t, int) and t == FULL else (P, ROWS)

            HALF = GROUPS // 2

            def walk(engine, step):
                for b in range(2):
                    step(0, b, 1)
                with engine.Fori(1, HALF - 1) as i:
                    for b in range(2):
                        step(i, b, 1)
                for b in range(2):
                    step(HALF - 1, b, 1)
                with engine.Fori(HALF, FULL // 2) as i:
                    for b in range(2):
                        step(i, b, 2)
                for i in range(FULL // 2, GROUPS):
                    for b in range(2):
                        step(i, b, 2)

            def later(i, b, n):
                return i + (b + n) // 2, (b + n) % 2

            def has_tile(t):
                return not isinstance(t, int) or 0 <= t < TILES

            def has_group(t):
                return not isinstance(t, int) or 0 <= t < E2

            def layer_of(t, layer):
                return (1 if t < GROUPS else 2) if isinstance(t, int) else layer

            @block.sync
            def _(sp):
                def load(i, b, layer):
                    t = 2 * i + b
                    if has_tile(t):
                        parts, rows = shape(t)
                        after(sp, xn_r, t - 1)
                        sp.dma_start(xt[b][0:parts, 0:rows, :].rearrange("p r w -> p (r w)"), nodes_of(x, t, rows, parts, D)).then_inc(x_in[b], 16)
                    g = t if layer == 1 else t - GROUPS
                    after(sp, msg_r, t - 1)
                    after(sp, same_r, t - 1)
                    for tile, vec in ((esrc, src), (edst, dst), (eew, edge_weight)):
                        sp.dma_start(tile[b][:, :], group_of(vec, g)).then_inc(e_in[b], 16)
                    first = g * GROUP
                    piece = dst[first:first + GROUP] if isinstance(first, int) else dst[bass.ds(first, GROUP)]
                    sp.dma_start(drow[b][:, :], piece.rearrange("(a n) -> a n", a=1).partition_broadcast(EP)).then_inc(e_in[b], 16)
                    if layer == 1:
                        if b == 0:
                            row = i * P * FILL_ROWS
                            view = agg2_d[row:row + P * FILL_ROWS, :] if isinstance(row, int) else agg2_d[bass.ds(row, P * FILL_ROWS), :]
                            sp.dma_start(view.rearrange("(p r) w -> p (r w)", p=P), zeros[:, 0:FILL_ROWS * D]).then_inc(zero2, 16)
                        keep(t - 1, 1 - b)
                    else:
                        sp.dma_start(dsrc[b][:, :], group_of(dsrc_d, g)).then_inc(m_in[b], 16)
                        sp.dma_start(m1t[b][:, :, :].rearrange("p c w -> p (c w)"), group_rows(msg_d, g)).then_inc(m_in[b], 16)

                def keep(t, b):
                    if isinstance(t, int) and t < 0:
                        return
                    sp.wait_ge(msg_r, t + 1)
                    sp.dma_start(group_rows(msg_d, t).rearrange("p (c w) -> p c w", c=CH), msg[b][:, :, 0:D]).then_inc(m_out[b], 16)
                    sp.dma_start(group_of(dsrc_d, t), dsrc[b][:, :]).then_inc(m_out[b], 16)

                for b in range(2):
                    load(0, b, 1)
                with sp.Fori(1, HALF) as i:
                    for b in range(2):
                        load(i, b, 1)
                keep(GROUPS - 1, 1)
                for b in range(2):
                    sp.wait_ge(m_out[b], 32 * HALF)
                with sp.Fori(HALF, FULL // 2) as i:
                    for b in range(2):
                        load(i, b, 2)
                for i in range(FULL // 2, GROUPS):
                    for b in range(2):
                        load(i, b, 2)
                sp.wait_ge(zero2, 16 * FILL)

            @block.gpsimd
            def _(pool):
                def gathers(i, b, layer):
                    t = 2 * i + b
                    if not has_group(t):
                        return
                    after(pool, msg_r, t - 1)
                    pool.wait_ge(e_in[b], 64 * (i + 1))
                    if layer == 1:
                        after(pool, m_out[b], 32 * i)
                    before_fixed(pool, carried_pool)
                    if layer == 1:
                        for c in range(CH):
                            where = bass.IndirectOffsetOnAxis(esrc[b][:, c:c + 1], 0)
                            pool.indirect_dma_start(xg[b][:, c, 0:D], None, x[:, :], where).then_inc(g_in[b], 16)
                            pool.indirect_dma_start(dsrc[b][:, c:c + 1], None, dinv_d[:, :], where).then_inc(g_in[b], 16)
                    else:
                        for c in range(CH):
                            where = bass.IndirectOffsetOnAxis(esrc[b][:, c:c + 1], 0)
                            pool.indirect_dma_start(xg[b][:, c, :], None, agg1_d[:, :], where).then_inc(g_in[b], 16)

                def inverse_roots(t, b):
                    if not has_tile(t):
                        return
                    pool.wait_ge(stat_r, t + 1)
                    after(pool, xn_r, t - 1)
                    if not isinstance(t, int) or t < GROUPS + 2:
                        after(pool, msg_r, t - 1)
                    before_fixed(pool, carried_pool)
                    ch = Chain(pool, r_steps, 2, t, carried_pool)
                    ch.link(pool.tensor_scalar(vars_eps[:, :], mvs[b][:, :, 1], LN_EPS, None, ALU.add))
                    pool.tensor_scalar(neg_mean[:, :], mvs[b][:, :, 0], -1.0, None, ALU.mult)
                    ch.now()
                    ch.link(pool.tensor_tensor(roots[b][:, :], vars_eps[:, :], minus_half[:, 0:ROWS + CH], ALU.pow))
                    ch.now()
                    pool.tensor_tensor(shift[b][:, :], neg_mean[:, :], roots[b][:, :], ALU.mult).then_inc(root_r, 1)
                    ch.end()

                def scatters(t, b, layer):
                    if not isinstance(t, int) or t > 0:
                        pool.wait_ge(scattered, 64 * t)
                    pool.wait_ge(comb_r, CH * (t + 1))
                    before_fixed(pool, carried_pool)
                    for c in range(CH):
                        where = bass.IndirectOffsetOnAxis(rowi[b][:, c:c + 1], 0)
                        if layer == 1:
                            pool.indirect_dma_start(agg1_d[:, :], where, comb[b][:, c, :], None,
                                                    compute_op=ALU.add).then_inc(scattered, 16)
                        else:
                            pool.indirect_dma_start(agg2_d[:, :], where, comb2[b][:, c, :], None,
                                                    compute_op=ALU.add).then_inc(scattered, 16)

                def step(i, b, layer):
                    t = 2 * i + b
                    inverse_roots(t + 1, 1 - b)
                    if not (isinstance(t, int) and t < GROUPS <= t + 2):
                        gathers(i + 1, b, layer)
                    scatters(t, b, layer)
                    if isinstance(t, int) and t == GROUPS - 1:
                        pool.wait_ge(scattered, 64 * GROUPS)
                        pool.wait_ge(zero2, 16 * FILL)
                        gathers(HALF, 0, 2)
                        gathers(HALF, 1, 2)

                for b in range(2):
                    pool.memset(comb[b][:, :, :], 0.0)
                    pool.memset(msg[b][:, :, :], 0.0)
                pool.memset(gsum[:, :, :], 0.0)
                pool.memset(esum[:, :], 0.0)
                for b in range(2):
                    pool.memset(mvs[b][:, :, :], 0.0)
                pool.memset(kmax[1][:, :], -1e30).then_inc(init, 1)
                gathers(0, 0, 1)
                inverse_roots(0, 0)
                gathers(0, 1, 1)
                walk(pool, step)
                pool.wait_ge(scattered, 64 * E2)

            @block.vector
            def _(dve):
                v = nc.vector

                def statistics(i, b, layer):
                    t = 2 * i + b
                    if not has_tile(t):
                        return
                    parts, rows = shape(t)
                    dve.wait_ge(x_in[b], 16 * (i + 1))
                    after(dve, root_r, t - 1)
                    ch = Chain(dve, s_steps, 1, t, carried_dve)
                    for r in range(rows):
                        last = v.bn_stats(stat_rows[b][0:parts, r, :], xt[b][0:parts, r, :])
                    if layer == 1:
                        dve.wait_ge(g_in[b], 16 * 2 * CH * (i + 1))
                        for c in range(CH):
                            last = v.bn_stats(stat_rows[b][0:EP, ROWS + c, :], xg[b][:, c, 0:D])
                    ch.link(last)
                    ch.now()
                    ch.end()
                    for r in range(rows):
                        last = v.bn_aggr(mvs[b][0:parts, r, :], stat_rows[b][0:parts, r, :])
                    if layer == 1:
                        for c in range(ROWS, ROWS + CH):
                            last = v.bn_aggr(mvs[b][0:EP, c, :], stat_rows[b][0:EP, c, :])
                    last.then_inc(stat_r, 1)

                def running_max(t, b):
                    if not has_tile(t):
                        return
                    parts, rows = shape(t)
                    dve.wait_ge(k_p, t + 1)
                    ch = Chain(dve, n_steps, 2, t)
                    ch.link(v.reduce_max(blkmax[:, :], pK[:, :, 0:parts * rows], AX.X))
                    ch.now()
                    ch.link(v.tensor_tensor(kmax[b][:, :], kmax[1 - b][:, :], blkmax[:, :], ALU.max))
                    ch.now()
                    ch.end()
                    v.tensor_scalar(negmax[b][:, :], kmax[b][:, :], -1.0, None, ALU.mult)
                    v.tensor_tensor(drop[b][:, :], kmax[1 - b][:, :], kmax[b][:, :], ALU.subtract).then_inc(max_r, 1)

                def add_sums(t, b):
                    if not has_tile(t):
                        return
                    dve.wait_ge(g_p, t + 1)
                    for c in range(2):
                        v.scalar_tensor_tensor(gsum[:, c, :], gsum[:, c, :], alpha[b][:, c:c + 1], pG[:, c, :], ALU.mult, ALU.add)
                        last = v.scalar_tensor_tensor(esum[:, c:c + 1], esum[:, c:c + 1], alpha[b][:, c:c + 1], rsum[b][:, c:c + 1], ALU.mult, ALU.add)
                    last.then_inc(g_r, 1)

                def messages(i, b, layer):
                    t = 2 * i + b
                    if not has_group(t):
                        return
                    ch = Chain(dve, e_steps, 5, t) if layer == 1 else Chain(dve, e2_steps, 6, t - GROUPS)
                    dve.wait_ge(e_in[b], 64 * (i + 1))
                    ch.link(v.tensor_copy(edstf[:, :], edst[b][:, :]))
                    after(dve, comb_p, CH * (t - 1))
                    ch.now()
                    for c in range(CH):
                        width = CH - c
                        v.scalar_tensor_tensor(same[b][:, c, c * EP:GROUP].rearrange("p (c l) -> p c l", c=width),
                                               dview[b][:, c:CH, :], edstf[:, c:c + 1],
                                               tri[:, 0:GROUP - c * EP].rearrange("p (c l) -> p c l", c=width),
                                               ALU.is_equal, ALU.mult, accum_out=cnt[:, c:c + 1])
                    ch.link(v.tensor_tensor(rowf[:, :], spare[:, :], edstf[:, :], ALU.subtract))
                    ch.now()
                    ch.link(v.scalar_tensor_tensor(toodd[:, :], cnt[:, :], 1.5, rowf[:, :], ALU.is_gt, ALU.mult))
                    if layer == 1:
                        dve.wait_ge(g_in[b], 16 * 2 * CH * (i + 1))
                        ch.link(v.tensor_tensor(coef[:, :], eew[b][:, :], dsrc[b][:, :], ALU.mult))
                    else:
                        dve.wait_ge(g_in[b], 16 * 2 * CH * HALF + 16 * CH * (i + 1 - HALF))
                        dve.wait_ge(m_in[b], 32 * (i + 1 - HALF))
                        ch.link(v.tensor_tensor(ca[:, :], dsrc[b][:, :], dsrc[b][:, :], ALU.mult))
                    after(dve, scattered, 64 * (t - 1))
                    ch.now()
                    v.tensor_tensor(rowi[b][:, :], toodd[:, :], edstf[:, :], ALU.add).then_inc(same_r, 1)
                    if layer == 1:
                        dve.wait_ge(root_r, t + 1)
                        v.tensor_tensor(cb[:, :], shift[b][0:EP, ROWS:ROWS + CH], coef[:, :], ALU.mult)
                        ch.link(v.tensor_tensor(ca[:, :], roots[b][0:EP, ROWS:ROWS + CH], coef[:, :], ALU.mult))
                        after(dve, m_out[b], 32 * i)
                        ch.now()
                        for c in range(CH):
                            v.tensor_scalar(msg[b][:, c, 0:D], xg[b][:, c, 0:D], ca[:, c:c + 1], cb[:, c:c + 1], ALU.mult, ALU.add)
                        last = v.tensor_copy(msg[b][:, :, D], coef[:, :])
                    else:
                        dve.wait_ge(m_out[b], 32 * HALF)
                        ch.link(v.tensor_tensor(cb[:, :], ca[:, :], eew[b][:, :], ALU.mult))
                        for c in range(CH):
                            last = v.tensor_scalar(m1t[b][:, c, :], m1t[b][:, c, :], ca[:, c:c + 1], None, ALU.mult)
                        ch.link(last)
                        ch.now()
                        for c in range(CH):
                            last = v.scalar_tensor_tensor(msg[b][:, c, 0:D], xg[b][:, c, 0:D], cb[:, c:c + 1], m1t[b][:, c, :], ALU.mult, ALU.add)
                    last.then_inc(msg_r, 1)
                    ch.end()

                def step(i, b, layer):
                    t = 2 * i + b
                    nxt = later(i, b, 1)
                    of_next = layer_of(t + 1, layer)
                    statistics(*nxt, of_next)
                    running_max(t, b)
                    add_sums(t - 1, 1 - b)
                    messages(*nxt, of_next)

                dve.wait_ge(init, 1)
                statistics(0, 0, 1)
                messages(0, 0, 1)
                walk(dve, step)

            @block.tensor
            def _(pe):
                te = nc.tensor

                def exp_sums(t, b):
                    if not has_tile(t):
                        return
                    parts, rows = shape(t)
                    pe.wait_ge(en_r, t + 1)
                    after(pe, g_r, t)
                    for c in range(2):
                        for r in range(rows):
                            last = te.matmul(pG[:, c, :], en[b][0:parts, r, c * P:(c + 1) * P], xn[b][0:parts, r, :],
                                             start=r == 0, stop=r == rows - 1)
                    last.then_inc(g_p, 1)

                def step(i, b, layer):
                    t = 2 * i + b
                    tile = has_tile(t)
                    if tile:
                        parts, rows = shape(t)
                        n = parts * rows

                    def edge_sums(c):
                        width = D + 1 if layer == 1 else D
                        if not (isinstance(t, int) and t == 0 and c < 2):
                            pe.wait_ge(comb_r, CH * t + c - 1)
                        for k in range(c + 1):
                            last = te.matmul(pC[c % 2][0:EP, 0:width], same[b][:, k, c * EP:(c + 1) * EP], msg[b][:, k, 0:width],
                                             start=k == 0, stop=k == c)
                        last.then_inc(comb_p, 1)

                    if tile:
                        pe.wait_ge(xn_r, t + 1)
                        after(pe, en_r, t)
                        for c in range(2):
                            for r in range(rows):
                                last = te.transpose(pT[:, c, r * parts:(r + 1) * parts], xn[b][0:parts, r, c * P:(c + 1) * P],
                                                    ident[0:parts, 0:parts])
                        last.then_inc(xT_p, 1)
                    pe.wait_ge(same_r, t + 1)
                    pe.wait_ge(msg_r, t + 1)
                    edge_sums(0)
                    edge_sums(1)
                    if tile:
                        pe.wait_ge(xT_r, t + 1)
                        after(pe, e_r, t)
                        for c in range(2):
                            for k in range(2):
                                last = te.matmul(pK[:, c, 0:n], wqkv[:, k, D + c * P:D + (c + 1) * P], xnT[:, k, 0:n],
                                                 start=k == 0, stop=k == 1)
                        last.then_inc(k_p, 1)
                    exp_sums(t - 1, 1 - b)
                    edge_sums(2)
                    if tile:
                        pe.wait_ge(e_r, t + 1)
                        for r in range(rows):
                            for c in range(2):
                                last = te.transpose(pT[0:parts, r // 2, (r % 2) * D + c * P:(r % 2) * D + (c + 1) * P],
                                                    eT[:, c, r * parts:(r + 1) * parts], ident[:, :])
                        last.then_inc(en_p, 1)
                    edge_sums(3)

                walk(pe, step)

            @block.scalar
            def _(act):
                a = nc.scalar

                def normalize(t, b):
                    if not has_tile(t):
                        return
                    parts, rows = shape(t)
                    act.wait_ge(root_r, t + 1)
                    after(act, g_p, t - 1)
                    for r in range(rows):
                        last = a.activation(xn[b][0:parts, r, :], xt[b][0:parts, r, :], ACT.Identity,
                                            bias=shift[b][0:parts, r:r + 1], scale=roots[b][0:parts, r:r + 1])
                    last.then_inc(xn_r, 1)

                def step(i, b, layer):
                    t = 2 * i + b

                    def take_sums(c):
                        act.wait_ge(comb_p, CH * t + c + 1)
                        if layer == 1:
                            last = a.activation(comb[b][:, c, 0:D + 1], pC[c % 2][0:EP, 0:D + 1], ACT.Copy)
                        else:
                            last = a.activation(comb2[b][:, c, :], pC[c % 2][0:EP, 0:D], ACT.Copy)
                        last.then_inc(comb_r, 1)

                    tile = has_tile(t)
                    if tile:
                        parts, rows = shape(t)
                        n = parts * rows
                        act.wait_ge(xT_p, t + 1)
                        after(act, k_p, t)
                        for c in range(2):
                            last = a.activation(xnT[:, c, 0:n], pT[:, c, 0:n], ACT.Copy)
                        last.then_inc(xT_r, 1)
                    after(act, scattered, 64 * (t - 1))
                    take_sums(0)
                    take_sums(1)
                    if tile:
                        act.wait_ge(max_r, t + 1)
                        after(act, en_p, t)
                        after(act, g_r, t - 1)
                        for c in range(2):
                            a.activation(eT[:, c, 0:n], pK[:, c, 0:n], ACT.Exp, bias=negmax[b][:, c:c + 1], accum_out=rsum[b][:, c:c + 1])
                        a.activation(alpha[b][:, :], drop[b][:, :], ACT.Exp).then_inc(e_r, 1)
                    normalize(t + 1, 1 - b)
                    take_sums(2)
                    if tile:
                        act.wait_ge(en_p, t + 1)
                        after(act, g_p, t - 1)
                        for r in range(0, rows, 2):
                            w = min(2, rows - r)
                            last = a.activation(en[b][0:parts, r:r + w, :], pT[0:parts, r // 2, 0:w * D].rearrange("p (r n) -> p r n", r=w), ACT.Copy)
                        last.then_inc(en_r, 1)
                    take_sums(3)

                act.wait_ge(init, 1)
                normalize(0, 0)
                walk(act, step)

        with ExitStack() as s2:
            rinv = s2.enter_context(nc.sbuf_tensor("rinv", [P, 2], f32))
            ctxn = s2.enter_context(nc.sbuf_tensor("ctxn", [P, 2, D], f32))
            ctxT = s2.enter_context(nc.sbuf_tensor("ctxT", [P, 2, D], f32))
            ctxb = s2.enter_context(nc.sbuf_tensor("ctxb", [P, 2, D], f32))
            c_dve, c_pe = sem("c_dve"), sem("c_pe")
            block = s2.enter_context(nc.Block())

            @block.vector
            def _(dve):
                v = nc.vector
                v.reciprocal(rinv[:, :], esum[:, :]).then_inc(c_dve, 1)
                dve.wait_ge(c_dve, 1)
                for c in range(2):
                    last = v.tensor_scalar(ctxn[:, c, :], gsum[:, c, :], rinv[:, c:c + 1], None, ALU.mult)
                last.then_inc(c_dve, 1)
                dve.wait_ge(c_pe, 1)
                v.tensor_copy(ctxT[:, :, :], pT[:, 0, :].rearrange("p (c n) -> p c n", c=2)).then_inc(c_dve, 1)
                dve.wait_ge(c_pe, 2)
                v.tensor_tensor(ctxb[:, :, :], pG[:, :, :], headmask[:, :, :], ALU.mult).then_inc(c_dve, 1)
                dve.wait_ge(c_pe, 3)
                v.tensor_copy(wM[:, :, :], pK[:, 0, :].rearrange("p (c n) -> p c n", c=2)).then_inc(c_dve, 1)
                dve.wait_ge(c_dve, 5)
                v.tensor_copy(wM_s[0][:, :, :], wM[:, :, :]).then_inc(c_dve, 1)
                dve.wait_ge(c_dve, 6)
                v.tensor_tensor(wM_s[1][:, :, :], wM[:, :, :], wM_s[0][:, :, :].bitcast(f32), ALU.subtract)

            @block.tensor
            def _(pe):
                t = nc.tensor
                pe.wait_ge(c_dve, 2)
                for c in range(2):
                    for k in range(2):
                        last = t.transpose(pT[:, 0, k * D + c * P:k * D + (c + 1) * P], ctxn[:, c, k * P:(k + 1) * P], ident[:, :])
                last.then_inc(c_pe, 1)
                pe.wait_ge(c_dve, 3)
                for c in range(2):
                    for k in range(2):
                        last = t.matmul(pG[:, c, :], ctxT[:, k, c * P:(c + 1) * P], wqkv[:, k, 2 * D:3 * D], start=k == 0, stop=k == 1)
                last.then_inc(c_pe, 1)
                pe.wait_ge(c_dve, 4)
                for c in range(2):
                    for k in range(2):
                        last = t.matmul(pK[:, 0, c * D:(c + 1) * D], wqT[:, k, c * P:(c + 1) * P], ctxb[:, k, :], start=k == 0, stop=k == 1)
                last.then_inc(c_pe, 1)

        early.close()
        narrow.close()
        pA = ps("pA", [P, 2, TILE])
        pZ = ps("pZ", [P, 2, TILE])
        pO = pK

        a1, a2, dv = two("a1", [P, ROWS, W1COLS]), two("a2", [P, ROWS, D]), two("dv", [P, ROWS])
        dd, deg1, mix2, mixn = two("dd", [P, ROWS]), two("deg1", [P, ROWS]), sb("mix2", [P, ROWS]), sb("mixn", [P, ROWS])
        var2, rsq, r2 = sb("var2", [P, ROWS]), sb("rsq", [P, ROWS]), two("r2", [P, ROWS])
        u1, u2 = sb("u1", [P, ROWS, D]), sb("u2", [P, ROWS, D])
        xnT_s, u1T_s, u2T_s, yT_s, absT_s = (parts_of(n, [P, 2, TILE]) for n in ("xnTs", "u1T", "u2T", "yTs", "absT"))
        absx, gT, yT = sb("absx", [P, 2, TILE]), sb("gT", [P, 2, TILE]), sb("yT", [P, 2, TILE])
        hpre, hid = sb("hpre", [P, ROWS, GATE]), sb("hid", [P, ROWS, GATE])
        hT = sb("hT", [GATE, TILE])
        xb, x2 = two("xb", [P, ROWS, D]), two("x2", [P, ROWS, D])
        stat2, mv2 = sb("stat2", [P, ROWS, 6]), sb("mv2", [P, ROWS, 2])
        ve2, rstd2, nm2, nmr2 = sb("ve2", [P, ROWS]), sb("rstd2", [P, ROWS]), sb("nm2", [P, ROWS]), sb("nmr2", [P, ROWS])
        xf = sb("xf", [P, ROWS, D])
        sgnT, osgn = sb("sgnT", [P, 2, TILE], bf16), sb("osgn", [P, ROWS, D], bf16)
        prod, x2b, res = sb("prod", [P, ROWS, D]), sb("x2b", [P, ROWS, D]), two("res", [P, ROWS, D])

        t_in, a_in, t_out = sems("t_in"), sems("a_in"), sems("t_out")
        (tstat_r, troot_r, scale_r, deg_r, a1_r, a2_r, base_r, tnorm_r, u1_r, u2_r) = (sem(n) for n in (
            "tstat_r", "troot_r", "scale_r", "deg_r", "a1_r", "a2_r", "base_r", "tnorm_r", "u1_r", "u2_r"))
        xnT_p, xnT_hi, xnT_lo, u1T_p, u1T_hi, u1T_lo, u2T_p, u2T_hi, u2T_lo = (sem(n) for n in (
            "xnT_p", "xnT_hi", "xnT_lo", "u1T_p", "u1T_hi", "u1T_lo", "u2T_p", "u2T_hi", "u2T_lo"))
        (h_p, hpre_r, hid_r, hT_p, hT_r, o_p, gate_p, gate_r, y_r, y_hi, y_lo, z_p, half_r, x2_r) = (sem(n) for n in (
            "h_p", "hpre_r", "hid_r", "hT_p", "hT_r", "o_p", "gate_p", "gate_r", "y_r", "y_hi", "y_lo", "z_p", "half_r", "x2_r"))
        (fstat_r, froot_r, xf_r, xf_p, absx_r, abs_hi, abs_lo, sgnT_r, sgn_p, ffn_p, osgn_r, prod_r, bias_r, res_r) = (sem(n) for n in (
            "fstat_r", "froot_r", "xf_r", "xf_p", "absx_r", "abs_hi", "abs_lo", "sgnT_r", "sgn_p", "ffn_p", "osgn_r", "prod_r",
            "bias_r", "res_r"))
        ts_steps, tx_steps, tr_steps, td_steps, tb_steps, fr_steps, fs_steps = (sem(n) for n in (
            "ts_steps", "tx_steps", "tr_steps", "td_steps", "tb_steps", "fr_steps", "fs_steps"))
        block = ctx.enter_context(nc.Block())

        def tile_rows(array, t):
            if isinstance(t, int):
                first = min(t * TILE, NODES - TILE)
                view = array[first:first + TILE, :]
            else:
                view = array[bass.ds(t * TILE, TILE), :]
            return view.rearrange("(p r) w -> p (r w)", r=ROWS)

        def flat(tile):
            return tile[:, :, :].rearrange("p r w -> p (r w)")

        def halves(bank_pair):
            return bank_pair[:, :, :].rearrange("p c (r n) -> p (c r) n", n=D)

        def walk_tiles(engine, step, first=1):
            for i in range(first):
                step(i, 0)
                step(i, 1)
            with engine.Fori(first, FULL // 2) as i:
                for b in range(2):
                    step(i, b)
            step(FULL // 2, 0)
            step(FULL // 2, 1)
            step(FULL // 2 + 1, 0)

        def later(i, b, n):
            return i + (b + n) // 2, (b + n) % 2

        def runs(t):
            return not isinstance(t, int) or 0 <= t < TILES

        @block.sync
        def _(sp):
            def load(i, b):
                t = 2 * i + b
                if not runs(t):
                    return
                after(sp, base_r, t - 1)
                after(sp, tnorm_r, t - 1)
                after(sp, u2_r, t - 1)
                sp.dma_start(flat(xt[b]), tile_rows(x, t)).then_inc(t_in[b], 16)
                sp.dma_start(dv[b][:, :], tile_rows(dinv_d, t)).then_inc(a_in[b], 16)
                sp.dma_start(flat(a1[b]), tile_rows(agg1_d, t)).then_inc(a_in[b], 16)
                sp.dma_start(flat(a2[b]), tile_rows(agg2_d, t)).then_inc(a_in[b], 16)

            def store(i, b):
                t = 2 * i + b
                if isinstance(t, int) and t < 0:
                    return
                sp.wait_ge(res_r, t + 1)
                if isinstance(t, int) and t == TILES - 1:
                    sp.wait_ge(t_out[0], 16 * (FULL // 2 + 1))
                sp.dma_start(tile_rows(out, t), flat(res[b])).then_inc(t_out[b], 16)

            def step(i, b):
                load(i, b)
                store(*later(i, b, -3))

            walk_tiles(sp, step, first=2)
            store(FULL // 2, 0)
            store(FULL // 2, 1)
            for b in range(2):
                sp.wait_ge(t_out[b], 16 * (FULL // 2 + 1))

        @block.gpsimd
        def _(pool):
            def degrees(i, b):
                t = 2 * i + b
                if not runs(t):
                    return
                pool.wait_ge(a_in[b], 48 * (i + 1))
                after(pool, x2_r, t - 1)
                before_fixed(pool, carried_pool)
                ch = Chain(pool, td_steps, 2, t, carried_pool)
                ch.link(pool.tensor_tensor(dd[b][:, :], dv[b][:, :], dv[b][:, :], ALU.mult))
                ch.link(pool.tensor_tensor(deg1[b][:, :], dv[b][:, :], a1[b][:, :, D], ALU.mult))
                ch.now()
                ch.end()
                pool.tensor_tensor(deg1[b][:, :], deg1[b][:, :], dd[b][:, :], ALU.add).then_inc(deg_r, 1)

            def tile_roots(t, b):
                if not runs(t):
                    return
                pool.wait_ge(tstat_r, t + 1)
                after(pool, tnorm_r, t - 1)
                after(pool, hpre_r, t - 1)
                before_fixed(pool, carried_pool)
                ch = Chain(pool, tr_steps, 5, t, carried_pool)
                ch.link(pool.tensor_scalar(veps[b][:, :], mv[b][:, :, 1], LN_EPS, None, ALU.add))
                pool.tensor_scalar(nmean[b][:, :], mv[b][:, :, 0], -1.0, None, ALU.mult)
                ch.now()
                ch.link(pool.tensor_tensor(rstd[b][:, :], veps[b][:, :], minus_half[:, 0:ROWS], ALU.pow))
                ch.now()
                pool.tensor_tensor(nmr[b][:, :], nmean[b][:, :], rstd[b][:, :], ALU.mult).then_inc(troot_r, 1)
                ch.link(pool.tensor_tensor(rsq[:, :], rstd[b][:, :], rstd[b][:, :], ALU.mult))
                ch.now()
                ch.link(pool.tensor_tensor(var2[:, :], rsq[:, :], mv[b][:, :, 1], ALU.mult))
                ch.now()
                ch.link(pool.tensor_scalar(var2[:, :], var2[:, :], LN_EPS, None, ALU.add))
                ch.now()
                ch.end()
                pool.tensor_tensor(r2[b][:, :], var2[:, :], minus_half[:, 0:ROWS], ALU.pow).then_inc(scale_r, 1)

            def base(i, b):
                t = 2 * i + b
                if not runs(t):
                    return
                pool.wait_ge(t_in[b], 16 * (i + 1))
                pool.wait_ge(troot_r, t + 1)
                after(pool, x2_r, t - 1)
                before_fixed(pool, carried_pool)
                ch = Chain(pool, tb_steps, 1, t, carried_pool)
                pool.tensor_scalar(mixn[:, :], nmr[b][:, :], KEEP * KEEP, None, ALU.mult)
                ch.link(pool.tensor_scalar(mix2[:, :], rstd[b][:, :], KEEP * KEEP, 1.0, ALU.mult, ALU.add))
                ch.now()
                ch.end()
                for r in range(ROWS):
                    last = pool.tensor_scalar(xb[b][:, r, :], xt[b][:, r, :], mix2[:, r:r + 1], mixn[:, r:r + 1], ALU.mult, ALU.add)
                last.then_inc(base_r, 1)

            def ffn_roots(t, b):
                if not runs(t):
                    return
                pool.wait_ge(fstat_r, t + 1)
                after(pool, xf_r, t)
                if not isinstance(t, int) or t > 0:
                    pool.wait_ge(res_r, t)
                before_fixed(pool, carried_pool)
                ch = Chain(pool, fr_steps, 2, t, carried_pool)
                ch.link(pool.tensor_scalar(ve2[:, :], mv2[:, :, 1], LN_EPS, None, ALU.add))
                pool.tensor_scalar(nm2[:, :], mv2[:, :, 0], -1.0, None, ALU.mult)
                ch.now()
                ch.link(pool.tensor_tensor(rstd2[:, :], ve2[:, :], minus_half[:, 0:ROWS], ALU.pow))
                ch.now()
                ch.end()
                pool.tensor_tensor(nmr2[:, :], nm2[:, :], rstd2[:, :], ALU.mult).then_inc(froot_r, 1)
                for r in range(ROWS):
                    last = pool.tensor_tensor(x2b[:, r, :], x2[b][:, r, :], ffnb_row[:, :], ALU.add)
                last.then_inc(bias_r, 1)

            def result(i, b):
                t = 2 * i + b
                if not runs(t):
                    return
                pool.wait_ge(bias_r, t + 1)
                pool.wait_ge(prod_r, t + 1)
                after(pool, t_out[b], 16 * i)
                before_fixed(pool, carried_pool)
                pool.tensor_tensor(res[b][:, :, :], prod[:, :, :], x2b[:, :, :], ALU.add).then_inc(res_r, 1)

            def step(i, b):
                t = 2 * i + b
                degrees(*later(i, b, 1))
                ffn_roots(t - 1, 1 - b)
                base(*later(i, b, 1))
                tile_roots(t + 2, b)
                result(*later(i, b, -1))

            tile_roots(0, 0)
            degrees(0, 0)
            base(0, 0)
            tile_roots(1, 1)
            walk_tiles(pool, step)

        @block.vector
        def _(dve):
            v = nc.vector

            def statistics(i, b):
                t = 2 * i + b
                if not runs(t):
                    return
                dve.wait_ge(t_in[b], 16 * (i + 1))
                after(dve, scale_r, t - 1)
                ch = Chain(dve, ts_steps, 1, t, carried_dve)
                for r in range(ROWS):
                    last = v.bn_stats(stat[b][:, r, :], xt[b][:, r, :])
                ch.link(last)
                ch.now()
                ch.end()
                for r in range(ROWS):
                    last = v.bn_aggr(mv[b][:, r, :], stat[b][:, r, :])
                last.then_inc(tstat_r, 1)

            def steps_over_graph(t, b):
                if not runs(t):
                    return
                dve.wait_ge(tnorm_r, t + 1)
                dve.wait_ge(deg_r, t + 1)
                dve.wait_ge(a1_r, t + 1)
                after(dve, u1T_p, 2 * t)
                for r in range(ROWS):
                    last = v.scalar_tensor_tensor(u1[:, r, :], xn[b][:, r, :], dd[b][:, r:r + 1], a1[b][:, r, 0:D], ALU.mult, ALU.add)
                last.then_inc(u1_r, 1)
                dve.wait_ge(a2_r, t + 1)
                after(dve, u2T_p, 2 * t)
                dve.wait_ge(u1_r, t + 1)
                for r in range(ROWS):
                    last = v.scalar_tensor_tensor(u2[:, r, :], u1[:, r, :], dd[b][:, r:r + 1], a2[b][:, r, :], ALU.mult, ALU.add)
                last.then_inc(u2_r, 1)

            def rest(parts, area, hi_ready, lo_ready, t):
                for c in range(2):
                    dve.wait_ge(hi_ready, 2 * t + c + 1)
                    last = v.tensor_tensor(parts[1][:, c, :], area[:, c, :], parts[0][:, c, :].bitcast(f32), ALU.subtract)
                last.then_inc(lo_ready, 1)

            def add_half(t, b, half):
                dve.wait_ge(z_p, 2 * t + half + 1)
                rows = slice(2 * half, 2 * half + 2)
                return v.tensor_tensor(x2[b][:, rows, :], x2[b][:, rows, :], pZ[:, half, :].rearrange("p (r n) -> p r n", n=D), ALU.add)

            def step(i, b):
                t = 2 * i + b
                if runs(t - 1):
                    add_half(t - 1, 1 - b, 1).then_inc(x2_r, 1)
                if runs(t):
                    rest(xnT_s, pT, xnT_hi, xnT_lo, t)
                    rest(u1T_s, pO, u1T_hi, u1T_lo, t)
                if runs(t - 1):
                    dve.wait_ge(x2_r, t)
                    after(dve, froot_r, t - 1)
                    ch = Chain(dve, fs_steps, 1, t - 1, carried_dve)
                    for r in range(ROWS):
                        last = v.bn_stats(stat2[:, r, :], x2[1 - b][:, r, :])
                    ch.link(last)
                    ch.now()
                    ch.end()
                    for r in range(ROWS):
                        last = v.bn_aggr(mv2[:, r, :], stat2[:, r, :])
                    last.then_inc(fstat_r, 1)
                if runs(t):
                    dve.wait_ge(scale_r, t + 1)
                    dve.wait_ge(h_p, t + 1)
                    for r in range(ROWS):
                        last = v.scalar_tensor_tensor(hpre[:, r, :], pT[:, 0, r * GATE:(r + 1) * GATE], r2[b][:, r:r + 1], h_row[:, :], ALU.mult, ALU.add)
                    last.then_inc(hpre_r, 1)
                    rest(u2T_s, pA, u2T_hi, u2T_lo, t)
                steps_over_graph(t + 1, 1 - b)
                if runs(t):
                    dve.wait_ge(base_r, t + 1)
                    after(dve, bias_r, t - 1)
                    after(dve, xf_r, t - 1)
                    for r in range(ROWS):
                        last = v.scalar_tensor_tensor(x2[b][:, r, :], s_row[:, :], deg1[b][:, r:r + 1], xb[b][:, r, :], ALU.mult, ALU.add)
                    last.then_inc(half_r, 1)
                    dve.wait_ge(o_p, t + 1)
                    dve.wait_ge(gate_r, t + 1)
                    v.scalar_tensor_tensor(yT[:, :, :], gT[:, :, :], 1.0, pO[:, :, :], ALU.add, ALU.mult).then_inc(y_r, 1)
                if runs(t - 1):
                    dve.wait_ge(absx_r, t)
                    v.tensor_scalar(absT_s[0][:, :, :], absx[:, :, :], FFN_EPS, None, ALU.add).then_inc(abs_hi, 1)
                    dve.wait_ge(abs_hi, t)
                    v.scalar_tensor_tensor(absT_s[1][:, :, :], absx[:, :, :], FFN_EPS, absT_s[0][:, :, :].bitcast(f32),
                                           ALU.add, ALU.subtract).then_inc(abs_lo, 1)
                if runs(t):
                    dve.wait_ge(y_hi, t + 1)
                    v.tensor_tensor(yT_s[1][:, :, :], yT[:, :, :], yT_s[0][:, :, :].bitcast(f32), ALU.subtract).then_inc(y_lo, 1)
                statistics(*later(i, b, 2))
                if runs(t - 1):
                    dve.wait_ge(ffn_p, t)
                    dve.wait_ge(osgn_r, t)
                    after(dve, res_r, t - 1)
                    v.tensor_tensor(prod[:, :, :], halves(pA), osgn[:, :, :], ALU.mult).then_inc(prod_r, 1)
                if runs(t):
                    dve.wait_ge(half_r, t + 1)
                    add_half(t, b, 0)

            statistics(0, 0)
            statistics(0, 1)
            steps_over_graph(0, 0)
            walk_tiles(dve, step)

        @block.tensor
        def _(pe):
            te = nc.tensor

            def turn(area, rows_tile, filled):
                for c in range(2):
                    for r in range(ROWS):
                        last = te.transpose(area[:, c, r * P:(r + 1) * P], rows_tile[:, r, c * P:(c + 1) * P], ident[:, :])
                    last.then_inc(filled, 1)

            def product(result, left, right, start, stop):
                for k in range(2):
                    for n, (l, r) in enumerate(PASSES):
                        last = te.matmul(result, left(k, l), right(k, r), start=start and k == 0 and n == 0,
                                         stop=stop and k == 1 and n == len(PASSES) - 1)
                return last

            def rows_of(parts, r):
                return lambda k, n: parts[n][:, k, r * P:(r + 1) * P]

            def weights(parts):
                return lambda k, n: parts[n][:, k, :]

            def graph_terms(half):
                te.matmul(pZ[:, half, :], ones[:, :], c_parts[:, :, :].rearrange("p a n -> p (a n)"), start=True, stop=False)
                for r in (2 * half, 2 * half + 1):
                    product(halves(pZ)[:, r, :], rows_of(u1T_s, r), weights(wB_s), False, False)
                    product(halves(pZ)[:, r, :], rows_of(u2T_s, r), weights(wA_s), False, False)

            def step(i, b):
                t = 2 * i + b
                if runs(t):
                    pe.wait_ge(tnorm_r, t + 1)
                    after(pe, osgn_r, t - 1)
                    turn(pT, xn[b], xnT_p)
                    pe.wait_ge(u1_r, t + 1)
                    after(pe, y_r, t)
                    turn(pO, u1, u1T_p)
                    pe.wait_ge(u2_r, t + 1)
                    after(pe, prod_r, t - 1)
                    turn(pA, u2, u2T_p)
                    pe.wait_ge(xnT_lo, t + 1)
                    for r in range(ROWS):
                        last = product(pT[:, 0, r * GATE:(r + 1) * GATE], rows_of(xnT_s, r), weights(wg1g_s), True, True)
                    last.then_inc(h_p, 1)
                    pe.wait_ge(u1T_lo, t + 1)
                    for c in range(2):
                        last = product(pO[:, c, :], lambda k, n: wM_s[n][:, k, c * P:(c + 1) * P], lambda k, n: xnT_s[n][:, k, :], True, True)
                    last.then_inc(o_p, 1)
                    pe.wait_ge(hid_r, t + 1)
                    before_fixed(pe, carried_pe)
                    for r in range(ROWS):
                        last = te.transpose(pT[0:GATE, 1, r * P:(r + 1) * P], hid[:, r, :], ident[:, :])
                    last.then_inc(hT_p, 1)
                    pe.wait_ge(u2T_lo, t + 1)
                    after(pe, x2_r, t)
                    graph_terms(0)
                    pe.wait_ge(hT_r, t + 1)
                    for c in range(2):
                        last = te.matmul(pA[:, c, :], wg2[:, c * P:(c + 1) * P], hT[:, :], start=True, stop=True)
                    last.then_inc(gate_p, 1)
                if runs(t - 1):
                    pe.wait_ge(xf_r, t)
                    if not runs(t):
                        pe.wait_ge(osgn_r, t - 1)
                    turn(pT, xf, xf_p)
                if runs(t):
                    graph_terms(1)
                if runs(t - 1):
                    pe.wait_ge(absx_r, t)
                    pe.wait_ge(sgnT_r, t)
                    for r in range(ROWS):
                        for k in range(2):
                            last = te.matmul(halves(pT)[:, r, :], sgnT[:, k, r * P:(r + 1) * P], wsgnT[:, k, :], start=k == 0, stop=k == 1)
                    last.then_inc(sgn_p, 1)
                    pe.wait_ge(abs_lo, t)
                    if runs(t):
                        pe.wait_ge(gate_r, t + 1)
                    else:
                        pe.wait_ge(prod_r, t - 1)
                    for r in range(ROWS):
                        last = product(halves(pA)[:, r, :], rows_of(absT_s, r), weights(wabsT_s), True, True)
                    last.then_inc(ffn_p, 1)
                if runs(t):
                    pe.wait_ge(y_lo, t + 1)
                    for r in range(ROWS):
                        last = product(halves(pZ)[:, r, :], rows_of(yT_s, r), weights(wproj_s), False, r % 2 == 1)
                        if r % 2 == 1:
                            last.then_inc(z_p, 1)

            walk_tiles(pe, step)

        @block.scalar
        def _(act):
            a = nc.scalar

            def first_parts(parts, area, filled, hi_ready, t):
                for c in range(2):
                    act.wait_ge(filled, 2 * t + c + 1)
                    a.activation(parts[0][:, c, :], area[:, c, :], ACT.Copy).then_inc(hi_ready, 1)

            def normalize(t, b):
                if not runs(t):
                    return
                act.wait_ge(troot_r, t + 1)
                after(act, u1_r, t - 1)
                after(act, xnT_p, 2 * (t - 1))
                for r in range(ROWS):
                    last = a.activation(xn[b][:, r, :], xt[b][:, r, :], ACT.Identity, bias=nmr[b][:, r:r + 1], scale=rstd[b][:, r:r + 1])
                last.then_inc(tnorm_r, 1)

            def scale_sums(sums, i, b, ready):
                t = 2 * i + b
                if not runs(t):
                    return
                act.wait_ge(a_in[b], 48 * (i + 1))
                for r in range(ROWS):
                    last = a.activation(sums[b][:, r, 0:D], sums[b][:, r, 0:D], ACT.Copy, scale=dv[b][:, r:r + 1])
                last.then_inc(ready, 1)

            def step(i, b):
                t = 2 * i + b
                nxt = later(i, b, 1)
                if runs(t):
                    first_parts(xnT_s, pT, xnT_p, xnT_hi, t)
                    first_parts(u1T_s, pO, u1T_p, u1T_hi, t)
                    first_parts(u2T_s, pA, u2T_p, u2T_hi, t)
                normalize(t + 1, 1 - b)
                scale_sums(a1, *nxt, a1_r)
                if runs(t):
                    act.wait_ge(hpre_r, t + 1)
                    a.activation(hid[:, :, :], hpre[:, :, :], ACT.Gelu).then_inc(hid_r, 1)
                scale_sums(a2, *nxt, a2_r)
                if runs(t):
                    act.wait_ge(hT_p, t + 1)
                    a.activation(hT[:, :], pT[0:GATE, 1, :], ACT.Copy).then_inc(hT_r, 1)
                if runs(t - 1):
                    act.wait_ge(froot_r, t)
                    after(act, xf_p, 2 * (t - 1))
                    for r in range(ROWS):
                        last = a.activation(xf[:, r, :], x2[1 - b][:, r, :], ACT.Identity, bias=nmr2[:, r:r + 1], scale=rstd2[:, r:r + 1])
                    last.then_inc(xf_r, 1)
                if runs(t):
                    act.wait_ge(gate_p, t + 1)
                    after(act, y_r, t)
                    for c in range(2):
                        last = a.activation(gT[:, c, :], pA[:, c, :], ACT.Tanh, bias=bg2c[:, c:c + 1], scale=0.5)
                    last.then_inc(gate_r, 1)
                if runs(t - 1):
                    act.wait_ge(xf_p, 2 * t)
                    a.activation(absx[:, :, :], pT[:, :, :], ACT.Abs).then_inc(absx_r, 1)
                    a.activation(sgnT[:, :, :], pT[:, :, :], ACT.Sign).then_inc(sgnT_r, 1)
                if runs(t):
                    act.wait_ge(y_r, t + 1)
                    a.activation(yT_s[0][:, :, :], yT[:, :, :], ACT.Copy).then_inc(y_hi, 1)
                if runs(t - 1):
                    act.wait_ge(sgn_p, t)
                    after(act, prod_r, t - 1)
                    a.activation(osgn[:, :, :], halves(pT), ACT.Sign).then_inc(osgn_r, 1)

            normalize(0, 0)
            scale_sums(a1, 0, 0, a1_r)
            scale_sums(a2, 0, 0, a2_r)
            walk_tiles(act, step)


_INS = ["x", "src", "dst", "edge_weight", "L0_gnn_W1", "L0_gnn_b1", "L0_gnn_W2", "L0_gnn_b2", "L0_mix_Wqkv", "L0_mix_Wproj",
        "L0_mix_bproj", "L0_mix_ln_g", "L0_mix_ln_b", "L0_mix_Wg1", "L0_mix_bg1", "L0_mix_Wg2", "L0_mix_bg2",
        "L0_ffn_weight", "L0_ffn_bias"]


def kernel(**inputs):
    import numpy as _np
    import concourse.bacc as _bacc
    from concourse import mybir as _mybir
    from concourse.bass_utils import run_bass_kernel_spmd as _run

    nc = _bacc.Bacc("TRN2", target_bir_lowering=False, num_devices=1)
    arrays, args = {}, []
    for name in _INS:
        a = _np.ascontiguousarray(inputs[name])
        arrays[f"in_{name}"] = a
        args.append(nc.dram_tensor(f"in_{name}", a.shape, _mybir.dt.from_np(a.dtype), kind="ExternalInput").ap())
    args.append(nc.dram_tensor("out_0", (NODES, D), _mybir.dt.float32, kind="ExternalOutput").ap())
    build_gps(nc, *args)
    r = _run(nc, [arrays], core_ids=[0])
    return r.results[0]["out_0"]
```

```python
from contextlib import ExitStack

import concourse.bass as bass
from concourse import mybir

NODES, D, EDGES = 50000, 256, 25000
HEADS, GATE = 8, 64
HD = D // HEADS
KEEP = 0.1
MIX = 1.0 - KEEP
LN_EPS, FFN_EPS, DEG_FLOOR = 1e-5, 1e-8, 1e-30

P, ROWS = 128, 4
TILE = P * ROWS
FULL = NODES // TILE
TAIL_ROWS = 3
TAIL_P = (NODES - FULL * TILE) // TAIL_ROWS
TILES = FULL + 1

EP, CH = 125, 4
GROUP = EP * CH
GROUPS = EDGES // GROUP
assert GROUPS * GROUP == EDGES and GROUPS % 2 == 0 and FULL * TILE + TAIL_P * TAIL_ROWS == NODES

LO = -(-NODES // P)
EC = EDGES // EP

SPARE = NODES
FILL = GROUPS // 2
FILL_ROWS = 16
STEP_ROWS = FILL * FILL_ROWS // GROUPS
SCRATCH_ROWS = P * FILL * FILL_ROWS
assert SCRATCH_ROWS >= SPARE + GROUP and LO * P <= SCRATCH_ROWS
W1COLS = D + 8


def after(engine, semaphore, value):
    if isinstance(value, int) and value <= 0:
        return
    engine.wait_ge(semaphore, value)


def before_fixed(engine, carried):
    engine.sem_inc(carried, 1)


class Chain:

    def __init__(self, engine, semaphore, per, rnd, carried=None):
        self.engine, self.semaphore, self.per, self.rnd, self.n, self.carried = engine, semaphore, per, rnd, 0, carried

    def link(self, instruction):
        instruction.then_inc(self.semaphore, 1)
        self.n += 1

    def now(self):
        self.engine.wait_ge(self.semaphore, self.rnd * self.per + self.n)
        if self.carried is not None:
            before_fixed(self.engine, self.carried)

    def end(self):
        assert self.n == self.per, (self.n, self.per)


def build_gps(nc, x, src, dst, edge_weight, W1, b1, W2, b2, Wqkv, Wproj, bproj, ln_g, ln_b,
              Wg1, bg1, Wg2, bg2, ffn_w, ffn_b, out):
    f32, f32r, bf16, i32 = mybir.dt.float32, mybir.dt.float32r, mybir.dt.bfloat16, mybir.dt.int32
    ALU, ACT, AX = mybir.AluOpType, mybir.ActivationFunctionType, mybir.AxisListType

    with ExitStack() as ctx:
        def sb(name, shape, dt=f32):
            return ctx.enter_context(nc.sbuf_tensor(name, shape, dt))

        def ps(name, shape, dt=f32):
            return ctx.enter_context(nc.psum_tensor(name, shape, dt))

        def sem(name):
            return ctx.enter_context(nc.semaphore(name))

        def parts_of(name, shape):
            return sb(f"{name}_hi", shape, f32r), sb(f"{name}_lo", shape, f32r)

        PASSES = ((0, 0), (0, 1), (1, 0))

        def sems(name):
            return [sem(f"{name}0"), sem(f"{name}1")]

        def two(name, shape, dt=f32):
            return [sb(f"{name}0", shape, dt), sb(f"{name}1", shape, dt)]

        dinv_d = nc.dram_tensor("dinv_d", (P * LO, 1), f32, kind="Internal").ap()
        agg1_d = nc.dram_tensor("agg1_d", (SCRATCH_ROWS, W1COLS), f32, kind="Internal").ap()
        agg2_d = nc.dram_tensor("agg2_d", (SCRATCH_ROWS, D), f32, kind="Internal").ap()
        msg_d = nc.dram_tensor("msg_d", (EDGES, D), f32, kind="Internal").ap()
        dsq_d = nc.dram_tensor("dsq_d", (EDGES,), f32, kind="Internal").ap()

        wqkv = sb("wqkv", [P, 2, 3 * D])
        bg2c, h_col = sb("bg2c", [P, 2]), sb("h_col", [P, 1])
        ffnb_row = sb("ffnb_row", [P, D])
        ident = sb("ident", [P, P])
        minus_half = sb("minus_half", [P, ROWS + CH])
        headmask = sb("headmask", [P, 2, D])
        wqT, wM = sb("wqT", [P, 2, D]), sb("wM", [P, 2, D])
        wsgnT = sb("wsgnT", [P, 2, D], bf16)
        wA_s, wB_s, wproj_s, wabsT_s, wM_s = (parts_of(n, [P, 2, D]) for n in ("wA", "wB", "wproj", "wabsT", "wM"))
        wg1g_s, wg2_s = parts_of("wg1g", [P, 2, 2 * GATE]), parts_of("wg2s", [P, D])
        ones, c_parts = sb("ones", [2, P], f32r), sb("c_parts", [2, 2, D], f32r)
        s_row, c_row = sb("s_row", [P, D]), sb("c_row", [P, D])

        xt = two("xt", [P, ROWS, D])
        stat = two("stat", [P, ROWS, 6])
        mv = two("mv", [P, ROWS, 2])
        veps, rstd, nmean, nmr = two("veps", [P, ROWS]), two("rstd", [P, ROWS]), two("nmean", [P, ROWS]), two("nmr", [P, ROWS])
        xn = two("xn", [P, ROWS, D])
        xnT = sb("xnT", [P, 2, TILE])

        gsum = sb("gsum", [P, 2, D])
        esum = sb("esum", [P, 2])

        early = ctx.enter_context(ExitStack())

        def sbe(name, shape, dt=f32):
            return early.enter_context(nc.sbuf_tensor(name, shape, dt))

        w1, w2, wproj, wffn = (sbe(n, [P, 2, D]) for n in ("w1", "w2", "wproj", "wffn"))
        w1T, wA, wB, wabsT = (sbe(n, [P, 2, D]) for n in ("w1T", "wA", "wB", "wabsT"))
        wg1, wg1g, wg2 = sbe("wg1", [P, 2, 2 * GATE]), sbe("wg1g", [P, 2, 2 * GATE]), sbe("wg2", [P, D])
        bg1c = sbe("bg1c", [P, 1])
        b1c, lngc, lnbc = sbe("b1c", [P, 2]), sbe("lngc", [P, 2]), sbe("lnbc", [P, 2])
        b1b = sbe("b1b", [P, 2, P])
        b1_row, b2_row, bproj_row = sbe("b1_row", [P, D]), sbe("b2_row", [P, D]), sbe("bproj_row", [P, D])
        c_hi, c_lo, c_steps = sbe("c_hi", [2, D], f32r), sbe("c_lo", [2, D]), sem("c_steps")
        zeros = sbe("zeros", [P, FILL_ROWS * W1COLS])
        tri = sbe("tri", [EP, GROUP])
        spare = sbe("spare", [EP, CH])

        pT = ps("pT", [P, 2, TILE])
        pK = ps("pK", [P, 2, TILE])
        narrow = ctx.enter_context(ExitStack())
        pG = narrow.enter_context(nc.psum_tensor("pG", [P, 2, D], f32))
        pB = narrow.enter_context(nc.psum_tensor("pB", [P, 512], f32))
        pC = [narrow.enter_context(nc.psum_tensor(f"pC{n}", [P, 512], f32)) for n in range(2)]

        rows_ready, carried_pool, carried_pe, carried_dve = sem("rows_ready"), sem("carried_pool"), sem("carried_pe"), sem("carried_dve")
        split_r = sem("split_r")
        loaded, setup_pool, setup_dve, setup_pe, setup_act = (
            sem("loaded"), sem("setup_pool"), sem("setup_dve"), sem("setup_pe"), sem("setup_act"))

        N_LOADS = 19
        with ExitStack() as s0:
            def sb0(name, shape, dt=f32):
                return s0.enter_context(nc.sbuf_tensor(name, shape, dt))

            dst_i = sb0("dst_i", [EP, EC], i32)
            ew_all = sb0("ew_all", [EP, EC])
            dstf, hi, lo, fix = sb0("dstf", [EP, EC]), sb0("hi", [EP, EC]), sb0("lo", [EP, EC]), sb0("fix", [EP, EC])
            hi_i = sb0("hi_i", [EP, EC], i32)
            iota_hi, iota_lo = sb0("iota_hi", [EP, P]), sb0("iota_lo", [EP, LO])
            UN = 4
            oneh = [sb0(f"oneh{u}", [EP, P]) for u in range(UN)]
            onel = [sb0(f"onel{u}", [EP, LO]) for u in range(UN)]
            deg, dpos, dinv = sb0("deg", [P, LO]), sb0("dpos", [P, LO]), sb0("dinv", [P, LO])
            droot, dsq = sb0("droot", [P, LO]), sb0("dsq", [P, LO])
            edges_in, hot_ready, hot_used = sem("edges_in"), sem("hot_ready"), sem("hot_used")
            deg_sum, deg_ready, root_ready, dinv_ready, dinv_stored, zero1 = (
                sem("deg_sum"), sem("deg_ready"), sem("root_ready"), sem("dinv_ready"), sem("dinv_stored"), sem("zero1"))
            root_steps = sem("root_steps")
            deg_steps, row_steps, abs_ready = sem("deg_steps"), sem("row_steps"), sem("abs_ready")
            block = s0.enter_context(nc.Block())

            @block.sync
            def _(sp):
                sp.dma_start(dst_i[:, :], dst.rearrange("(p c) -> p c", c=EC)).then_inc(edges_in, 16)
                sp.dma_start(ew_all[:, :], edge_weight.rearrange("(p c) -> p c", c=EC)).then_inc(edges_in, 16)
                for tile, w in ((wqkv, Wqkv), (w1, W1), (w2, W2), (wproj, Wproj), (wffn, ffn_w)):
                    sp.dma_start(tile[:, :, :], w.rearrange("(c p) n -> p c n", p=P)).then_inc(loaded, 16)
                for half in (slice(0, GATE), slice(GATE, 2 * GATE)):
                    sp.dma_start(wg1[:, :, half], Wg1.rearrange("(c p) n -> p c n", p=P)).then_inc(loaded, 16)
                    sp.dma_start(wg2[half, :], Wg2[:, :]).then_inc(loaded, 16)
                    sp.dma_start(bg1c[half, :], bg1.rearrange("(p a) -> p a", a=1)).then_inc(loaded, 16)
                with nc.allow_non_contiguous_dma("four short columns of parameters"):
                    for tile, v in ((b1c, b1), (lngc, ln_g), (lnbc, ln_b), (bg2c, bg2)):
                        sp.dma_start(tile[:, :], v.rearrange("(c p) -> p c", p=P)).then_inc(loaded, 16)
                for tile, v in ((b1_row, b1), (b2_row, b2), (bproj_row, bproj), (ffnb_row, ffn_b)):
                    sp.dma_start(tile[:, :], v.rearrange("(a n) -> a n", a=1).partition_broadcast(P)).then_inc(loaded, 16)
                sp.wait_ge(dinv_ready, 1)
                sp.dma_start(dinv_d.rearrange("(p c) a -> p (c a)", c=LO), dinv[:, :]).then_inc(dinv_stored, 16)
                sp.wait_ge(dinv_stored, 16)

            @block.gpsimd
            def _(pool):
                pool.iota(iota_hi[:, :], [[1, P]], base=0, channel_multiplier=0, allow_small_or_imprecise_dtypes=True)
                pool.iota(iota_lo[:, :], [[1, LO]], base=0, channel_multiplier=0, allow_small_or_imprecise_dtypes=True).then_inc(setup_pool, 1)
                pool.memset(zeros[:, :], 0.0).then_inc(setup_pool, 1)
                pool.memset(minus_half[:, :], -0.5)
                pool.iota(spare[:, :], [[1, CH]], base=SPARE, channel_multiplier=CH, allow_small_or_imprecise_dtypes=True)
                pool.memset(ident[:, :], 0.0)
                pool.memset(headmask[:, :, :], 1.0)
                pool.memset(tri[:, :], 1.0).then_inc(setup_pool, 1)
                pool.wait_ge(setup_pool, 3)
                pool.affine_select(out=ident[:, :], in_=ident[:, :], compare_op=ALU.not_equal, fill=1.0,
                                   base=0, pattern=[[-1, P]], channel_multiplier=1)
                pool.affine_select(out=tri[:, 0:EP], in_=tri[:, 0:EP], compare_op=ALU.is_ge, fill=0.0,
                                   base=0, pattern=[[1, EP]], channel_multiplier=-1)
                per_chunk = P // HD
                for c in range(2):
                    m = headmask[:, c, :].rearrange("p (h v) -> p h v", v=HD)
                    last = pool.affine_select(out=m, in_=m, compare_op=ALU.is_ge, fill=0.0,
                                              base=c * P, pattern=[[-HD, HEADS], [0, HD]], channel_multiplier=1)
                last.then_inc(setup_pool, 1)
                pool.wait_ge(setup_pool, 4)
                for c in range(2):
                    m = headmask[:, c, :].rearrange("p (h v) -> p h v", v=HD)
                    last = pool.affine_select(out=m, in_=m, compare_op=ALU.is_ge, fill=0.0,
                                              base=HD - 1 - c * P, pattern=[[HD, HEADS], [0, HD]], channel_multiplier=-1)
                last.then_inc(setup_pool, 1)

            @block.vector
            def _(dve):
                v = nc.vector
                dve.wait_ge(edges_in, 32)
                dve.wait_ge(setup_pool, 1)
                ch = Chain(dve, setup_dve, 8, 0)
                ch.link(v.tensor_copy(dstf[:, :], dst_i[:, :]))
                ch.now()
                ch.link(v.tensor_scalar(hi_i[:, :], dstf[:, :], 1.0 / LO, -0.5, ALU.mult, ALU.add))
                ch.now()
                ch.link(v.tensor_copy(hi[:, :], hi_i[:, :]))
                ch.now()
                ch.link(v.scalar_tensor_tensor(lo[:, :], hi[:, :], -float(LO), dstf[:, :], ALU.mult, ALU.add))
                ch.now()
                v.tensor_scalar(fix[:, :], lo[:, :], float(LO) - 0.5, None, ALU.is_gt)
                ch.link(v.tensor_scalar(hi_i[:, :], lo[:, :], -0.5, None, ALU.is_lt))
                ch.now()
                ch.link(v.tensor_tensor(fix[:, :], fix[:, :], hi_i[:, :], ALU.subtract))
                ch.now()
                ch.link(v.tensor_tensor(hi[:, :], hi[:, :], fix[:, :], ALU.add))
                ch.link(v.scalar_tensor_tensor(lo[:, :], fix[:, :], -float(LO), lo[:, :], ALU.mult, ALU.add))
                ch.now()
                ch.end()

                def hot(i, u):
                    c = i * UN + u
                    after(dve, hot_used, c - UN + 1)
                    col = slice(c, c + 1) if isinstance(c, int) else bass.ds(c, 1)
                    v.tensor_scalar(oneh[u][:, :], iota_hi[:, :], hi[:, col], None, ALU.is_equal)
                    v.tensor_scalar(onel[u][:, :], iota_lo[:, :], lo[:, col], ew_all[:, col],
                                    ALU.is_equal, ALU.mult).then_inc(hot_ready, 1)

                for u in range(UN):
                    hot(0, u)
                with dve.Fori(1, EC // UN) as i:
                    for u in range(UN):
                        hot(i, u)
                dve.wait_ge(deg_sum, 1)
                ch = Chain(dve, deg_steps, 1, 0)
                ch.link(v.tensor_scalar(deg[:, :], pB[:, 0:LO], 1.0, None, ALU.add))
                ch.now()
                ch.end()
                v.tensor_scalar(dpos[:, :], deg[:, :], 0.0, None, ALU.is_gt)
                v.tensor_scalar(deg[:, :], deg[:, :], DEG_FLOOR, None, ALU.max).then_inc(deg_ready, 1)
                dve.wait_ge(root_ready, 1)
                ch = Chain(dve, root_steps, 5, 0)
                ch.link(v.reciprocal(dinv[:, :], droot[:, :]))
                ch.now()
                ch.link(v.tensor_tensor(dsq[:, :], dinv[:, :], dinv[:, :], ALU.mult))
                ch.link(v.tensor_tensor(dinv[:, :], dinv[:, :], dpos[:, :], ALU.mult))
                ch.now()
                ch.link(v.scalar_tensor_tensor(dsq[:, :], dsq[:, :], -0.5, deg[:, :], ALU.mult, ALU.mult))
                ch.now()
                ch.link(v.tensor_scalar(dsq[:, :], dsq[:, :], 1.5, None, ALU.add))
                ch.now()
                ch.end()
                v.tensor_tensor(dinv[:, :], dinv[:, :], dsq[:, :], ALU.mult).then_inc(dinv_ready, 1)
                dve.wait_ge(loaded, 16 * N_LOADS)
                dve.wait_ge(setup_pool, 5)
                v.tensor_tensor(wB[:, :, :], w1[:, :, :], w2[:, :, :], ALU.add)
                for c in range(2):
                    v.tensor_scalar(wg1g[:, c, :], wg1[:, c, :], lngc[:, c:c + 1], None, ALU.mult)
                    v.tensor_copy(b1b[:, c, :], b1c[:, c:c + 1].broadcast_to([P, P]))
                v.tensor_scalar(b1_row[:, :], b1_row[:, :], MIX * KEEP, None, ALU.mult)
                ch = Chain(dve, row_steps, 2, 0)
                v.tensor_scalar(bg2c[:, :], bg2c[:, :], 0.5, None, ALU.mult)
                ch.link(v.tensor_scalar(wproj[:, :, :], wproj[:, :, :], 0.5, None, ALU.mult))
                ch.now()
                ch.link(v.scalar_tensor_tensor(c_row[:, :], b2_row[:, :], MIX, b1_row[:, :], ALU.mult, ALU.add))
                ch.now()
                v.tensor_scalar(wB[:, :, :], wB[:, :, :], MIX * KEEP, None, ALU.mult)
                v.tensor_tensor(c_row[:, :], c_row[:, :], bproj_row[:, :], ALU.add).then_inc(rows_ready, 1)
                ch.end()
                dve.wait_ge(setup_pe, 1)
                v.tensor_copy(w1T[:, :, :], pT[:, 0, :].rearrange("p (c n) -> p c n", c=2))
                v.tensor_copy(wqT[:, :, :], pT[:, 1, :].rearrange("p (c n) -> p c n", c=2)).then_inc(setup_act, 1)
                dve.wait_ge(abs_ready, 1)
                v.tensor_scalar(wabsT[:, :, :], wabsT[:, :, :], FFN_EPS, None, ALU.add)
                dve.wait_ge(setup_pe, 2)
                v.tensor_scalar(s_row[:, :], pC[0][:, 0:D], MIX * MIX, None, ALU.mult)
                v.tensor_tensor(h_col[:, :], pC[1][:, 0:1], bg1c[:, :], ALU.add)
                v.tensor_scalar(wA[:, :, :], pG[:, :, :], MIX * MIX, None, ALU.mult).then_inc(setup_act, 1)
                dve.wait_ge(setup_act, 2)
                pairs = ((wA, wA_s), (wB, wB_s), (wproj, wproj_s), (wabsT, wabsT_s), (wg1g, wg1g_s))
                v.tensor_copy(wg2_s[0][:, :], wg2[:, :])
                for w, parts in pairs:
                    last = v.tensor_copy(parts[0][:, :, :], w[:, :, :])
                last.then_inc(split_r, 1)
                dve.wait_ge(split_r, 1)
                for w, parts in pairs:
                    v.tensor_tensor(parts[1][:, :, :], w[:, :, :], parts[0][:, :, :].bitcast(f32), ALU.subtract)
                v.tensor_tensor(wg2_s[1][:, :], wg2[:, :], wg2_s[0][:, :].bitcast(f32), ALU.subtract)
                ch = Chain(dve, c_steps, 3, 0)
                v.tensor_scalar(ones[:, :], zeros[0:2, 0:P], 1.0, None, ALU.add)
                ch.link(v.tensor_copy(c_hi[:, :], c_row[0:2, :]))
                ch.now()
                ch.link(v.tensor_tensor(c_lo[:, :], c_row[0:2, :], c_hi[:, :].bitcast(f32), ALU.subtract))
                ch.now()
                ch.link(v.tensor_scalar(c_lo[:, :], c_lo[:, :], ident[0:2, 1:2], None, ALU.mult))
                ch.now()
                ch.end()
                for r in range(2):
                    v.scalar_tensor_tensor(c_parts[:, r, :], c_hi[:, :].bitcast(f32), ident[0:2, 0:1], c_lo[:, :], ALU.mult, ALU.add)

            @block.tensor
            def _(pe):
                t = nc.tensor
                pe.wait_ge(setup_pool, 2)
                t.matmul(pB[:, 0:LO], zeros[0:EP, 0:P], zeros[0:EP, 0:LO], start=True, stop=False)

                def add_chunk(i, u):
                    pe.wait_ge(hot_ready, i * UN + u + 1)
                    t.matmul(pB[:, 0:LO], oneh[u][:, :], onel[u][:, :], start=False, stop=False).then_inc(hot_used, 1)

                with pe.Fori(0, EC // UN) as i:
                    for u in range(UN):
                        add_chunk(i, u)
                t.matmul(pB[:, 0:LO], zeros[0:EP, 0:P], zeros[0:EP, 0:LO], start=False, stop=True).then_inc(deg_sum, 1)
                pe.wait_ge(loaded, 16 * N_LOADS)
                pe.wait_ge(setup_pool, 5)
                for area, w in ((pT[:, 0, :], w1), (pT[:, 1, :], wqkv), (pK[:, 0, :], wffn)):
                    for c in range(2):
                        for k in range(2):
                            last = t.transpose(area[:, k * D + c * P:k * D + (c + 1) * P], w[:, c, k * P:(k + 1) * P], ident[:, :])
                last.then_inc(setup_pe, 1)
                pe.wait_ge(setup_act, 1)
                pe.wait_ge(rows_ready, 1)
                for c in range(2):
                    for k in range(2):
                        t.matmul(pG[:, c, :], w1T[:, k, c * P:(c + 1) * P], w2[:, k, :], start=k == 0, stop=k == 1)
                for k in range(2):
                    t.matmul(pC[0][:, 0:D], b1b[:, k, :], w2[:, k, :], start=k == 0, stop=k == 1)
                for k in range(2):
                    last = t.matmul(pC[1][:, 0:1], wg1[:, k, :], lnbc[:, k:k + 1], start=k == 0, stop=k == 1)
                last.then_inc(setup_pe, 1)

            @block.scalar
            def _(act):
                act.wait_ge(setup_pool, 2)
                with act.Fori(0, FILL) as i:
                    act.dma_start(agg1_d.rearrange("(k p r) w -> k p (r w)", k=FILL, p=P)[bass.ds(i, 1), :, :].rearrange("k p n -> (k p) n"),
                                  zeros[:, :]).then_inc(zero1, 16)
                act.wait_ge(deg_ready, 1)
                nc.scalar.activation(droot[:, :], deg[:, :], ACT.Sqrt).then_inc(root_ready, 1)
                act.wait_ge(setup_pe, 1)
                nc.scalar.activation(wabsT[:, :, :], pK[:, 0, :].rearrange("p (c n) -> p c n", c=2), ACT.Abs).then_inc(abs_ready, 1)
                nc.scalar.activation(wsgnT[:, :, :], pK[:, 0, :].rearrange("p (c n) -> p c n", c=2), ACT.Sign)
                act.wait_ge(zero1, 16 * FILL)

        E2 = GROUPS * 2
        with ExitStack() as s1:
            def sb1(name, shape, dt=f32):
                return s1.enter_context(nc.sbuf_tensor(name, shape, dt))

            def two1(name, shape, dt=f32):
                return [sb1(f"{name}0", shape, dt), sb1(f"{name}1", shape, dt)]

            eT = sb1("eT", [P, 2, TILE])
            en = two1("en", [P, ROWS, D])
            blkmax = sb1("blkmax", [P, 2])
            kmax, negmax, drop, alpha, rsum = (two1("kmax", [P, 2]), two1("negmax", [P, 2]), two1("drop", [P, 2]),
                                               two1("alpha", [P, 2]), two1("rsum", [P, 2]))
            esrc, edst = two1("esrc", [EP, CH], i32), two1("edst", [EP, CH], i32)
            drow = two1("drow", [EP, GROUP], i32)
            dview = [a[:, :].rearrange("p (l c) -> p c l", c=CH) for a in drow]
            eew, dsrc, edstf = two1("eew", [EP, CH]), two1("dsrc", [EP, CH]), sb1("edstf", [EP, CH])
            xg = two1("xg", [EP, CH, W1COLS])
            m1t = two1("m1t", [EP, CH, D])
            stat_rows, mvs = sb1("stat_rows", [P, ROWS + CH, 6]), sb1("mvs", [P, ROWS + CH, 2])
            vars_eps, roots, shift = sb1("vars_eps", [P, ROWS + CH]), two1("roots", [P, ROWS]), two1("shift", [P, ROWS])
            coef, ca, cb = sb1("coef", [EP, CH]), sb1("ca", [EP, CH]), sb1("cb", [EP, CH])
            msg = two1("msg", [EP, CH, W1COLS])
            msg_hi, msg_lo = two1("msg_hi", [EP, CH, D], f32r), two1("msg_lo", [EP, CH, D], f32r)
            same = two1("same", [EP, CH, GROUP], f32r)
            cnt, toodd, rowf = sb1("cnt", [EP, CH]), sb1("toodd", [EP, CH]), sb1("rowf", [EP, CH])
            rowi = two1("rowi", [EP, CH], i32)
            comb = two1("comb", [EP, CH, W1COLS])
            comb2 = [a[:, :, :].rearrange("p c w -> p (c w)")[:, 0:CH * D].rearrange("p (c w) -> p c w", c=CH) for a in comb]

            x_in, e_in, g_in, m_in, m_out = sems("x_in"), sems("e_in"), sems("g_in"), sems("m_in"), sems("m_out")
            zero2, scattered = sem("zero2"), sem("scattered")
            (stat_r, root_r, xn_r, xT_p, xT_r, k_p, max_r, e_r, en_p, en_r, g_p, g_r) = (sem(n) for n in (
                "stat_r", "root_r", "xn_r", "xT_p", "xT_r", "k_p", "max_r", "e_r", "en_p", "en_r", "g_p", "g_r"))
            gstat_r, groot_r, gs_steps = sem("gstat_r"), sem("groot_r"), sem("gs_steps")
            group_root = sb1("group_root", [EP, CH])
            dsq = two1("dsq", [EP, CH])
            kept_r, hi_r, lo_r, xn2_r, m_steps = sem("kept_r"), sem("hi_r"), sem("lo_r"), sem("xn2_r"), sem("m_steps")
            msg_r, same_r, row_r, comb_p, comb_r, shift_r = (
                sem("msg_r"), sem("same_r"), sem("row_r"), sem("comb_p"), sem("comb_r"), sem("shift_r"))
            n_steps, e_steps, e2_steps, s_steps, init = sem("n_steps"), sem("e_steps"), sem("e2_steps"), sem("s_steps"), sem("init")
            block = s1.enter_context(nc.Block())

            def nodes_of(array, t, rows, parts, width):
                first = t * TILE
                view = array[first:first + parts * rows, :] if isinstance(first, int) else array[bass.ds(first, parts * rows), :]
                return view.rearrange("(p r) w -> p (r w)", r=rows)

            def group_of(vector, g):
                first = g * GROUP
                view = vector[first:first + GROUP] if isinstance(first, int) else vector[bass.ds(first, GROUP)]
                return view.rearrange("(p c) -> p c", c=CH)

            def group_rows(array, g):
                first = g * GROUP
                view = array[first:first + GROUP, :] if isinstance(first, int) else array[bass.ds(first, GROUP), :]
                return view.rearrange("(p c) w -> p (c w)", c=CH)

            def shape(t):
                return (TAIL_P, TAIL_ROWS) if isinstance(t, int) and t == FULL else (P, ROWS)

            HALF = GROUPS // 2

            def walk(engine, step):
                for b in range(2):
                    step(0, b, 1)
                with engine.Fori(1, HALF - 1) as i:
                    for b in range(2):
                        step(i, b, 1)
                for b in range(2):
                    step(HALF - 1, b, 1)
                with engine.Fori(HALF, FULL // 2 - 1) as i:
                    for b in range(2):
                        step(i, b, 2)
                for i in range(FULL // 2 - 1, GROUPS):
                    for b in range(2):
                        step(i, b, 2)

            def later(i, b, n):
                return i + (b + n) // 2, (b + n) % 2

            def has_tile(t):
                return not isinstance(t, int) or 0 <= t < TILES

            def has_group(t):
                return not isinstance(t, int) or 0 <= t < E2

            def layer_of(t, layer):
                return (1 if t < GROUPS else 2) if isinstance(t, int) else layer

            @block.sync
            def _(sp):
                def load(i, b, layer):
                    t = 2 * i + b
                    if has_tile(t):
                        parts, rows = shape(t)
                        after(sp, xn_r, t - 1)
                        if layer == 2:
                            after(sp, xn2_r, t - 1)
                        sp.dma_start(xt[b][0:parts, 0:rows, :].rearrange("p r w -> p (r w)"), nodes_of(x, t, rows, parts, D)).then_inc(x_in[b], 16)
                    g = t if layer == 1 else t - GROUPS
                    after(sp, msg_r, t - 1)
                    after(sp, same_r, t - 1)
                    for tile, vec in ((esrc, src), (edst, dst), (eew, edge_weight)):
                        sp.dma_start(tile[b][:, :], group_of(vec, g)).then_inc(e_in[b], 16)
                    first = g * GROUP
                    piece = dst[first:first + GROUP] if isinstance(first, int) else dst[bass.ds(first, GROUP)]
                    sp.dma_start(drow[b][:, :], piece.rearrange("(a n) -> a n", a=1).partition_broadcast(EP)).then_inc(e_in[b], 16)
                    if layer == 1:
                        keep(t - 2, b)
                    else:
                        sp.dma_start(dsq[b][:, :], group_of(dsq_d, g)).then_inc(m_in[b], 16)
                        sp.dma_start(m1t[b][:, :, :].rearrange("p c w -> p (c w)"), group_rows(msg_d, g)).then_inc(m_in[b], 16)

                def keep(t, b):
                    if isinstance(t, int) and t < 0:
                        return
                    sp.wait_ge(kept_r, t + 1)
                    sp.dma_start(group_rows(msg_d, t), m1t[b][:, :, :].rearrange("p c w -> p (c w)")).then_inc(m_out[b], 16)
                    sp.dma_start(group_of(dsq_d, t), dsq[b][:, :]).then_inc(m_out[b], 16)

                for b in range(2):
                    load(0, b, 1)
                with sp.Fori(1, HALF) as i:
                    for b in range(2):
                        load(i, b, 1)
                keep(GROUPS - 2, 0)
                keep(GROUPS - 1, 1)
                for b in range(2):
                    sp.wait_ge(m_out[b], 32 * HALF)
                with sp.Fori(HALF, FULL // 2) as i:
                    for b in range(2):
                        load(i, b, 2)
                for i in range(FULL // 2, GROUPS):
                    for b in range(2):
                        load(i, b, 2)

            @block.gpsimd
            def _(pool):
                def gathers(i, b, layer, chunks=range(CH)):
                    t = 2 * i + b
                    if not has_group(t):
                        return
                    if 0 in chunks:
                        after(pool, msg_r, t - 1)
                        pool.wait_ge(e_in[b], 64 * (i + 1))
                        before_fixed(pool, carried_pool)
                    for c in chunks:
                        where = bass.IndirectOffsetOnAxis(esrc[b][:, c:c + 1], 0)
                        if layer == 1:
                            pool.indirect_dma_start(xg[b][:, c, 0:D], None, x[:, :], where).then_inc(g_in[b], 16)
                            pool.indirect_dma_start(dsrc[b][:, c:c + 1], None, dinv_d[:, :], where).then_inc(g_in[b], 16)
                        else:
                            pool.indirect_dma_start(xg[b][:, c, :], None, agg1_d[:, :], where).then_inc(g_in[b], 16)

                def tile_roots(t, b):
                    if not has_tile(t):
                        return
                    pool.wait_ge(stat_r, t + 1)
                    after(pool, xn_r, t - 1)
                    before_fixed(pool, carried_pool)
                    pool.tensor_tensor(roots[b][:, 0:ROWS], vars_eps[:, 0:ROWS], minus_half[:, 0:ROWS], ALU.pow).then_inc(root_r, 1)

                def group_roots(t):
                    pool.wait_ge(gstat_r, t + 1)
                    after(pool, msg_r, t)
                    before_fixed(pool, carried_pool)
                    pool.tensor_tensor(group_root[:, :], vars_eps[0:EP, ROWS:ROWS + CH], minus_half[0:EP, 0:CH], ALU.pow).then_inc(groot_r, 1)

                def normalize(t, b):
                    if not has_tile(t):
                        return
                    parts, rows = shape(t)
                    pool.wait_ge(shift_r, t + 1)
                    after(pool, g_p, t - 1)
                    before_fixed(pool, carried_pool)
                    for r in range(ROWS // 2, rows):
                        last = pool.tensor_scalar(xn[b][0:parts, r, :], xt[b][0:parts, r, :], roots[b][0:parts, r:r + 1],
                                                  shift[b][0:parts, r:r + 1], ALU.mult, ALU.add)
                    last.then_inc(xn2_r, 1)

                def scatters(t, b, layer):
                    if not isinstance(t, int) or t > 0:
                        pool.wait_ge(scattered, 64 * t)
                    pool.wait_ge(row_r, t + 1)
                    pool.wait_ge(comb_r, CH * (t + 1))
                    before_fixed(pool, carried_pool)
                    for c in range(CH):
                        where = bass.IndirectOffsetOnAxis(rowi[b][:, c:c + 1], 0)
                        if layer == 1:
                            pool.indirect_dma_start(agg1_d[:, :], where, comb[b][:, c, :], None,
                                                    compute_op=ALU.add).then_inc(scattered, 16)
                        else:
                            pool.indirect_dma_start(agg2_d[:, :], where, comb2[b][:, c, :], None,
                                                    compute_op=ALU.add).then_inc(scattered, 16)

                def step(i, b, layer):
                    t = 2 * i + b
                    tile_roots(t + 1, 1 - b)
                    ahead = not (isinstance(t, int) and t < GROUPS <= t + 2)
                    if ahead:
                        gathers(i + 1, b, layer, (0,))
                    if layer_of(t + 1, layer) == 1:
                        group_roots(t + 1)
                    if ahead:
                        gathers(i + 1, b, layer, range(1, CH))
                    if layer == 2:
                        normalize(t + 1, 1 - b)
                    scatters(t, b, layer)
                    if isinstance(t, int) and t == GROUPS - 1:
                        pool.wait_ge(scattered, 64 * GROUPS)
                        pool.wait_ge(zero2, 16 * GROUPS)
                        gathers(HALF, 0, 2)
                        gathers(HALF, 1, 2)

                pool.sem_inc(hi_r, GROUPS)
                pool.sem_inc(lo_r, GROUPS)
                pool.sem_inc(xn2_r, GROUPS + 1)
                for b in range(2):
                    pool.memset(comb[b][:, :, :], 0.0)
                    pool.memset(msg[b][:, :, :], 0.0)
                pool.memset(gsum[:, :, :], 0.0)
                pool.memset(esum[:, :], 0.0)
                pool.memset(mvs[:, :, :], 0.0)
                pool.memset(kmax[1][:, :], -1e30).then_inc(init, 1)
                gathers(0, 0, 1)
                tile_roots(0, 0)
                group_roots(0)
                gathers(0, 1, 1)
                walk(pool, step)
                pool.wait_ge(scattered, 64 * E2)

            @block.vector
            def _(dve):
                v = nc.vector

                def statistics(i, b):
                    t = 2 * i + b
                    if not has_tile(t):
                        return
                    parts, rows = shape(t)
                    dve.wait_ge(x_in[b], 16 * (i + 1))
                    after(dve, root_r, t)
                    ch = Chain(dve, s_steps, 2, t, carried_dve)
                    for r in range(rows):
                        last = v.bn_stats(stat_rows[0:parts, r, :], xt[b][0:parts, r, :])
                    ch.link(last)
                    ch.now()
                    for r in range(rows):
                        last = v.bn_aggr(mvs[0:parts, r, :], stat_rows[0:parts, r, :])
                    ch.link(last)
                    ch.now()
                    ch.end()
                    v.tensor_scalar(vars_eps[:, 0:ROWS], mvs[:, 0:ROWS, 1], LN_EPS, None, ALU.add).then_inc(stat_r, 1)

                def group_statistics(i, b):
                    t = 2 * i + b
                    dve.wait_ge(g_in[b], 16 * 2 * CH * (i + 1))
                    after(dve, groot_r, t)
                    ch = Chain(dve, gs_steps, 2, t, carried_dve)
                    for c in range(CH):
                        last = v.bn_stats(stat_rows[0:EP, ROWS + c, :], xg[b][:, c, 0:D])
                    ch.link(last)
                    ch.now()
                    for c in range(ROWS, ROWS + CH):
                        last = v.bn_aggr(mvs[0:EP, c, :], stat_rows[0:EP, c, :])
                    ch.link(last)
                    ch.now()
                    ch.end()
                    v.tensor_scalar(vars_eps[0:EP, ROWS:ROWS + CH], mvs[0:EP, ROWS:ROWS + CH, 1], LN_EPS, None, ALU.add).then_inc(gstat_r, 1)

                def shifts(t, b, layer):
                    if not has_tile(t):
                        return
                    dve.wait_ge(root_r, t + 1)
                    after(dve, xn_r, t - 1)
                    if layer == 2:
                        after(dve, xn2_r, t - 1)
                    v.scalar_tensor_tensor(shift[b][:, :], mvs[:, 0:ROWS, 0], -1.0, roots[b][:, :], ALU.mult, ALU.mult).then_inc(shift_r, 1)

                def running_max(t, b):
                    if not has_tile(t):
                        return
                    parts, rows = shape(t)
                    dve.wait_ge(k_p, t + 1)
                    ch = Chain(dve, n_steps, 2, t)
                    ch.link(v.reduce_max(blkmax[:, :], pK[:, :, 0:parts * rows], AX.X))
                    ch.now()
                    ch.link(v.tensor_tensor(kmax[b][:, :], kmax[1 - b][:, :], blkmax[:, :], ALU.max))
                    ch.now()
                    ch.end()
                    v.tensor_scalar(negmax[b][:, :], kmax[b][:, :], -1.0, None, ALU.mult)
                    v.tensor_tensor(drop[b][:, :], kmax[1 - b][:, :], kmax[b][:, :], ALU.subtract).then_inc(max_r, 1)

                def add_sums(t, b):
                    if not has_tile(t):
                        return
                    dve.wait_ge(g_p, t + 1)
                    for c in range(2):
                        v.scalar_tensor_tensor(gsum[:, c, :], gsum[:, c, :], alpha[b][:, c:c + 1], pG[:, c, :], ALU.mult, ALU.add)
                        last = v.scalar_tensor_tensor(esum[:, c:c + 1], esum[:, c:c + 1], alpha[b][:, c:c + 1], rsum[b][:, c:c + 1], ALU.mult, ALU.add)
                    last.then_inc(g_r, 1)

                def matrix(i, b):
                    t = 2 * i + b
                    if not has_group(t):
                        return
                    ch = Chain(dve, m_steps, 3, t)
                    dve.wait_ge(e_in[b], 64 * (i + 1))
                    ch.link(v.tensor_copy(edstf[:, :], edst[b][:, :]))
                    after(dve, comb_p, CH * (t - 1))
                    ch.now()
                    for c in range(CH):
                        width = CH - c
                        v.scalar_tensor_tensor(same[b][:, c, c * EP:GROUP].rearrange("p (c l) -> p c l", c=width),
                                               dview[b][:, c:CH, :], edstf[:, c:c + 1],
                                               tri[:, 0:GROUP - c * EP].rearrange("p (c l) -> p c l", c=width),
                                               ALU.is_equal, ALU.mult, accum_out=cnt[:, c:c + 1])
                    ch.link(v.tensor_tensor(rowf[:, :], spare[:, :], edstf[:, :], ALU.subtract))
                    ch.now()
                    ch.link(v.scalar_tensor_tensor(toodd[:, :], cnt[:, :], 1.5, rowf[:, :], ALU.is_gt, ALU.mult))
                    ch.now()
                    ch.end()
                    v.tensor_tensor(rowf[:, :], toodd[:, :], edstf[:, :], ALU.add).then_inc(same_r, 1)

                def messages(i, b, layer):
                    t = 2 * i + b
                    if not has_group(t):
                        return
                    ch = Chain(dve, e_steps, 3, t) if layer == 1 else Chain(dve, e2_steps, 1, t - GROUPS)
                    if layer == 2:
                        after(dve, hi_r, t - 1)
                    if layer == 1:
                        dve.wait_ge(g_in[b], 16 * 2 * CH * (i + 1))
                        after(dve, m_out[b], 32 * i)
                        v.tensor_tensor(dsq[b][:, :], dsrc[b][:, :], dsrc[b][:, :], ALU.mult)
                        ch.link(v.tensor_tensor(coef[:, :], eew[b][:, :], dsrc[b][:, :], ALU.mult))
                    else:
                        dve.wait_ge(g_in[b], 16 * 2 * CH * HALF + 16 * CH * (i + 1 - HALF))
                        dve.wait_ge(m_in[b], 32 * (i + 1 - HALF))
                        ch.link(v.tensor_tensor(cb[:, :], dsq[b][:, :], eew[b][:, :], ALU.mult))
                    ch.now()
                    if layer == 1:
                        dve.wait_ge(groot_r, t + 1)
                        ch.link(v.tensor_tensor(ca[:, :], group_root[:, :], coef[:, :], ALU.mult))
                        ch.now()
                        ch.link(v.scalar_tensor_tensor(cb[:, :], mvs[0:EP, ROWS:ROWS + CH, 0], -1.0, ca[:, :], ALU.mult, ALU.mult))
                        ch.now()
                        for c in range(CH):
                            v.tensor_scalar(msg[b][:, c, 0:D], xg[b][:, c, 0:D], ca[:, c:c + 1], cb[:, c:c + 1], ALU.mult, ALU.add)
                        last = v.tensor_copy(msg[b][:, :, D], coef[:, :])
                    else:
                        for c in range(CH):
                            last = v.scalar_tensor_tensor(msg[b][:, c, 0:D], xg[b][:, c, 0:D], cb[:, c:c + 1], m1t[b][:, c, :], ALU.mult, ALU.add)
                    last.then_inc(msg_r, 1)
                    ch.end()

                def rest_of_messages(t, b):
                    if not has_group(t):
                        return
                    dve.wait_ge(hi_r, t + 1)
                    v.tensor_tensor(msg_lo[b][:, :, :], msg[b][:, :, 0:D], msg_hi[b][:, :, :].bitcast(f32), ALU.subtract).then_inc(lo_r, 1)

                def target_rows(t, b):
                    if not has_group(t):
                        return
                    dve.wait_ge(same_r, t + 1)
                    after(dve, scattered, 64 * (t - 1))
                    v.tensor_copy(rowi[b][:, :], rowf[:, :]).then_inc(row_r, 1)

                def step(i, b, layer):
                    t = 2 * i + b
                    nxt = later(i, b, 1)
                    of_next = layer_of(t + 1, layer)
                    last_of_layer_1 = isinstance(t, int) and t == GROUPS - 1
                    if layer == 1:
                        matrix(*nxt)
                        if of_next == 1:
                            group_statistics(*nxt)
                        running_max(t, b)
                        shifts(t + 1, 1 - b, of_next)
                        if not last_of_layer_1:
                            messages(*nxt, of_next)
                        add_sums(t - 1, 1 - b)
                        target_rows(t + 1, 1 - b)
                        if last_of_layer_1:
                            messages(*nxt, of_next)
                    else:
                        matrix(*nxt)
                        messages(*nxt, of_next)
                        shifts(t + 1, 1 - b, of_next)
                        running_max(t, b)
                        add_sums(t - 1, 1 - b)
                        target_rows(t + 1, 1 - b)
                    if of_next == 2:
                        rest_of_messages(t + 1, 1 - b)
                    statistics(*later(i, b, 2))

                dve.wait_ge(init, 1)
                statistics(0, 0)
                matrix(0, 0)
                group_statistics(0, 0)
                shifts(0, 0, 1)
                messages(0, 0, 1)
                target_rows(0, 0)
                statistics(0, 1)
                walk(dve, step)

            @block.tensor
            def _(pe):
                te = nc.tensor

                def exp_sums(t, b):
                    if not has_tile(t):
                        return
                    parts, rows = shape(t)
                    pe.wait_ge(en_r, t + 1)
                    after(pe, g_r, t)
                    for c in range(2):
                        for r in range(rows):
                            last = te.matmul(pG[:, c, :], en[b][0:parts, r, c * P:(c + 1) * P], xn[b][0:parts, r, :],
                                             start=r == 0, stop=r == rows - 1)
                    last.then_inc(g_p, 1)

                def step(i, b, layer):
                    t = 2 * i + b
                    tile = has_tile(t)
                    if tile:
                        parts, rows = shape(t)
                        n = parts * rows

                    def edge_sums(c):
                        w = D + 1 if layer == 1 else D
                        if not (isinstance(t, int) and t == 0 and c < 2):
                            pe.wait_ge(comb_r, CH * t + c - 1)
                        for k in range(c + 1):
                            alike = same[b][:, k, c * EP:(c + 1) * EP]
                            if layer == 1:
                                last = te.matmul(pC[c % 2][0:EP, 0:w], alike.bitcast(f32), msg[b][:, k, 0:w], start=k == 0, stop=k == c)
                            else:
                                te.matmul(pC[c % 2][0:EP, 0:w], alike, msg_hi[b][:, k, :], start=k == 0, stop=False)
                                last = te.matmul(pC[c % 2][0:EP, 0:w], alike, msg_lo[b][:, k, :], start=False, stop=k == c)
                        last.then_inc(comb_p, 1)

                    if tile:
                        pe.wait_ge(xn_r, t + 1)
                        if layer == 2:
                            pe.wait_ge(xn2_r, t + 1)
                        after(pe, en_r, t)
                        for c in range(2):
                            for r in range(rows):
                                last = te.transpose(pT[:, c, r * parts:(r + 1) * parts], xn[b][0:parts, r, c * P:(c + 1) * P],
                                                    ident[0:parts, 0:parts])
                            last.then_inc(xT_p, 1)
                    pe.wait_ge(same_r, t + 1)
                    if layer == 1:
                        pe.wait_ge(msg_r, t + 1)
                    else:
                        pe.wait_ge(lo_r, t + 1)
                    edge_sums(0)
                    edge_sums(1)
                    if tile:
                        pe.wait_ge(xT_r, t + 1)
                        after(pe, e_r, t)
                        for c in range(2):
                            for k in range(2):
                                last = te.matmul(pK[:, c, 0:n], wqkv[:, k, D + c * P:D + (c + 1) * P], xnT[:, k, 0:n],
                                                 start=k == 0, stop=k == 1)
                        last.then_inc(k_p, 1)
                    exp_sums(t - 1, 1 - b)
                    edge_sums(2)
                    if tile:
                        pe.wait_ge(e_r, t + 1)
                        for r in range(rows):
                            for c in range(2):
                                last = te.transpose(pT[0:parts, r // 2, (r % 2) * D + c * P:(r % 2) * D + (c + 1) * P],
                                                    eT[:, c, r * parts:(r + 1) * parts], ident[:, :])
                        last.then_inc(en_p, 1)
                    edge_sums(3)

                walk(pe, step)

            @block.scalar
            def _(act):
                a = nc.scalar

                def normalize(t, b, layer):
                    if not has_tile(t):
                        return
                    parts, rows = shape(t)
                    act.wait_ge(shift_r, t + 1)
                    after(act, g_p, t - 1)
                    for r in range(rows if layer == 1 else ROWS // 2):
                        last = a.activation(xn[b][0:parts, r, :], xt[b][0:parts, r, :], ACT.Identity,
                                            bias=shift[b][0:parts, r:r + 1], scale=roots[b][0:parts, r:r + 1])
                    last.then_inc(xn_r, 1)

                def first_of_messages(t, b):
                    if not has_group(t):
                        return
                    act.wait_ge(msg_r, t + 1)
                    after(act, comb_p, CH * (t - 1))
                    a.activation(msg_hi[b][:, :, :], msg[b][:, :, 0:D], ACT.Copy).then_inc(hi_r, 1)

                def scaled_messages(i, b):
                    t = 2 * i + b
                    act.wait_ge(msg_r, t + 1)
                    after(act, m_out[b], 32 * i)
                    for c in range(CH):
                        last = a.activation(m1t[b][:, c, :], msg[b][:, c, 0:D], ACT.Copy, scale=dsq[b][:, c:c + 1])
                    last.then_inc(kept_r, 1)

                def step(i, b, layer):
                    t = 2 * i + b

                    def take_sums(c):
                        act.wait_ge(comb_p, CH * t + c + 1)
                        if layer == 1:
                            last = a.activation(comb[b][:, c, 0:D + 1], pC[c % 2][0:EP, 0:D + 1], ACT.Copy)
                        else:
                            last = a.activation(comb2[b][:, c, :], pC[c % 2][0:EP, 0:D], ACT.Copy)
                        last.then_inc(comb_r, 1)

                    tile = has_tile(t)
                    if tile:
                        parts, rows = shape(t)
                        n = parts * rows
                        after(act, k_p, t)
                        for c in range(2):
                            act.wait_ge(xT_p, 2 * t + c + 1)
                            last = a.activation(xnT[:, c, 0:n], pT[:, c, 0:n], ACT.Copy)
                        last.then_inc(xT_r, 1)
                    after(act, scattered, 64 * (t - 1))
                    take_sums(0)
                    take_sums(1)
                    if layer == 1:
                        row = t * P * STEP_ROWS
                        view = agg2_d[row:row + P * STEP_ROWS, :] if isinstance(row, int) else agg2_d[bass.ds(row, P * STEP_ROWS), :]
                        act.dma_start(view.rearrange("(p r) w -> p (r w)", p=P), zeros[:, 0:STEP_ROWS * D]).then_inc(zero2, 16)
                        scaled_messages(i, b)
                    else:
                        first_of_messages(t + 1, 1 - b)
                    if tile:
                        act.wait_ge(max_r, t + 1)
                        after(act, en_p, t)
                        after(act, g_r, t - 1)
                        for c in range(2):
                            a.activation(eT[:, c, 0:n], pK[:, c, 0:n], ACT.Exp, bias=negmax[b][:, c:c + 1], accum_out=rsum[b][:, c:c + 1])
                        a.activation(alpha[b][:, :], drop[b][:, :], ACT.Exp).then_inc(e_r, 1)
                    normalize(t + 1, 1 - b, layer)
                    if layer == 1:
                        take_sums(2)
                    if tile:
                        act.wait_ge(en_p, t + 1)
                        after(act, g_p, t - 1)
                        for r in range(0, rows, 2):
                            w = min(2, rows - r)
                            last = a.activation(en[b][0:parts, r:r + w, :], pT[0:parts, r // 2, 0:w * D].rearrange("p (r n) -> p r n", r=w), ACT.Copy)
                        last.then_inc(en_r, 1)
                    if layer == 2:
                        take_sums(2)
                    take_sums(3)
                    if isinstance(t, int) and t == GROUPS - 1:
                        first_of_messages(t + 1, 1 - b)

                act.wait_ge(init, 1)
                normalize(0, 0, 1)
                walk(act, step)

        with ExitStack() as s2:
            rinv = s2.enter_context(nc.sbuf_tensor("rinv", [P, 2], f32))
            ctxn = s2.enter_context(nc.sbuf_tensor("ctxn", [P, 2, D], f32))
            ctxT = s2.enter_context(nc.sbuf_tensor("ctxT", [P, 2, D], f32))
            ctxb = s2.enter_context(nc.sbuf_tensor("ctxb", [P, 2, D], f32))
            c_dve, c_pe = sem("c_dve"), sem("c_pe")
            block = s2.enter_context(nc.Block())

            @block.vector
            def _(dve):
                v = nc.vector
                v.reciprocal(rinv[:, :], esum[:, :]).then_inc(c_dve, 1)
                dve.wait_ge(c_dve, 1)
                for c in range(2):
                    last = v.tensor_scalar(ctxn[:, c, :], gsum[:, c, :], rinv[:, c:c + 1], None, ALU.mult)
                last.then_inc(c_dve, 1)
                dve.wait_ge(c_pe, 1)
                v.tensor_copy(ctxT[:, :, :], pT[:, 0, :].rearrange("p (c n) -> p c n", c=2)).then_inc(c_dve, 1)
                dve.wait_ge(c_pe, 2)
                v.tensor_tensor(ctxb[:, :, :], pG[:, :, :], headmask[:, :, :], ALU.mult).then_inc(c_dve, 1)
                dve.wait_ge(c_pe, 3)
                v.tensor_copy(wM[:, :, :], pK[:, 0, :].rearrange("p (c n) -> p c n", c=2)).then_inc(c_dve, 1)
                dve.wait_ge(c_dve, 5)
                v.tensor_copy(wM_s[0][:, :, :], wM[:, :, :]).then_inc(c_dve, 1)
                dve.wait_ge(c_dve, 6)
                v.tensor_tensor(wM_s[1][:, :, :], wM[:, :, :], wM_s[0][:, :, :].bitcast(f32), ALU.subtract)

            @block.tensor
            def _(pe):
                t = nc.tensor
                pe.wait_ge(c_dve, 2)
                for c in range(2):
                    for k in range(2):
                        last = t.transpose(pT[:, 0, k * D + c * P:k * D + (c + 1) * P], ctxn[:, c, k * P:(k + 1) * P], ident[:, :])
                last.then_inc(c_pe, 1)
                pe.wait_ge(c_dve, 3)
                for c in range(2):
                    for k in range(2):
                        last = t.matmul(pG[:, c, :], ctxT[:, k, c * P:(c + 1) * P], wqkv[:, k, 2 * D:3 * D], start=k == 0, stop=k == 1)
                last.then_inc(c_pe, 1)
                pe.wait_ge(c_dve, 4)
                for c in range(2):
                    for k in range(2):
                        last = t.matmul(pK[:, 0, c * D:(c + 1) * D], wqT[:, k, c * P:(c + 1) * P], ctxb[:, k, :], start=k == 0, stop=k == 1)
                last.then_inc(c_pe, 1)

        early.close()
        narrow.close()
        pA = ps("pA", [P, 2, TILE])
        pZ = ps("pZ", [P, 2, TILE])
        pO = pK

        a1, a2, dv = two("a1", [P, ROWS, W1COLS]), two("a2", [P, ROWS, D]), two("dv", [P, ROWS])
        dd, deg1, mix2, mixn = two("dd", [P, ROWS]), two("deg1", [P, ROWS]), sb("mix2", [P, ROWS]), sb("mixn", [P, ROWS])
        var2, rsq, r2 = sb("var2", [P, ROWS]), sb("rsq", [P, ROWS]), two("r2", [P, ROWS])
        u1, u2 = sb("u1", [P, ROWS, D]), sb("u2", [P, ROWS, D])
        xnT_s, u1T_s, u2T_s, yT_s, absT_s = (parts_of(n, [P, 2, TILE]) for n in ("xnTs", "u1T", "u2T", "yTs", "absT"))
        absx, gT, yT = sb("absx", [P, 2, TILE]), sb("gT", [P, 2, TILE]), sb("yT", [P, 2, TILE])
        hscale, hpre, hid, hid_s = sb("hscale", [P, TILE]), sb("hpre", [P, TILE]), sb("hid", [P, TILE]), sb("hid_s", [P, TILE], f32r)
        xb, x2 = two("xb", [P, ROWS, D]), two("x2", [P, ROWS, D])
        stat2, mv2 = sb("stat2", [P, ROWS, 6]), sb("mv2", [P, ROWS, 2])
        ve2, rstd2, nm2, nmr2 = sb("ve2", [P, ROWS]), sb("rstd2", [P, ROWS]), sb("nm2", [P, ROWS]), sb("nmr2", [P, ROWS])
        xf = sb("xf", [P, ROWS, D])
        sgnT, osgn = sb("sgnT", [P, 2, TILE], bf16), sb("osgn", [P, ROWS, D], bf16)
        prod, x2b, res = sb("prod", [P, ROWS, D]), sb("x2b", [P, ROWS, D]), two("res", [P, ROWS, D])

        t_in, a_in, t_out = sems("t_in"), sems("a_in"), sems("t_out")
        (tstat_r, troot_r, scale_r, deg_r, a1_r, a2_r, base_r, tnorm_r, u1_r, u2_r) = (sem(n) for n in (
            "tstat_r", "troot_r", "scale_r", "deg_r", "a1_r", "a2_r", "base_r", "tnorm_r", "u1_r", "u2_r"))
        xnT_p, xnT_hi, xnT_lo, u1T_p, u1T_hi, u1T_lo, u2T_p, u2T_hi, u2T_lo = (sem(n) for n in (
            "xnT_p", "xnT_hi", "xnT_lo", "u1T_p", "u1T_hi", "u1T_lo", "u2T_p", "u2T_hi", "u2T_lo"))
        (h_p, hpre_r, hid_r, hid_hi, hid_lo, o_p, gate_p, gate_r, y_r, y_hi, y_lo, z_p, half_r, x2_r) = (sem(n) for n in (
            "h_p", "hpre_r", "hid_r", "hid_hi", "hid_lo", "o_p", "gate_p", "gate_r", "y_r", "y_hi", "y_lo", "z_p", "half_r", "x2_r"))
        (fstat_r, froot_r, xf_r, xf_p, absx_r, abs_hi, abs_lo, sgnT_r, sgn_p, ffn_p, osgn_r, prod_r, bias_r, res_r) = (sem(n) for n in (
            "fstat_r", "froot_r", "xf_r", "xf_p", "absx_r", "abs_hi", "abs_lo", "sgnT_r", "sgn_p", "ffn_p", "osgn_r", "prod_r",
            "bias_r", "res_r"))
        hscale_p, hscale_r = sem("hscale_p"), sem("hscale_r")
        ts_steps, tx_steps, tr_steps, td_steps, tb_steps, fr_steps, fs_steps = (sem(n) for n in (
            "ts_steps", "tx_steps", "tr_steps", "td_steps", "tb_steps", "fr_steps", "fs_steps"))
        block = ctx.enter_context(nc.Block())

        def tile_rows(array, t):
            if isinstance(t, int):
                first = min(t * TILE, NODES - TILE)
                view = array[first:first + TILE, :]
            else:
                view = array[bass.ds(t * TILE, TILE), :]
            return view.rearrange("(p r) w -> p (r w)", r=ROWS)

        def flat(tile):
            return tile[:, :, :].rearrange("p r w -> p (r w)")

        def halves(bank_pair):
            return bank_pair[:, :, :].rearrange("p c (r n) -> p (c r) n", n=D)

        def walk_tiles(engine, step, first=1):
            for i in range(first):
                step(i, 0)
                step(i, 1)
            with engine.Fori(first, FULL // 2) as i:
                for b in range(2):
                    step(i, b)
            step(FULL // 2, 0)
            step(FULL // 2, 1)
            step(FULL // 2 + 1, 0)

        def later(i, b, n):
            return i + (b + n) // 2, (b + n) % 2

        def runs(t):
            return not isinstance(t, int) or 0 <= t < TILES

        @block.sync
        def _(sp):
            def load(i, b):
                t = 2 * i + b
                if not runs(t):
                    return
                after(sp, base_r, t - 1)
                after(sp, tnorm_r, t - 1)
                after(sp, u2_r, t - 1)
                sp.dma_start(flat(xt[b]), tile_rows(x, t)).then_inc(t_in[b], 16)
                sp.dma_start(dv[b][:, :], tile_rows(dinv_d, t)).then_inc(a_in[b], 16)
                sp.dma_start(flat(a1[b]), tile_rows(agg1_d, t)).then_inc(a_in[b], 16)
                sp.dma_start(flat(a2[b]), tile_rows(agg2_d, t)).then_inc(a_in[b], 16)

            def store(i, b):
                t = 2 * i + b
                if isinstance(t, int) and t < 0:
                    return
                sp.wait_ge(res_r, t + 1)
                if isinstance(t, int) and t == TILES - 1:
                    sp.wait_ge(t_out[0], 16 * (FULL // 2 + 1))
                sp.dma_start(tile_rows(out, t), flat(res[b])).then_inc(t_out[b], 16)

            def step(i, b):
                load(i, b)
                store(*later(i, b, -3))

            walk_tiles(sp, step, first=2)
            store(FULL // 2, 0)
            store(FULL // 2, 1)
            for b in range(2):
                sp.wait_ge(t_out[b], 16 * (FULL // 2 + 1))

        @block.gpsimd
        def _(pool):
            def degrees(i, b):
                t = 2 * i + b
                if not runs(t):
                    return
                pool.wait_ge(a_in[b], 48 * (i + 1))
                after(pool, x2_r, t - 1)
                before_fixed(pool, carried_pool)
                ch = Chain(pool, td_steps, 2, t, carried_pool)
                ch.link(pool.tensor_tensor(dd[b][:, :], dv[b][:, :], dv[b][:, :], ALU.mult))
                ch.link(pool.tensor_tensor(deg1[b][:, :], dv[b][:, :], a1[b][:, :, D], ALU.mult))
                ch.now()
                ch.end()
                pool.tensor_tensor(deg1[b][:, :], deg1[b][:, :], dd[b][:, :], ALU.add).then_inc(deg_r, 1)

            def tile_roots(t, b):
                if not runs(t):
                    return
                pool.wait_ge(tstat_r, t + 1)
                after(pool, tnorm_r, t - 1)
                after(pool, hpre_r, t - 1)
                before_fixed(pool, carried_pool)
                ch = Chain(pool, tr_steps, 5, t, carried_pool)
                ch.link(pool.tensor_scalar(veps[b][:, :], mv[b][:, :, 1], LN_EPS, None, ALU.add))
                pool.tensor_scalar(nmean[b][:, :], mv[b][:, :, 0], -1.0, None, ALU.mult)
                ch.now()
                ch.link(pool.tensor_tensor(rstd[b][:, :], veps[b][:, :], minus_half[:, 0:ROWS], ALU.pow))
                ch.now()
                pool.tensor_tensor(nmr[b][:, :], nmean[b][:, :], rstd[b][:, :], ALU.mult).then_inc(troot_r, 1)
                ch.link(pool.tensor_tensor(rsq[:, :], rstd[b][:, :], rstd[b][:, :], ALU.mult))
                ch.now()
                ch.link(pool.tensor_tensor(var2[:, :], rsq[:, :], mv[b][:, :, 1], ALU.mult))
                ch.now()
                ch.link(pool.tensor_scalar(var2[:, :], var2[:, :], LN_EPS, None, ALU.add))
                ch.now()
                ch.end()
                pool.tensor_tensor(r2[b][:, :], var2[:, :], minus_half[:, 0:ROWS], ALU.pow).then_inc(scale_r, 1)

            def base(i, b):
                t = 2 * i + b
                if not runs(t):
                    return
                pool.wait_ge(t_in[b], 16 * (i + 1))
                pool.wait_ge(troot_r, t + 1)
                after(pool, x2_r, t - 1)
                before_fixed(pool, carried_pool)
                ch = Chain(pool, tb_steps, 1, t, carried_pool)
                pool.tensor_scalar(mixn[:, :], nmr[b][:, :], KEEP * KEEP, None, ALU.mult)
                ch.link(pool.tensor_scalar(mix2[:, :], rstd[b][:, :], KEEP * KEEP, 1.0, ALU.mult, ALU.add))
                ch.now()
                ch.end()
                for r in range(ROWS):
                    last = pool.tensor_scalar(xb[b][:, r, :], xt[b][:, r, :], mix2[:, r:r + 1], mixn[:, r:r + 1], ALU.mult, ALU.add)
                last.then_inc(base_r, 1)

            def ffn_roots(t, b):
                if not runs(t):
                    return
                pool.wait_ge(fstat_r, t + 1)
                after(pool, xf_r, t)
                if not isinstance(t, int) or t > 0:
                    pool.wait_ge(res_r, t)
                before_fixed(pool, carried_pool)
                ch = Chain(pool, fr_steps, 2, t, carried_pool)
                ch.link(pool.tensor_scalar(ve2[:, :], mv2[:, :, 1], LN_EPS, None, ALU.add))
                pool.tensor_scalar(nm2[:, :], mv2[:, :, 0], -1.0, None, ALU.mult)
                ch.now()
                ch.link(pool.tensor_tensor(rstd2[:, :], ve2[:, :], minus_half[:, 0:ROWS], ALU.pow))
                ch.now()
                ch.end()
                pool.tensor_tensor(nmr2[:, :], nm2[:, :], rstd2[:, :], ALU.mult).then_inc(froot_r, 1)
                for r in range(ROWS):
                    last = pool.tensor_tensor(x2b[:, r, :], x2[b][:, r, :], ffnb_row[:, :], ALU.add)
                last.then_inc(bias_r, 1)

            def result(i, b):
                t = 2 * i + b
                if not runs(t):
                    return
                pool.wait_ge(bias_r, t + 1)
                pool.wait_ge(prod_r, t + 1)
                after(pool, t_out[b], 16 * i)
                before_fixed(pool, carried_pool)
                pool.tensor_tensor(res[b][:, :, :], prod[:, :, :], x2b[:, :, :], ALU.add).then_inc(res_r, 1)

            def step(i, b):
                t = 2 * i + b
                degrees(*later(i, b, 1))
                ffn_roots(t - 1, 1 - b)
                base(*later(i, b, 1))
                if runs(t):
                    pool.wait_ge(y_hi, t + 1)
                    before_fixed(pool, carried_pool)
                    pool.tensor_tensor(yT_s[1][:, :, :], yT[:, :, :], yT_s[0][:, :, :].bitcast(f32), ALU.subtract).then_inc(y_lo, 1)
                tile_roots(t + 2, b)
                result(*later(i, b, -1))

            tile_roots(0, 0)
            degrees(0, 0)
            base(0, 0)
            tile_roots(1, 1)
            walk_tiles(pool, step)

        @block.vector
        def _(dve):
            v = nc.vector

            def statistics(i, b):
                t = 2 * i + b
                if not runs(t):
                    return
                dve.wait_ge(t_in[b], 16 * (i + 1))
                after(dve, scale_r, t - 1)
                ch = Chain(dve, ts_steps, 1, t, carried_dve)
                for r in range(ROWS):
                    last = v.bn_stats(stat[b][:, r, :], xt[b][:, r, :])
                ch.link(last)
                ch.now()
                ch.end()
                for r in range(ROWS):
                    last = v.bn_aggr(mv[b][:, r, :], stat[b][:, r, :])
                last.then_inc(tstat_r, 1)

            def steps_over_graph(t, b):
                if not runs(t):
                    return
                dve.wait_ge(tnorm_r, t + 1)
                dve.wait_ge(deg_r, t + 1)
                dve.wait_ge(a1_r, t + 1)
                after(dve, u1T_p, 2 * t)
                for r in range(ROWS):
                    last = v.scalar_tensor_tensor(u1[:, r, :], xn[b][:, r, :], dd[b][:, r:r + 1], a1[b][:, r, 0:D], ALU.mult, ALU.add)
                last.then_inc(u1_r, 1)
                dve.wait_ge(a2_r, t + 1)
                after(dve, u2T_p, 2 * t)
                dve.wait_ge(u1_r, t + 1)
                for r in range(ROWS):
                    last = v.scalar_tensor_tensor(u2[:, r, :], u1[:, r, :], dd[b][:, r:r + 1], a2[b][:, r, :], ALU.mult, ALU.add)
                last.then_inc(u2_r, 1)

            def rest(parts, area, hi_ready, lo_ready, t):
                for c in range(2):
                    dve.wait_ge(hi_ready, 2 * t + c + 1)
                    last = v.tensor_tensor(parts[1][:, c, :], area[:, c, :], parts[0][:, c, :].bitcast(f32), ALU.subtract)
                last.then_inc(lo_ready, 1)

            def add_half(t, b, half):
                dve.wait_ge(z_p, 2 * t + half + 1)
                rows = slice(2 * half, 2 * half + 2)
                return v.tensor_tensor(x2[b][:, rows, :], x2[b][:, rows, :], pZ[:, half, :].rearrange("p (r n) -> p r n", n=D), ALU.add)

            def step(i, b):
                t = 2 * i + b
                if runs(t - 1):
                    add_half(t - 1, 1 - b, 1).then_inc(x2_r, 1)
                if runs(t):
                    rest(xnT_s, pT, xnT_hi, xnT_lo, t)
                    rest(u1T_s, pO, u1T_hi, u1T_lo, t)
                if runs(t - 1):
                    dve.wait_ge(x2_r, t)
                    after(dve, froot_r, t - 1)
                    ch = Chain(dve, fs_steps, 1, t - 1, carried_dve)
                    for r in range(ROWS):
                        last = v.bn_stats(stat2[:, r, :], x2[1 - b][:, r, :])
                    ch.link(last)
                    ch.now()
                    ch.end()
                    for r in range(ROWS):
                        last = v.bn_aggr(mv2[:, r, :], stat2[:, r, :])
                    last.then_inc(fstat_r, 1)
                if runs(t):
                    dve.wait_ge(h_p, t + 1)
                    dve.wait_ge(hscale_r, t + 1)
                    v.tensor_tensor(hpre[:, :], pT[:, 0, :], hscale[:, :], ALU.mult).then_inc(hpre_r, 1)
                    rest(u2T_s, pA, u2T_hi, u2T_lo, t)
                    dve.wait_ge(hid_hi, t + 1)
                    upper = slice(GATE, 2 * GATE)
                    v.tensor_tensor(hid_s[upper, :], hid[upper, :], hid_s[upper, :].bitcast(f32), ALU.subtract).then_inc(hid_lo, 1)
                steps_over_graph(t + 1, 1 - b)
                if runs(t):
                    dve.wait_ge(o_p, t + 1)
                    dve.wait_ge(gate_r, t + 1)
                    v.scalar_tensor_tensor(yT[:, :, :], gT[:, :, :], 1.0, pO[:, :, :], ALU.add, ALU.mult).then_inc(y_r, 1)
                if runs(t - 1):
                    dve.wait_ge(absx_r, t)
                    v.tensor_scalar(absT_s[0][:, :, :], absx[:, :, :], FFN_EPS, None, ALU.add).then_inc(abs_hi, 1)
                    dve.wait_ge(abs_hi, t)
                    v.scalar_tensor_tensor(absT_s[1][:, :, :], absx[:, :, :], FFN_EPS, absT_s[0][:, :, :].bitcast(f32),
                                           ALU.add, ALU.subtract).then_inc(abs_lo, 1)
                if runs(t):
                    dve.wait_ge(base_r, t + 1)
                    after(dve, bias_r, t - 1)
                    after(dve, xf_r, t - 1)
                    for r in range(ROWS):
                        last = v.scalar_tensor_tensor(x2[b][:, r, :], s_row[:, :], deg1[b][:, r:r + 1], xb[b][:, r, :], ALU.mult, ALU.add)
                    last.then_inc(half_r, 1)
                statistics(*later(i, b, 2))
                if runs(t - 1):
                    dve.wait_ge(ffn_p, t)
                    dve.wait_ge(osgn_r, t)
                    after(dve, res_r, t - 1)
                    v.tensor_tensor(prod[:, :, :], halves(pA), osgn[:, :, :], ALU.mult).then_inc(prod_r, 1)
                if runs(t):
                    dve.wait_ge(half_r, t + 1)
                    add_half(t, b, 0)

            statistics(0, 0)
            statistics(0, 1)
            steps_over_graph(0, 0)
            walk_tiles(dve, step)

        @block.tensor
        def _(pe):
            te = nc.tensor

            def turn(area, rows_tile, filled):
                for c in range(2):
                    for r in range(ROWS):
                        last = te.transpose(area[:, c, r * P:(r + 1) * P], rows_tile[:, r, c * P:(c + 1) * P], ident[:, :])
                    last.then_inc(filled, 1)

            def product(result, left, right, start, stop):
                for k in range(2):
                    for n, (l, r) in enumerate(PASSES):
                        last = te.matmul(result, left(k, l), right(k, r), start=start and k == 0 and n == 0,
                                         stop=stop and k == 1 and n == len(PASSES) - 1)
                return last

            def rows_of(parts, r):
                return lambda k, n: parts[n][:, k, r * P:(r + 1) * P]

            def weights(parts):
                return lambda k, n: parts[n][:, k, :]

            def graph_terms(half, t):
                te.matmul(pZ[:, half, :], ones[:, :], c_parts[:, :, :].rearrange("p a n -> p (a n)"), start=True, stop=False)
                for r in (2 * half, 2 * half + 1):
                    product(halves(pZ)[:, r, :], rows_of(u1T_s, r), weights(wB_s), False, False)
                pe.wait_ge(u2T_lo, t + 1)
                for r in (2 * half, 2 * half + 1):
                    product(halves(pZ)[:, r, :], rows_of(u2T_s, r), weights(wA_s), False, False)

            def step(i, b):
                t = 2 * i + b
                if runs(t):
                    pe.wait_ge(tnorm_r, t + 1)
                    after(pe, osgn_r, t - 1)
                    turn(pT, xn[b], xnT_p)
                    pe.wait_ge(u1_r, t + 1)
                    after(pe, y_r, t)
                    turn(pO, u1, u1T_p)
                    pe.wait_ge(u2_r, t + 1)
                    after(pe, prod_r, t - 1)
                    turn(pA, u2, u2T_p)
                    pe.wait_ge(xnT_lo, t + 1)
                    pe.wait_ge(scale_r, t + 1)
                    before_fixed(pe, carried_pe)
                    for r in range(ROWS):
                        last = te.transpose(pT[:, 1, r * P:(r + 1) * P], r2[b][:, r:r + 1].broadcast_to([P, P]), ident[:, :])
                    last.then_inc(hscale_p, 1)
                    product(pT[:, 0, :], weights(wg1g_s), weights(xnT_s), True, True).then_inc(h_p, 1)
                    pe.wait_ge(u1T_lo, t + 1)
                    for c in range(2):
                        last = product(pO[:, c, :], lambda k, n: wM_s[n][:, k, c * P:(c + 1) * P], lambda k, n: xnT_s[n][:, k, :], True, True)
                    last.then_inc(o_p, 1)
                    after(pe, x2_r, t)
                    graph_terms(0, t)
                    pe.wait_ge(hid_lo, t + 1)
                    for c in range(2):
                        te.matmul(pA[:, c, :], wg2_s[0][:, c * P:(c + 1) * P], hid_s[:, :], start=True, stop=False)
                        last = te.matmul(pA[:, c, :], wg2_s[1][0:GATE, c * P:(c + 1) * P], hid_s[0:GATE, :], start=False, stop=True)
                    last.then_inc(gate_p, 1)
                if runs(t - 1):
                    pe.wait_ge(xf_r, t)
                    if not runs(t):
                        pe.wait_ge(osgn_r, t - 1)
                    turn(pT, xf, xf_p)
                if runs(t):
                    graph_terms(1, t)
                if runs(t - 1):
                    pe.wait_ge(absx_r, t)
                    pe.wait_ge(sgnT_r, t)
                    for r in range(ROWS):
                        for k in range(2):
                            last = te.matmul(halves(pT)[:, r, :], sgnT[:, k, r * P:(r + 1) * P], wsgnT[:, k, :], start=k == 0, stop=k == 1)
                    last.then_inc(sgn_p, 1)
                    pe.wait_ge(abs_lo, t)
                    if runs(t):
                        pe.wait_ge(gate_r, t + 1)
                    else:
                        pe.wait_ge(prod_r, t - 1)
                    for r in range(ROWS):
                        last = product(halves(pA)[:, r, :], rows_of(absT_s, r), weights(wabsT_s), True, True)
                    last.then_inc(ffn_p, 1)
                if runs(t):
                    pe.wait_ge(y_lo, t + 1)
                    for r in range(ROWS):
                        last = product(halves(pZ)[:, r, :], rows_of(yT_s, r), weights(wproj_s), False, r % 2 == 1)
                        if r % 2 == 1:
                            last.then_inc(z_p, 1)

            walk_tiles(pe, step)

        @block.scalar
        def _(act):
            a = nc.scalar

            def first_parts(parts, area, filled, hi_ready, t):
                for c in range(2):
                    act.wait_ge(filled, 2 * t + c + 1)
                    a.activation(parts[0][:, c, :], area[:, c, :], ACT.Copy).then_inc(hi_ready, 1)

            def normalize(t, b):
                if not runs(t):
                    return
                act.wait_ge(troot_r, t + 1)
                after(act, u1_r, t - 1)
                after(act, xnT_p, 2 * (t - 1))
                for r in range(ROWS):
                    last = a.activation(xn[b][:, r, :], xt[b][:, r, :], ACT.Identity, bias=nmr[b][:, r:r + 1], scale=rstd[b][:, r:r + 1])
                last.then_inc(tnorm_r, 1)

            def scale_sums(sums, i, b, ready):
                t = 2 * i + b
                if not runs(t):
                    return
                act.wait_ge(a_in[b], 48 * (i + 1))
                for r in range(ROWS):
                    last = a.activation(sums[b][:, r, 0:D], sums[b][:, r, 0:D], ACT.Copy, scale=dv[b][:, r:r + 1])
                last.then_inc(ready, 1)

            def step(i, b):
                t = 2 * i + b
                if runs(t):
                    first_parts(xnT_s, pT, xnT_p, xnT_hi, t)
                    first_parts(u1T_s, pO, u1T_p, u1T_hi, t)
                    first_parts(u2T_s, pA, u2T_p, u2T_hi, t)
                    act.wait_ge(hscale_p, t + 1)
                    a.activation(hscale[:, :], pT[:, 1, :], ACT.Copy).then_inc(hscale_r, 1)
                normalize(t + 1, 1 - b)
                if runs(t):
                    act.wait_ge(hpre_r, t + 1)
                    a.activation(hid[:, :], hpre[:, :], ACT.Gelu, bias=h_col[:, :]).then_inc(hid_r, 1)
                    act.wait_ge(hid_r, t + 1)
                    a.activation(hid_s[:, :], hid[:, :], ACT.Copy).then_inc(hid_hi, 1)
                if runs(t - 1):
                    act.wait_ge(froot_r, t)
                    after(act, xf_p, 2 * (t - 1))
                    for r in range(ROWS):
                        last = a.activation(xf[:, r, :], x2[1 - b][:, r, :], ACT.Identity, bias=nmr2[:, r:r + 1], scale=rstd2[:, r:r + 1])
                    last.then_inc(xf_r, 1)
                if runs(t):
                    act.wait_ge(gate_p, t + 1)
                    after(act, y_r, t)
                    for c in range(2):
                        last = a.activation(gT[:, c, :], pA[:, c, :], ACT.Tanh, bias=bg2c[:, c:c + 1], scale=0.5)
                    last.then_inc(gate_r, 1)
                if runs(t - 1):
                    act.wait_ge(xf_p, 2 * t)
                    a.activation(absx[:, :, :], pT[:, :, :], ACT.Abs).then_inc(absx_r, 1)
                    a.activation(sgnT[:, :, :], pT[:, :, :], ACT.Sign).then_inc(sgnT_r, 1)
                if runs(t):
                    act.wait_ge(y_r, t + 1)
                    a.activation(yT_s[0][:, :, :], yT[:, :, :], ACT.Copy).then_inc(y_hi, 1)
                if runs(t - 1):
                    act.wait_ge(sgn_p, t)
                    after(act, prod_r, t - 1)
                    a.activation(osgn[:, :, :], halves(pT), ACT.Sign).then_inc(osgn_r, 1)
                scale_sums(a1, *later(i, b, 2), a1_r)
                scale_sums(a2, *later(i, b, 2), a2_r)

            normalize(0, 0)
            for b in range(2):
                scale_sums(a1, 0, b, a1_r)
                scale_sums(a2, 0, b, a2_r)
            walk_tiles(act, step)


_INS = ["x", "src", "dst", "edge_weight", "L0_gnn_W1", "L0_gnn_b1", "L0_gnn_W2", "L0_gnn_b2", "L0_mix_Wqkv", "L0_mix_Wproj",
        "L0_mix_bproj", "L0_mix_ln_g", "L0_mix_ln_b", "L0_mix_Wg1", "L0_mix_bg1", "L0_mix_Wg2", "L0_mix_bg2",
        "L0_ffn_weight", "L0_ffn_bias"]


def kernel(**inputs):
    import numpy as _np
    import concourse.bacc as _bacc
    from concourse import mybir as _mybir
    from concourse.bass_utils import run_bass_kernel_spmd as _run

    nc = _bacc.Bacc("TRN2", target_bir_lowering=False, num_devices=1)
    arrays, args = {}, []
    for name in _INS:
        a = _np.ascontiguousarray(inputs[name])
        arrays[f"in_{name}"] = a
        args.append(nc.dram_tensor(f"in_{name}", a.shape, _mybir.dt.from_np(a.dtype), kind="ExternalInput").ap())
    args.append(nc.dram_tensor("out_0", (NODES, D), _mybir.dt.float32, kind="ExternalOutput").ap())
    build_gps(nc, *args)
    r = _run(nc, [arrays], core_ids=[0])
    return r.results[0]["out_0"]
```
